# Optimizing a Trainium2 kernel written in Bass

```python
import numpy as np
import jax
import jax.numpy as jnp

def _softmax(x, axis=-1):
    return jax.nn.softmax(x, axis=axis)

def _gelu(x):
    return jax.nn.gelu(x, approximate=True)

def _silu(x):
    return jax.nn.silu(x)

def _sigmoid(x):
    return jax.nn.sigmoid(x)

def _layernorm(x, axis=-1, eps=1e-05):
    m = jnp.mean(x, axis=axis, keepdims=True)
    v = jnp.var(x, axis=axis, keepdims=True)
    return (x - m) / jnp.sqrt(v + eps)

def _scatter_add(tgt, idx, src, axis=0):
    return tgt.at[idx].add(src)

def _segment_sum(src, seg, n):
    return jax.ops.segment_sum(src, seg, n)
kernel_name = 'mk_seq_postln_d2_jaxref_r8_b3e881'

def setup_inputs(seed: int=0):
    np.random.seed(seed)
    _w = jnp.asarray

    def _L0_attn_setup():
        import jax, jax.numpy as jnp
        import numpy as np
        D = 128
        H = 16
        K = 64
        B = 4
        T = 128
        LAYER_ID = 12
        NUM_LAYERS = 24
        D_MIX = 32
        D_DECAY = 64

        def _bidir_shift(x):
            left = jnp.pad(x[:, :-1, :], ((0, 0), (1, 0), (0, 0)))
            right = jnp.pad(x[:, 1:, :], ((0, 0), (0, 1), (0, 0)))
            return 0.5 * (left + right)

        def _lion_attention(r, k, v, w):
            Tn = r.shape[2]
            cs = jnp.cumsum(w, axis=2)
            cs_b = cs - w
            shift_f = cs[:, :, Tn // 2:Tn // 2 + 1, :]
            shift_b = cs_b[:, :, Tn // 2:Tn // 2 + 1, :]
            cf = jnp.clip(cs - shift_f, -60.0, 60.0)
            cb = jnp.clip(cs_b - shift_b, -60.0, 60.0)
            A_f = jnp.einsum('bhik,bhjk->bhij', r * jnp.exp(cf), k * jnp.exp(-cf))
            A_b = jnp.einsum('bhik,bhjk->bhij', r * jnp.exp(-cb), k * jnp.exp(cb))
            idx = jnp.arange(Tn)
            lower = idx[:, None] >= idx[None, :]
            A = jnp.where(lower, A_f, A_b)
            return jnp.einsum('bhij,bhjk->bhik', A, v)
        key = jax.random.key(seed)
        ks = jax.random.split(key, 12)
        r01 = LAYER_ID / (NUM_LAYERS - 1)
        r10 = 1.0 - LAYER_ID / NUM_LAYERS
        ddd = jnp.arange(D, dtype=jnp.float32) / D
        maa = lambda p: (1.0 - ddd ** p).reshape(1, 1, D)
        inp = {}
        inp['x'] = jax.random.normal(ks[0], (B, T, D), jnp.float32)
        inp['time_maa_x'] = maa(r10)
        inp['time_maa_w'] = maa(r10)
        inp['time_maa_k'] = maa(r10)
        inp['time_maa_v'] = (1.0 - (ddd ** r10 + 0.3 * r01)).reshape(1, 1, D)
        inp['time_maa_r'] = maa(0.5 * r10)
        inp['time_maa_g'] = maa(0.5 * r10)
        inp['time_maa_w1'] = jax.random.uniform(ks[1], (D, D_MIX * 5), jnp.float32, -0.01, 0.01)
        inp['time_maa_w2'] = jax.random.uniform(ks[2], (5, D_MIX, D), jnp.float32, -0.01, 0.01)
        n = jnp.arange(D, dtype=jnp.float32)
        inp['time_decay'] = (-6.0 + 5.0 * (n / (D - 1)) ** (0.7 + 1.3 * r01)).reshape(1, 1, D)
        inp['time_decay_w1'] = jax.random.uniform(ks[3], (D, D_DECAY), jnp.float32, -0.01, 0.01)
        inp['time_decay_w2'] = jax.random.uniform(ks[4], (D_DECAY, D), jnp.float32, -0.01, 0.01)
        for nm, kk in zip(['W_r', 'W_k', 'W_v', 'W_g', 'W_o'], ks[5:10]):
            inp[nm] = jax.random.normal(kk, (D, D), jnp.float32) * 0.02
        inp['ln_w'] = jnp.ones((D,), jnp.float32)
        inp['ln_b'] = jnp.zeros((D,), jnp.float32)
        return inp
    _L0_attn_in = _L0_attn_setup()

    def _L0_ffn_setup():
        import jax, jax.numpy as jnp
        import numpy as np
        TEMPERATURE = 1.0
        TOPK = 2
        key = jax.random.key(seed)
        ks = jax.random.split(key, 6)
        S, B, H, F, E = (256, 4, 128, 512, 8)
        x = jax.random.normal(ks[0], (S, B, H), dtype=jnp.float32)
        gate_w = jax.random.normal(ks[1], (E, H), dtype=jnp.float32) * (1.0 / np.sqrt(H))
        w1 = jax.random.normal(ks[2], (E, H, F), dtype=jnp.float32) * (1.0 / np.sqrt(H))
        b1 = jnp.zeros((E, F), dtype=jnp.float32)
        w2 = jax.random.normal(ks[3], (E, F, H), dtype=jnp.float32) * (1.0 / np.sqrt(F))
        b2 = jnp.zeros((E, H), dtype=jnp.float32)
        return {'x': x, 'gate_w': gate_w, 'w1': w1, 'b1': b1, 'w2': w2, 'b2': b2}
    _L0_ffn_in = _L0_ffn_setup()

    def _L1_attn_setup():
        import jax, jax.numpy as jnp
        import numpy as np
        B, L, H = (2, 512, 128)
        NH, DK, DV = (4, 32, 32)
        CHUNK = 32
        CONV_K, FIR_S, FIR_L = (4, 3, 63)
        GATE_HID = 128
        FLOOR_NOW = 0.05

        def _l2norm(x, eps=1e-06):
            return x * jax.lax.rsqrt(jnp.sum(x * x, -1, keepdims=True) + eps)

        def _depthwise_causal(x_bcl, w_c1k):
            K = w_c1k.shape[-1]
            return jax.lax.conv_general_dilated(x_bcl, w_c1k, (1,), [(K - 1, 0)], dimension_numbers=('NCH', 'OIH', 'NCH'), feature_group_count=x_bcl.shape[1])

        def _short_conv_silu(x, w):
            y = _depthwise_causal(jnp.swapaxes(x, 1, 2), w[:, None, :])
            return jax.nn.silu(jnp.swapaxes(y, 1, 2))

        def _fir(x, filt):
            b, l, h, d = x.shape
            xf = jnp.swapaxes(x.reshape(b, l, h * d), 1, 2)
            y = _depthwise_causal(xf, filt.reshape(h * d, 1, -1))
            return jnp.swapaxes(y, 1, 2).reshape(b, l, h, d)

        def _delta_rule_chunkwise(q, k, v, beta, chunk=CHUNK):
            b, h, Lq, dk = q.shape
            dv = v.shape[-1]
            q = _l2norm(q)
            k = _l2norm(k)
            v = v * beta[..., None]
            k_beta = k * beta[..., None]
            n = Lq // chunk
            rs = lambda t: t.reshape(b, h, n, chunk, -1)
            q, k, v, k_beta = map(rs, (q, k, v, k_beta))
            idx = jnp.arange(chunk)
            strict_lower = idx[:, None] > idx[None, :]
            incl_lower = idx[:, None] >= idx[None, :]
            A = jnp.where(strict_lower, -jnp.einsum('bhnck,bhnjk->bhncj', k_beta, k), 0.0)
            for i in range(1, chunk):
                row = A[..., i, :]
                A = A.at[..., i, :].set(row + jnp.einsum('bhnj,bhnjc->bhnc', row, A))
            T = A + jnp.eye(chunk, dtype=A.dtype)
            u = jnp.einsum('bhncj,bhnjd->bhncd', T, v)
            w = jnp.einsum('bhncj,bhnjd->bhncd', T, k_beta)

            def step(S, inp):
                q_i, k_i, u_i, w_i = inp
                attn = jnp.where(incl_lower, jnp.einsum('bhck,bhjk->bhcj', q_i, k_i), 0.0)
                u_adj = u_i - jnp.einsum('bhck,bhkd->bhcd', w_i, S)
                o_i = jnp.einsum('bhck,bhkd->bhcd', q_i, S) + jnp.einsum('bhcj,bhjd->bhcd', attn, u_adj)
                S = S + jnp.einsum('bhck,bhcd->bhkd', k_i, u_adj)
                return (S, o_i)
            mv = lambda t: jnp.moveaxis(t, 2, 0)
            S0 = jnp.zeros((b, h, dk, dv), q.dtype)
            S, out = jax.lax.scan(step, S0, (mv(q), mv(k), mv(u), mv(w)))
            out = jnp.moveaxis(out, 0, 2).reshape(b, h, Lq, dv)
            return (out, S)

        def _stats(x):
            mean = jnp.mean(x, -1, keepdims=True)
            var = jnp.var(x, -1, keepdims=True)
            am = jnp.mean(jnp.abs(x), -1, keepdims=True)
            l2 = jnp.linalg.norm(x, axis=-1, keepdims=True)
            return jnp.concatenate([mean, var, am, l2], -1)

        def _forward(hs, Wq, Wk, Wv, cwq, cwk, cwv, Wb, Wid, alpha_id, firs, firl, gW1, gb1, gW2, gb2, log_temp, floor_param, conv_res_logit, o_norm_w, Wo):
            b, l, _ = hs.shape
            q = _short_conv_silu(hs @ Wq, cwq)
            k = _short_conv_silu(hs @ Wk, cwk)
            v = _short_conv_silu(hs @ Wv, cwv)
            q = q.reshape(b, l, NH, DK)
            k = k.reshape(b, l, NH, DK)
            v_direct = v.reshape(b, l, NH, DV)
            beta = jax.nn.sigmoid(hs @ Wb)
            tp = lambda t: jnp.transpose(t, (0, 2, 1, 3))
            delta_out, _S = _delta_rule_chunkwise(tp(q), tp(k), tp(v_direct), jnp.transpose(beta, (0, 2, 1)))
            delta_out = tp(delta_out)
            local_short = _fir(v_direct, firs)
            local_long = _fir(v_direct, firl)
            stats = jnp.concatenate([_stats(t) for t in (local_short, local_long, delta_out, v_direct)], -1)
            hs_exp = jnp.broadcast_to(hs[:, :, None, :], (b, l, NH, hs.shape[-1]))
            gin = jnp.concatenate([hs_exp, stats], -1)
            logits = jax.nn.gelu(gin @ gW1 + gb1, approximate=False) @ gW2 + gb2
            logits = logits / jnp.exp(log_temp)[None, None]
            probs = jax.nn.softmax(logits, -1)
            floor = FLOOR_NOW * jax.nn.sigmoid(floor_param)
            probs = probs * (1.0 - jnp.sum(floor, -1, keepdims=True)) + floor
            o = probs[..., 0:1] * local_short + probs[..., 1:2] * local_long + probs[..., 2:3] * delta_out + probs[..., 3:4] * v_direct
            o = o + jax.nn.sigmoid(conv_res_logit)[None, None, :, None] * local_short
            id_val = (hs @ Wid).reshape(b, l, NH, DV)
            o = o + alpha_id[None, None, :, None] * id_val
            o = o * jax.lax.rsqrt(jnp.mean(o * o, -1, keepdims=True) + 1e-05) * o_norm_w
            return o.reshape(b, l, NH * DV) @ Wo
        key = jax.random.key(seed)
        ks = jax.random.split(key, 16)
        nrm = lambda i, shape, sc=0.02: jax.random.normal(ks[i], shape, jnp.float32) * sc

        def dirac_fir(i, K):
            f = jnp.zeros((NH, DV, K), jnp.float32).at[..., -1].set(1.0)
            return f + 0.01 * jax.random.normal(ks[i], (NH, DV, K), jnp.float32)
        return {'hs': jax.random.normal(ks[0], (B, L, H), jnp.float32), 'Wq': nrm(1, (H, NH * DK)), 'Wk': nrm(2, (H, NH * DK)), 'Wv': nrm(3, (H, NH * DV)), 'cwq': nrm(4, (NH * DK, CONV_K), 0.2), 'cwk': nrm(5, (NH * DK, CONV_K), 0.2), 'cwv': nrm(6, (NH * DV, CONV_K), 0.2), 'Wb': nrm(7, (H, NH)), 'Wid': nrm(8, (H, NH * DV)), 'alpha_id': 0.5 * jnp.ones((NH,), jnp.float32), 'firs': dirac_fir(9, FIR_S), 'firl': dirac_fir(10, FIR_L), 'gW1': nrm(11, (H + 16, GATE_HID)), 'gb1': jnp.zeros((GATE_HID,), jnp.float32), 'gW2': nrm(12, (GATE_HID, 4)), 'gb2': jnp.zeros((4,), jnp.float32).at[3].set(1.5), 'log_temp': jnp.zeros((NH, 4), jnp.float32), 'floor_param': jnp.zeros((NH, 4), jnp.float32), 'conv_res_logit': jnp.full((NH,), float(np.log(0.05 / 0.95)), jnp.float32), 'o_norm_w': jnp.ones((DV,), jnp.float32), 'Wo': nrm(13, (NH * DV, H))}
    _L1_attn_in = _L1_attn_setup()

    def _L1_ffn_setup():
        import jax, jax.numpy as jnp
        import numpy as np
        D = 128
        N_EXP = 8
        TOP_K = 1
        key = jax.random.key(seed)
        ks = jax.random.split(key, 7)
        s = 0.02
        return {'x': jax.random.normal(ks[0], (4, 256, D), jnp.float32), 'gate_w': jax.random.normal(ks[1], (D, N_EXP), jnp.float32) * s, 'gate_b': jnp.zeros((N_EXP,), jnp.float32), 'w1': jax.random.normal(ks[2], (N_EXP, D, 4 * D), jnp.float32) * s, 'b1': jnp.zeros((N_EXP, 4 * D), jnp.float32), 'w2': jax.random.normal(ks[3], (N_EXP, 4 * D, D), jnp.float32) * s, 'b2': jnp.zeros((N_EXP, D), jnp.float32)}
    _L1_ffn_in = _L1_ffn_setup()
    _d = {'L0_attn_x': _L0_attn_in['x'], 'L0_attn_time_maa_x': _L0_attn_in['time_maa_x'], 'L0_attn_time_maa_w': _L0_attn_in['time_maa_w'], 'L0_attn_time_maa_k': _L0_attn_in['time_maa_k'], 'L0_attn_time_maa_v': _L0_attn_in['time_maa_v'], 'L0_attn_time_maa_r': _L0_attn_in['time_maa_r'], 'L0_attn_time_maa_g': _L0_attn_in['time_maa_g'], 'L0_attn_time_maa_w1': _L0_attn_in['time_maa_w1'], 'L0_attn_time_maa_w2': _L0_attn_in['time_maa_w2'], 'L0_attn_time_decay': _L0_attn_in['time_decay'], 'L0_attn_time_decay_w1': _L0_attn_in['time_decay_w1'], 'L0_attn_time_decay_w2': _L0_attn_in['time_decay_w2'], 'L0_attn_W_r': _L0_attn_in['W_r'], 'L0_attn_W_k': _L0_attn_in['W_k'], 'L0_attn_W_v': _L0_attn_in['W_v'], 'L0_attn_W_g': _L0_attn_in['W_g'], 'L0_attn_W_o': _L0_attn_in['W_o'], 'L0_attn_ln_w': _L0_attn_in['ln_w'], 'L0_attn_ln_b': _L0_attn_in['ln_b'], 'L0_ffn_gate_w': _L0_ffn_in['gate_w'], 'L0_ffn_w1': _L0_ffn_in['w1'], 'L0_ffn_b1': _L0_ffn_in['b1'], 'L0_ffn_w2': _L0_ffn_in['w2'], 'L0_ffn_b2': _L0_ffn_in['b2'], 'L1_attn_Wq': _L1_attn_in['Wq'], 'L1_attn_Wk': _L1_attn_in['Wk'], 'L1_attn_Wv': _L1_attn_in['Wv'], 'L1_attn_cwq': _L1_attn_in['cwq'], 'L1_attn_cwk': _L1_attn_in['cwk'], 'L1_attn_cwv': _L1_attn_in['cwv'], 'L1_attn_Wb': _L1_attn_in['Wb'], 'L1_attn_Wid': _L1_attn_in['Wid'], 'L1_attn_alpha_id': _L1_attn_in['alpha_id'], 'L1_attn_firs': _L1_attn_in['firs'], 'L1_attn_firl': _L1_attn_in['firl'], 'L1_attn_gW1': _L1_attn_in['gW1'], 'L1_attn_gb1': _L1_attn_in['gb1'], 'L1_attn_gW2': _L1_attn_in['gW2'], 'L1_attn_gb2': _L1_attn_in['gb2'], 'L1_attn_log_temp': _L1_attn_in['log_temp'], 'L1_attn_floor_param': _L1_attn_in['floor_param'], 'L1_attn_conv_res_logit': _L1_attn_in['conv_res_logit'], 'L1_attn_o_norm_w': _L1_attn_in['o_norm_w'], 'L1_attn_Wo': _L1_attn_in['Wo'], 'L1_ffn_gate_w': _L1_ffn_in['gate_w'], 'L1_ffn_gate_b': _L1_ffn_in['gate_b'], 'L1_ffn_w1': _L1_ffn_in['w1'], 'L1_ffn_b1': _L1_ffn_in['b1'], 'L1_ffn_w2': _L1_ffn_in['w2'], 'L1_ffn_b2': _L1_ffn_in['b2']}
    _x0 = _d['L0_attn_x']
    _d['L0_attn_x'] = jax.random.normal(jax.random.fold_in(jax.random.key(seed), 1), (16, 256, 128), dtype=_x0.dtype)
    del _x0
    return _d

def reference(L0_attn_x, L0_attn_time_maa_x, L0_attn_time_maa_w, L0_attn_time_maa_k, L0_attn_time_maa_v, L0_attn_time_maa_r, L0_attn_time_maa_g, L0_attn_time_maa_w1, L0_attn_time_maa_w2, L0_attn_time_decay, L0_attn_time_decay_w1, L0_attn_time_decay_w2, L0_attn_W_r, L0_attn_W_k, L0_attn_W_v, L0_attn_W_g, L0_attn_W_o, L0_attn_ln_w, L0_attn_ln_b, L0_ffn_gate_w, L0_ffn_w1, L0_ffn_b1, L0_ffn_w2, L0_ffn_b2, L1_attn_Wq, L1_attn_Wk, L1_attn_Wv, L1_attn_cwq, L1_attn_cwk, L1_attn_cwv, L1_attn_Wb, L1_attn_Wid, L1_attn_alpha_id, L1_attn_firs, L1_attn_firl, L1_attn_gW1, L1_attn_gb1, L1_attn_gW2, L1_attn_gb2, L1_attn_log_temp, L1_attn_floor_param, L1_attn_conv_res_logit, L1_attn_o_norm_w, L1_attn_Wo, L1_ffn_gate_w, L1_ffn_gate_b, L1_ffn_w1, L1_ffn_b1, L1_ffn_w2, L1_ffn_b2):

    def _L0_attn_ref(x, time_maa_x, time_maa_w, time_maa_k, time_maa_v, time_maa_r, time_maa_g, time_maa_w1, time_maa_w2, time_decay, time_decay_w1, time_decay_w2, W_r, W_k, W_v, W_g, W_o, ln_w, ln_b):
        import jax, jax.numpy as jnp
        import numpy as np
        D = 128
        H = 16
        K = 64
        B = 4
        T = 128
        LAYER_ID = 12
        NUM_LAYERS = 24
        D_MIX = 32
        D_DECAY = 64

        def _bidir_shift(x):
            left = jnp.pad(x[:, :-1, :], ((0, 0), (1, 0), (0, 0)))
            right = jnp.pad(x[:, 1:, :], ((0, 0), (0, 1), (0, 0)))
            return 0.5 * (left + right)

        def _lion_attention(r, k, v, w):
            Tn = r.shape[2]
            cs = jnp.cumsum(w, axis=2)
            cs_b = cs - w
            shift_f = cs[:, :, Tn // 2:Tn // 2 + 1, :]
            shift_b = cs_b[:, :, Tn // 2:Tn // 2 + 1, :]
            cf = jnp.clip(cs - shift_f, -60.0, 60.0)
            cb = jnp.clip(cs_b - shift_b, -60.0, 60.0)
            A_f = jnp.einsum('bhik,bhjk->bhij', r * jnp.exp(cf), k * jnp.exp(-cf))
            A_b = jnp.einsum('bhik,bhjk->bhij', r * jnp.exp(-cb), k * jnp.exp(cb))
            idx = jnp.arange(Tn)
            lower = idx[:, None] >= idx[None, :]
            A = jnp.where(lower, A_f, A_b)
            return jnp.einsum('bhij,bhjk->bhik', A, v)
        Bn, Tn, Dn = x.shape
        Hh, Kk = (H, Dn // H)
        dxprev = _bidir_shift(x) - x
        xxx = jnp.tanh((x + dxprev * time_maa_x) @ time_maa_w1)
        mm = jnp.einsum('btfm,fmd->fbtd', xxx.reshape(Bn, Tn, 5, D_MIX), time_maa_w2)
        mw, mk, mv, mr, mg = (mm[0], mm[1], mm[2], mm[3], mm[4])
        xw = x + dxprev * (time_maa_w + mw)
        xk = x + dxprev * (time_maa_k + mk)
        xv = x + dxprev * (time_maa_v + mv)
        xr = x + dxprev * (time_maa_r + mr)
        xg = x + dxprev * (time_maa_g + mg)
        r = xr @ W_r.T
        k = xk @ W_k.T
        v = xv @ W_v.T
        g = jax.nn.silu(xg @ W_g.T)
        w = time_decay + jnp.tanh(xw @ time_decay_w1) @ time_decay_w2
        to_h = lambda t: t.reshape(Bn, Tn, Hh, Kk).transpose(0, 2, 1, 3)
        y = _lion_attention(to_h(r), to_h(k), to_h(v), -jnp.exp(to_h(w)))
        y = y.transpose(0, 2, 1, 3).reshape(Bn * Tn, Dn)
        eps = 1e-05 * 64.0
        yg = y.reshape(Bn * Tn, Hh, Kk)
        mu = jnp.mean(yg, axis=-1, keepdims=True)
        var = jnp.var(yg, axis=-1, keepdims=True)
        yn = ((yg - mu) * jax.lax.rsqrt(var + eps)).reshape(Bn * Tn, Dn) * ln_w + ln_b
        y = yn.reshape(Bn, Tn, Dn)
        return y * g @ W_o.T

    def _L0_ffn_ref(x, gate_w, w1, b1, w2, b2):
        import jax, jax.numpy as jnp
        import numpy as np
        TEMPERATURE = 1.0
        TOPK = 2
        s, b, h = x.shape
        x_flat = x.reshape(s * b, h)
        logits = x_flat @ gate_w.T
        probs = jax.nn.softmax(logits / TEMPERATURE, axis=-1)
        topk_probs, topk_idx = jax.lax.top_k(probs, TOPK)
        hidden = jax.nn.relu(jnp.einsum('th,ehf->tef', x_flat, w1) + b1[None])
        all_out = jnp.einsum('tef,efh->teh', hidden, w2) + b2[None]
        gathered = jnp.take_along_axis(all_out, topk_idx[:, :, None], axis=1)
        y_flat = jnp.sum(gathered * topk_probs[:, :, None], axis=1)
        return y_flat.reshape(s, b, h)

    def _L1_attn_ref(hs, Wq, Wk, Wv, cwq, cwk, cwv, Wb, Wid, alpha_id, firs, firl, gW1, gb1, gW2, gb2, log_temp, floor_param, conv_res_logit, o_norm_w, Wo):
        import jax, jax.numpy as jnp
        import numpy as np
        B, L, H = (2, 512, 128)
        NH, DK, DV = (4, 32, 32)
        CHUNK = 32
        CONV_K, FIR_S, FIR_L = (4, 3, 63)
        GATE_HID = 128
        FLOOR_NOW = 0.05

        def _l2norm(x, eps=1e-06):
            return x * jax.lax.rsqrt(jnp.sum(x * x, -1, keepdims=True) + eps)

        def _depthwise_causal(x_bcl, w_c1k):
            K = w_c1k.shape[-1]
            return jax.lax.conv_general_dilated(x_bcl, w_c1k, (1,), [(K - 1, 0)], dimension_numbers=('NCH', 'OIH', 'NCH'), feature_group_count=x_bcl.shape[1])

        def _short_conv_silu(x, w):
            y = _depthwise_causal(jnp.swapaxes(x, 1, 2), w[:, None, :])
            return jax.nn.silu(jnp.swapaxes(y, 1, 2))

        def _fir(x, filt):
            b, l, h, d = x.shape
            xf = jnp.swapaxes(x.reshape(b, l, h * d), 1, 2)
            y = _depthwise_causal(xf, filt.reshape(h * d, 1, -1))
            return jnp.swapaxes(y, 1, 2).reshape(b, l, h, d)

        def _delta_rule_chunkwise(q, k, v, beta, chunk=CHUNK):
            b, h, Lq, dk = q.shape
            dv = v.shape[-1]
            q = _l2norm(q)
            k = _l2norm(k)
            v = v * beta[..., None]
            k_beta = k * beta[..., None]
            n = Lq // chunk
            rs = lambda t: t.reshape(b, h, n, chunk, -1)
            q, k, v, k_beta = map(rs, (q, k, v, k_beta))
            idx = jnp.arange(chunk)
            strict_lower = idx[:, None] > idx[None, :]
            incl_lower = idx[:, None] >= idx[None, :]
            A = jnp.where(strict_lower, -jnp.einsum('bhnck,bhnjk->bhncj', k_beta, k), 0.0)
            for i in range(1, chunk):
                row = A[..., i, :]
                A = A.at[..., i, :].set(row + jnp.einsum('bhnj,bhnjc->bhnc', row, A))
            T = A + jnp.eye(chunk, dtype=A.dtype)
            u = jnp.einsum('bhncj,bhnjd->bhncd', T, v)
            w = jnp.einsum('bhncj,bhnjd->bhncd', T, k_beta)

            def step(S, inp):
                q_i, k_i, u_i, w_i = inp
                attn = jnp.where(incl_lower, jnp.einsum('bhck,bhjk->bhcj', q_i, k_i), 0.0)
                u_adj = u_i - jnp.einsum('bhck,bhkd->bhcd', w_i, S)
                o_i = jnp.einsum('bhck,bhkd->bhcd', q_i, S) + jnp.einsum('bhcj,bhjd->bhcd', attn, u_adj)
                S = S + jnp.einsum('bhck,bhcd->bhkd', k_i, u_adj)
                return (S, o_i)
            mv = lambda t: jnp.moveaxis(t, 2, 0)
            S0 = jnp.zeros((b, h, dk, dv), q.dtype)
            S, out = jax.lax.scan(step, S0, (mv(q), mv(k), mv(u), mv(w)))
            out = jnp.moveaxis(out, 0, 2).reshape(b, h, Lq, dv)
            return (out, S)

        def _stats(x):
            mean = jnp.mean(x, -1, keepdims=True)
            var = jnp.var(x, -1, keepdims=True)
            am = jnp.mean(jnp.abs(x), -1, keepdims=True)
            l2 = jnp.linalg.norm(x, axis=-1, keepdims=True)
            return jnp.concatenate([mean, var, am, l2], -1)

        def _forward(hs, Wq, Wk, Wv, cwq, cwk, cwv, Wb, Wid, alpha_id, firs, firl, gW1, gb1, gW2, gb2, log_temp, floor_param, conv_res_logit, o_norm_w, Wo):
            b, l, _ = hs.shape
            q = _short_conv_silu(hs @ Wq, cwq)
            k = _short_conv_silu(hs @ Wk, cwk)
            v = _short_conv_silu(hs @ Wv, cwv)
            q = q.reshape(b, l, NH, DK)
            k = k.reshape(b, l, NH, DK)
            v_direct = v.reshape(b, l, NH, DV)
            beta = jax.nn.sigmoid(hs @ Wb)
            tp = lambda t: jnp.transpose(t, (0, 2, 1, 3))
            delta_out, _S = _delta_rule_chunkwise(tp(q), tp(k), tp(v_direct), jnp.transpose(beta, (0, 2, 1)))
            delta_out = tp(delta_out)
            local_short = _fir(v_direct, firs)
            local_long = _fir(v_direct, firl)
            stats = jnp.concatenate([_stats(t) for t in (local_short, local_long, delta_out, v_direct)], -1)
            hs_exp = jnp.broadcast_to(hs[:, :, None, :], (b, l, NH, hs.shape[-1]))
            gin = jnp.concatenate([hs_exp, stats], -1)
            logits = jax.nn.gelu(gin @ gW1 + gb1, approximate=False) @ gW2 + gb2
            logits = logits / jnp.exp(log_temp)[None, None]
            probs = jax.nn.softmax(logits, -1)
            floor = FLOOR_NOW * jax.nn.sigmoid(floor_param)
            probs = probs * (1.0 - jnp.sum(floor, -1, keepdims=True)) + floor
            o = probs[..., 0:1] * local_short + probs[..., 1:2] * local_long + probs[..., 2:3] * delta_out + probs[..., 3:4] * v_direct
            o = o + jax.nn.sigmoid(conv_res_logit)[None, None, :, None] * local_short
            id_val = (hs @ Wid).reshape(b, l, NH, DV)
            o = o + alpha_id[None, None, :, None] * id_val
            o = o * jax.lax.rsqrt(jnp.mean(o * o, -1, keepdims=True) + 1e-05) * o_norm_w
            return o.reshape(b, l, NH * DV) @ Wo
        return _forward(hs, Wq, Wk, Wv, cwq, cwk, cwv, Wb, Wid, alpha_id, firs, firl, gW1, gb1, gW2, gb2, log_temp, floor_param, conv_res_logit, o_norm_w, Wo)

    def _L1_ffn_ref(x, gate_w, gate_b, w1, b1, w2, b2):
        import jax, jax.numpy as jnp
        import numpy as np
        D = 128
        N_EXP = 8
        TOP_K = 1
        b, s, d = x.shape
        xf = x.reshape(-1, d)
        logits = xf @ gate_w + gate_b
        pb = jax.nn.softmax(logits, axis=-1)
        _, idx = jax.lax.top_k(pb, TOP_K)
        sel = jnp.any(idx[:, :, None] == jnp.arange(N_EXP)[None, None, :], axis=1)
        weights = pb * sel

        def expert_step(acc, params):
            w1e, b1e, w2e, b2e, wgt = params
            h = jax.nn.gelu(xf @ w1e + b1e, approximate=False)
            y = h @ w2e + b2e
            return (acc + wgt[:, None] * y, None)
        out0 = jnp.zeros_like(xf)
        out, _ = jax.lax.scan(expert_step, out0, (w1, b1, w2, b2, weights.T))
        return out.reshape(b, s, d)
    x = L0_attn_x
    x = _layernorm(x + _L0_attn_ref(x, L0_attn_time_maa_x, L0_attn_time_maa_w, L0_attn_time_maa_k, L0_attn_time_maa_v, L0_attn_time_maa_r, L0_attn_time_maa_g, L0_attn_time_maa_w1, L0_attn_time_maa_w2, L0_attn_time_decay, L0_attn_time_decay_w1, L0_attn_time_decay_w2, L0_attn_W_r, L0_attn_W_k, L0_attn_W_v, L0_attn_W_g, L0_attn_W_o, L0_attn_ln_w, L0_attn_ln_b), axis=-1)
    x = _layernorm(x + _L0_ffn_ref(x, L0_ffn_gate_w, L0_ffn_w1, L0_ffn_b1, L0_ffn_w2, L0_ffn_b2), axis=-1)
    x = _layernorm(x + _L1_attn_ref(x, L1_attn_Wq, L1_attn_Wk, L1_attn_Wv, L1_attn_cwq, L1_attn_cwk, L1_attn_cwv, L1_attn_Wb, L1_attn_Wid, L1_attn_alpha_id, L1_attn_firs, L1_attn_firl, L1_attn_gW1, L1_attn_gb1, L1_attn_gW2, L1_attn_gb2, L1_attn_log_temp, L1_attn_floor_param, L1_attn_conv_res_logit, L1_attn_o_norm_w, L1_attn_Wo), axis=-1)
    x = _layernorm(x + _L1_ffn_ref(x, L1_ffn_gate_w, L1_ffn_gate_b, L1_ffn_w1, L1_ffn_b1, L1_ffn_w2, L1_ffn_b2), axis=-1)
    return x

_drawn_inputs = setup_inputs


def setup_inputs(seed=0):
    import zlib

    import numpy as np

    out = dict(_drawn_inputs(seed))
    spreads = {'L0_attn_ln_w': (1.0, 0.6),
     'L0_attn_ln_b': (0.0, 0.8),
     'L0_ffn_b1': (0.0, 0.27),
     'L0_ffn_b2': (0.0, 0.1),
     'L1_attn_alpha_id': (0.5, 0.6),
     'L1_attn_gb1': (0.0, 0.8),
     'L1_attn_log_temp': (0.0, 0.8),
     'L1_attn_floor_param': (0.0, 0.8),
     'L1_attn_conv_res_logit': (-2.944438934326172, 0.6),
     'L1_attn_o_norm_w': (1.0, 0.2),
     'L1_ffn_gate_b': (0.0, 0.633),
     'L1_ffn_b1': (0.0, 0.8),
     'L1_ffn_b2': (0.0, 0.45)}
    factors = {'L0_attn_time_maa_x': 8.0,
     'L0_attn_time_maa_w': 64.0,
     'L0_attn_time_maa_k': 3.443,
     'L0_attn_time_maa_v': 4.294,
     'L0_attn_time_maa_r': 3.667,
     'L0_attn_time_maa_g': 3.745,
     'L0_attn_time_maa_w1': 8.0,
     'L0_attn_time_maa_w2': 8.0,
     'L0_attn_time_decay': 2.813,
     'L0_attn_time_decay_w1': 64.0,
     'L0_attn_time_decay_w2': 64.0,
     'L1_attn_Wq': 31.22,
     'L1_attn_Wk': 38.587,
     'L1_attn_cwq': 52.946,
     'L1_attn_cwk': 29.358,
     'L1_attn_Wb': 36.649,
     'L1_attn_firs': 8.0,
     'L1_attn_firl': 4.572,
     'L1_attn_gW1': 8.0,
     'L1_attn_gW2': 8.0,
     'L1_attn_gb2': 8.0,
     'L1_ffn_gate_w': 2.959,
     'L1_ffn_w1': 6.145,
     'L1_ffn_w2': 5.549}
    for name, (base, spread) in spreads.items():
        noise = np.random.default_rng([zlib.crc32(name.encode()), seed]).standard_normal(out[name].shape)
        drawn = base * np.exp(spread * noise) if base else spread * noise
        out[name] = jnp.asarray(drawn.astype(out[name].dtype))
    for name, factor in factors.items():
        out[name] = (out[name] * factor).astype(out[name].dtype)
    return out
```

```python
from contextlib import ExitStack

import numpy as np

import concourse.bass as bass
from concourse import mybir

F32 = mybir.dt.float32
U32 = mybir.dt.uint32
ALU = mybir.AluOpType
ACT = mybir.ActivationFunctionType
AX_X = mybir.AxisListType.X

P = 128
SEQ = 256
NSEQ = 16
TOK = NSEQ * SEQ
GT = 4
GTOK = GT * P
GSEQ = GTOK // SEQ
NG = TOK // GTOK
LN_EPS = 1e-5


class Steps:

    def __init__(self, sem):
        self.sem, self.n = sem, 0

    def restart(self, eng):
        eng.sem_clear(self.sem)
        self.n = 0

    def mark(self, ins):
        ins.then_inc(self.sem, 1)
        self.n += 1
        return self.n


def shape_constants():
    p = np.arange(P)
    c = {}
    c["ident"] = np.eye(P)
    c["flip"] = np.eye(P)[::-1]
    j, i = (p % 32)[:, None], np.arange(32)[None, :]
    c["diag"] = np.concatenate([i < j, i >= j], 1)
    c["head4"] = ((p % 32) // 8)[:, None] == np.arange(4)[None, :]
    c["vhead"] = (p // 32)[:, None] == ((p % 32) // 8)[None, :]
    c["same8"] = (p // 8)[:, None] == (p // 8)[None, :]
    c["mean8"] = c["same8"] / 8.0
    c["center8"] = np.eye(P) - c["mean8"]
    c["experts"] = np.broadcast_to(np.arange(8.0), (P, 8))
    c["repeat"] = np.concatenate([p[:, None] == 32 * q + (p % 32)[None, :] for q in range(4)], 1)
    c["strict"] = -1.0 * (i > j)
    c["incl"] = 1.0 * (i >= j)
    c["same32"] = (p // 32)[:, None] == (p // 32)[None, :]
    c["mean32"] = c["same32"] / 32.0
    c["heads32"] = (p // 32)[:, None] == np.arange(4)[None, :]
    return {k: v.astype(np.float32) for k, v in c.items()}


def constant_columns():
    at, where = 0, {}
    for k, v in shape_constants().items():
        where[k] = (at, at + v.shape[1])
        at += v.shape[1]
    return where, at


def stream_rows(sp, x_rows, o_rows, xt, xo, s_x, s_xo, s_out):
    one = lambda rows, n: rows[bass.ds(n, 1)].rearrange("g p t c -> (g p) t c")

    def group(n, b, more):
        sp.wait_ge(s_out, 16 * n)
        if more:
            sp.dma_start(xt[1 - b][:], one(x_rows, n + 1)).then_inc(s_x[1 - b], 16)
        sp.wait_ge(s_xo, n + 1)
        sp.dma_start(one(o_rows, n), xo[b][:]).then_inc(s_out, 16)

    sp.dma_start(xt[0][:], one(x_rows, 0)).then_inc(s_x[0], 16)
    with sp.Fori(0, NG // 2 - 1) as it:
        for b in range(2):
            group(it * 2 + b, b, True)
    group(NG - 2, 0, True)
    group(NG - 1, 1, False)


def lion_stage(nc, sem, x_in, x_out, w, consts):
    where, ncon = constant_columns()
    D_MIX, D_DECAY, NF = 32, 64, 5
    x_rows = x_in.rearrange("(g t p) c -> g p t c", t=GT, p=P)
    o_rows = x_out.rearrange("(g t p) c -> g p t c", t=GT, p=P)
    ctx = ExitStack()
    with ctx:
        def sb(name, shape, dt=F32):
            return ctx.enter_context(nc.sbuf_tensor("a_" + name, shape, dt))

        def bank(name, shape=(P, GTOK)):
            return ctx.enter_context(nc.psum_tensor("a_" + name, list(shape), F32))

        con = sb("con", [P, ncon])
        C = {k: con[:, a:b] for k, (a, b) in where.items()}
        maa = sb("maa", [P, 6])
        maa_w1 = sb("maa_w1", [P, NF * D_MIX])
        maa_w2 = sb("maa_w2", [P, NF, P])
        dec_w1 = sb("dec_w1", [P, D_DECAY])
        dec_w2 = sb("dec_w2", [D_DECAY, P])
        decay = sb("decay", [P, 1])
        wT = sb("wT", [P, 5, P])
        lnwb = sb("lnwb", [P, 2])
        eps = sb("eps", [P, 2])
        xt = [sb(f"xt{i}", [P, GT, P]) for i in range(2)]
        xp = sb("xp", [P, GSEQ, SEQ + 2])
        dx = sb("dx", [P, GTOK])
        nb = sb("nb", [P, GTOK])
        xin = sb("xin", [P, GTOK])
        hid1 = sb("hid1", [P, GTOK])
        hid2 = sb("hid2", [D_MIX, GTOK])
        xf = [sb(f"xf{i}", [P, GTOK]) for i in range(NF)]
        hdec = sb("hdec", [D_DECAY, GTOK])
        ew = sb("ew", [P, GTOK])
        ones = sb("ones", [P, SEQ])
        E = sb("E", [P, 2, GTOK])
        ex = sb("ex", [P, 2, 2, GTOK])
        rk = sb("rk", [P, 4, GTOK])
        kx = sb("kx", [P, 2, GTOK // 32, 4, 32])
        vx = sb("vx", [P, GTOK // 32, P])
        vt = sb("vt", [P, GT, P])
        kt = sb("kt", [P, GT, P])
        st = sb("st", [P, GT, P])
        at = [sb(f"at{i}", [P, 4, 2, 160]) for i in range(2)]
        y = sb("y", [P, GTOK])
        sq = sb("sq", [P, GTOK])
        sd = sb("sd", [P, GTOK])
        rs = sb("rs", [P, GTOK])
        gs = sb("gs", [P, GTOK])
        yn = sb("yn", [P, GTOK])
        z = sb("z", [P, GT, P])
        bst = sb("bst", [P, GT, 6])
        mv = sb("mv", [P, GT, 2])
        sdv = sb("sdv", [P, GT])
        rsv = sb("rsv", [P, GT])
        xo = [sb(f"xo{i}", [P, GT, P]) for i in range(2)]
        S4 = bank("scores", (P, 4, GTOK))
        B = [S4[:, i, :] for i in range(4)] + [bank(f"b{i}")[:, :] for i in range(4, 8)]

        s_w, s_zero = sem("lion_weights_in"), sem("lion_constants_set")
        s_x = [sem(f"lion_rows_in_{i}") for i in range(2)]
        s_T, s_xp, s_xin = sem("lion_x_transposed"), sem("lion_x_channel_major"), sem("lion_mix_input")
        s_h, s_ht, s_mm = sem("lion_mix_hidden"), sem("lion_mix_tanh"), sem("lion_mix_factors")
        s_xf, s_hd, s_hdt = sem("lion_factor_inputs"), sem("lion_decay_hidden"), sem("lion_decay_tanh")
        s_wd, s_ew = sem("lion_decay_logits"), sem("lion_decay_exp")
        s_nf, s_ex = sem("lion_running_sums"), sem("lion_decay_factors")
        s_rk, s_g, s_gs = sem("lion_r_k_projected"), sem("lion_gate_projected"), sem("lion_gate_silu")
        s_v, s_vt = sem("lion_v_projected"), sem("lion_v_rows")
        s_vxp, s_vx = sem("lion_v_chunks_projected"), sem("lion_v_chunks")
        s_kd, s_ktp, s_kt = sem("lion_keys_scaled"), sem("lion_keys_transposed"), sem("lion_key_rows")
        s_kx = sem("lion_keys_spread")
        s_stp, s_st = sem("lion_states"), sem("lion_states_masked")
        s_sc, s_ata, s_atd = sem("lion_scores"), sem("lion_scores_copied"), sem("lion_diagonals_masked")
        s_y, s_ys, s_cen, s_sq = sem("lion_y"), sem("lion_y_copied"), sem("lion_y_centered"), sem("lion_y_squared")
        s_var, s_sd, s_yn = sem("lion_y_variance"), sem("lion_y_deviation"), sem("lion_y_gated")
        s_o, s_z, s_lsd, s_xo = sem("lion_projected"), sem("lion_sum_stats"), sem("lion_sum_deviation"), sem("lion_rows_ready")
        s_out = sem("lion_rows_out")
        s_dve, s_act = sem("lion_vector_steps"), sem("lion_scalar_steps")

        block = ctx.enter_context(nc.Block())

        @block.sync
        def _(sp):
            loads = [(con[:], consts), (maa[:], w["maa"]), (maa_w1[:], w["maa_w1"]),
                     (dec_w1[:], w["dec_w1"]), (dec_w2[:], w["dec_w2"]), (decay[:], w["decay"]),
                     (wT[:], w["wT"]), (lnwb[:], w["lnwb"])]
            for dst, src in loads:
                sp.dma_start(dst, src).then_inc(s_w, 16)
            sp.wait_ge(s_zero, 1)
            for f in range(NF):
                r = D_MIX * (f % 4)
                sp.dma_start(maa_w2[r:r + D_MIX, f, :], w["maa_w2"][f]).then_inc(s_w, 16)
            stream_rows(sp, x_rows, o_rows, xt, xo, s_x, s_xo, s_out)
            sp.wait_ge(s_out, 16 * NG)

        NW = 16 * (8 + NF)

        @block.tensor
        def _(pe):
            mm = nc.tensor.matmul
            pe.wait_ge(s_w, NW)
            pe.wait_ge(s_zero, 4)
            with pe.Fori(0, NG // 2) as it:
                for b in range(2):
                    n = it * 2 + b
                    pe.wait_ge(s_x[b], 16 * it + 16)
                    for t in range(GT):
                        i = nc.tensor.transpose(B[0][:, t * P:(t + 1) * P], xt[b][:, t, :], C["ident"])
                    i.then_inc(s_T, 1)
                    pe.wait_ge(s_xin, n + 1)
                    mm(B[1], maa_w1[:, 0:P], xin[:], start=True, stop=True)
                    mm(B[2][0:D_MIX, :], maa_w1[:, P:P + D_MIX], xin[:], start=True, stop=True).then_inc(s_h, 1)
                    pe.wait_ge(s_ht, n + 1)
                    for f in range(NF):
                        lhs, rhs = (maa_w2[:, f, :], hid1[:]) if f < 4 else (maa_w2[0:D_MIX, f, :], hid2[:])
                        mm(B[3 + f], lhs, rhs, start=True, stop=True).then_inc(s_mm, 1)
                    pe.wait_ge(s_xf, NF * n + 1)
                    mm(B[0][0:D_DECAY, :], dec_w1[:], xf[0][:], start=True, stop=True).then_inc(s_hd, 1)
                    pe.wait_ge(s_xf, NF * n + 2)
                    mm(B[3], wT[:, 1, :], xf[1][:], start=True, stop=True)
                    pe.wait_ge(s_hdt, n + 1)
                    mm(B[1], dec_w2[:], hdec[:], start=True, stop=True).then_inc(s_wd, 1)
                    pe.wait_ge(s_xf, NF * n + 3)
                    for t in range(GT):
                        i = mm(B[5][:, t * P:(t + 1) * P], xf[2][:, t * P:(t + 1) * P], wT[:, 2, :],
                               start=True, stop=True)
                    i.then_inc(s_v, 1)
                    pe.wait_ge(s_xf, NF * n + 4)
                    mm(B[2], wT[:, 0, :], xf[3][:], start=True, stop=True).then_inc(s_rk, 1)
                    pe.wait_ge(s_xf, NF * n + 5)
                    mm(B[4], wT[:, 3, :], xf[4][:], start=True, stop=True).then_inc(s_g, 1)
                    pe.wait_ge(s_vt, n + 1)
                    for c in range(GTOK // 32):
                        h = c // 4
                        if c % 4 == 0 and h >= 2:
                            pe.wait_ge(s_vx, 4 * n + h - 1)
                        i = mm(B[6 + h % 2][:, (c % 4) * P:(c % 4 + 1) * P],
                               C["repeat"][:, (c % 4) * P:(c % 4 + 1) * P], vt[:, h, :], start=True, stop=True)
                        if c % 4 == 3:
                            i.then_inc(s_vxp, 1)
                    pe.wait_ge(s_kd, n + 1)
                    for t in range(GT):
                        i = nc.tensor.transpose(B[0][:, t * P:(t + 1) * P],
                                                rk[:, 1 + 2 * (t % 2), t * P:(t + 1) * P], C["ident"])
                    i.then_inc(s_ktp, 1)
                    pe.wait_ge(s_kt, n + 1)
                    for t in range(GT):
                        i = mm(B[1][:, t * P:(t + 1) * P], kt[:, t ^ 1, :], vt[:, t ^ 1, :], start=True, stop=True)
                    i.then_inc(s_stp, 1)
                    pe.wait_ge(s_kx, n + 1)
                    pe.wait_ge(s_st, n + 1)

                    def attend(m):
                        t, h = m // 2, m % 2
                        pe.wait_ge(s_atd, 8 * n + m + 1)
                        if h == 0:
                            d = 2 * (1 - t % 2)
                            mm(B[5][:, t * P:(t + 1) * P], st[:, t, :], rk[:, d, t * P:(t + 1) * P],
                               start=(t == 0), stop=False, skip_group_check=True)
                        for g in range(4):
                            for q in (2 * h, 2 * h + 1):
                                k = 32 * q + 32
                                val = vx[:, 4 * t + q, 32 * g:32 * g + 32]
                                mm(B[5][32 * g:32 * g + 32, t * P:t * P + k], val, at[m % 2][:, g, q % 2, 0:k],
                                   start=False, stop=False, skip_group_check=True)
                                i = mm(B[5][32 * g:32 * g + 32, t * P + k - 32:(t + 1) * P], val,
                                       at[m % 2][:, g, q % 2, k:160],
                                       start=False, stop=(q == 3), skip_group_check=True)
                        if m == 7:
                            i.then_inc(s_y, 1)

                    for m in range(2 * GT):
                        t, h = m // 2, m % 2
                        if m:
                            pe.wait_ge(s_ata, 8 * n + m)
                        for g in range(4):
                            rows = slice(32 * g, 32 * g + 32)
                            for q in (2 * h, 2 * h + 1):
                                o = (q % 2) * 160
                                keys = lambda d: kx[rows, d, 4 * t + q].rearrange("p h j -> p (h j)")
                                mm(B[g][:, o:o + 32 * q + 32], keys(1),
                                   rk[rows, 2, t * P:t * P + 32 * q + 32],
                                   start=True, stop=True, skip_group_check=True)
                                i = mm(B[g][:, o + 32 * q + 32:o + 160], keys(0),
                                       rk[rows, 0, t * P + 32 * q:(t + 1) * P],
                                       start=True, stop=True, skip_group_check=True)
                        i.then_inc(s_sc, 1)
                        if m:
                            attend(m - 1)
                    attend(2 * GT - 1)
                    pe.wait_ge(s_ys, n + 1)
                    mm(B[6], C["center8"], y[:], start=True, stop=True).then_inc(s_cen, 1)
                    pe.wait_ge(s_sq, n + 1)
                    mm(B[7], C["mean8"], sq[:], start=True, stop=True).then_inc(s_var, 1)
                    pe.wait_ge(s_yn, n + 1)
                    for t in range(GT):
                        i = mm(B[4][:, t * P:(t + 1) * P], yn[:, t * P:(t + 1) * P], wT[:, 4, :], start=True, stop=True)
                    i.then_inc(s_o, 1)

        @block.gpsimd
        def _(pool):
            nc.gpsimd.memset(maa_w2[:], 0.0).then_inc(s_zero, 1)
            nc.gpsimd.memset(eps[:, 0:1], 64e-5).then_inc(s_zero, 1)
            nc.gpsimd.memset(eps[:, 1:2], LN_EPS).then_inc(s_zero, 1)
            nc.gpsimd.memset(ones[:], 1.0).then_inc(s_zero, 1)
            nc.gpsimd.memset(xp[:, :, 0:1], 0.0).then_inc(s_zero, 1)
            nc.gpsimd.memset(xp[:, :, SEQ + 1:SEQ + 2], 0.0).then_inc(s_zero, 1)

        @block.scalar
        def _(act):
            act.wait_ge(s_w, NW)
            act.wait_ge(s_zero, 6)
            op = nc.scalar.activation
            own = Steps(s_act)
            with act.Fori(0, NG // 2) as it:
                for b in range(2):
                    n = it * 2 + b
                    own.restart(act)
                    act.wait_ge(s_T, n + 1)
                    op(xp[:, :, 1:SEQ + 1], B[0].rearrange("p (s t) -> p s t", s=GSEQ), ACT.Copy).then_inc(s_xp, 1)
                    act.wait_ge(s_h, n + 1)
                    op(hid1[:], B[1], ACT.Tanh)
                    op(hid2[:], B[2][0:D_MIX, :], ACT.Tanh).then_inc(s_ht, 1)
                    act.wait_ge(s_hd, n + 1)
                    op(hdec[:], B[0][0:D_DECAY, :], ACT.Tanh).then_inc(s_hdt, 1)
                    act.wait_ge(s_wd, n + 1)
                    op(ew[:], B[1], ACT.Exp, bias=decay[:, 0:1]).then_inc(s_ew, 1)
                    act.wait_ge(s_v, n + 1)
                    op(vt[:].rearrange("p t c -> p (t c)"), B[5], ACT.Copy).then_inc(s_vt, 1)
                    act.wait_ge(s_nf, n + 1)
                    op(ex[:, 0, :, :], E[:], ACT.Exp).then_inc(s_ex, 1)
                    op(ex[:, 1, :, :], E[:], ACT.Exp, scale=-1.0).then_inc(s_ex, 1)
                    act.wait_ge(s_g, n + 1)
                    op(gs[:], B[4], ACT.Silu).then_inc(s_gs, 1)
                    act.wait_ge(s_ktp, n + 1)
                    op(kt[:].rearrange("p t c -> p (t c)"), B[0], ACT.Copy).then_inc(s_kt, 1)
                    for m in range(2 * GT):
                        t, h = m // 2, m % 2
                        act.wait_ge(s_sc, 8 * n + m + 1)
                        op(at[m % 2][:].rearrange("p g q k -> p g (q k)"), S4[:, :, 0:320], ACT.Copy).then_inc(s_ata, 1)
                    act.wait_ge(s_y, n + 1)
                    op(y[:], B[5], ACT.Copy).then_inc(s_ys, 1)
                    act.wait_ge(s_cen, n + 1)
                    op(sq[:], B[6], ACT.Square).then_inc(s_sq, 1)
                    act.wait_ge(s_var, n + 1)
                    op(sd[:], B[7], ACT.Sqrt, bias=eps[:, 0:1]).then_inc(s_sd, 1)
                    act.wait_ge(s_z, n + 1)
                    op(sdv[:], mv[:, :, 1], ACT.Sqrt, bias=eps[:, 1:2]).then_inc(s_lsd, 1)

        @block.vector
        def _(dve):
            v = nc.vector
            dve.wait_ge(s_w, NW)
            dve.wait_ge(s_zero, 6)
            own = Steps(s_dve)

            def then(ins):
                dve.wait_ge(s_dve, own.mark(ins))

            with dve.Fori(0, NG // 2) as it:
                for b in range(2):
                    n = it * 2 + b
                    own.restart(dve)
                    dve.wait_ge(s_xp, n + 1)
                    x3 = xp[:, :, 1:SEQ + 1]
                    seqs = lambda a: a.rearrange("p (s t) -> p s t", s=GSEQ)
                    then(v.tensor_tensor(seqs(nb[:]), xp[:, :, 0:SEQ], xp[:, :, 2:SEQ + 2], ALU.add))
                    then(v.scalar_tensor_tensor(seqs(dx[:]), seqs(nb[:]), 0.5, x3, ALU.mult, ALU.subtract))
                    v.scalar_tensor_tensor(seqs(xin[:]), seqs(dx[:]), maa[:, 0:1], x3, ALU.mult, ALU.add
                                           ).then_inc(s_xin, 1)
                    for f in range(NF):
                        dve.wait_ge(s_mm, NF * n + f + 1)
                        u = (nb, xin)[f % 2]
                        if f == 1:
                            dve.wait_ge(s_h, n + 1)
                        then(v.scalar_tensor_tensor(u[:], B[3 + f], maa[:, 1 + f:2 + f], dx[:], ALU.add, ALU.mult))
                        v.tensor_tensor(seqs(xf[f][:]), seqs(u[:]), x3, ALU.add).then_inc(s_xf, 1)
                    dve.wait_ge(s_ew, n + 1)
                    for s in range(GSEQ):
                        r = slice(s * SEQ, (s + 1) * SEQ)
                        i = own.mark(v.tensor_tensor_scan(E[:, 0, r], ones[:], ew[:, r], 0.0, ALU.mult, ALU.add))
                    dve.wait_ge(s_dve, i)
                    then(v.tensor_tensor(E[:, 1, :], E[:, 0, :], ew[:], ALU.subtract))
                    mid = sd[:, 0:2 * GSEQ]
                    then(v.tensor_copy(mid.rearrange("p (d s) -> p d s", d=2),
                                       E[:].rearrange("p d (s t) -> p d s t", s=GSEQ)[:, :, :, SEQ // 2]))
                    for d in range(2):
                        for s in range(GSEQ):
                            r = slice(s * SEQ, (s + 1) * SEQ)
                            i = own.mark(v.tensor_scalar(E[:, d, r], E[:, d, r], mid[:, 2 * d + s:2 * d + s + 1],
                                                         -60.0, ALU.subtract, ALU.max))
                    dve.wait_ge(s_dve, i)
                    v.tensor_scalar(E[:], E[:], 60.0, None, ALU.min).then_inc(s_nf, 1)
                    for h in range(2):
                        dve.wait_ge(s_vxp, 4 * n + h + 1)
                        v.tensor_tensor(vx[:, 4 * h:4 * h + 4, :], B[6 + h % 2].rearrange("p (c k) -> p c k", c=4),
                                        C["vhead"].unsqueeze(1).broadcast_to([P, 4, P]), ALU.mult).then_inc(s_vx, 1)
                    dve.wait_ge(s_ex, 2 * n + 2)
                    dve.wait_ge(s_rk, n + 1)
                    v.tensor_tensor(rk[:, 1, :], B[3], ex[:, 0, 0, :], ALU.mult)
                    i = own.mark(v.tensor_tensor(rk[:, 3, :], B[3], ex[:, 1, 1, :], ALU.mult))
                    v.tensor_tensor(rk[:, 0, :], B[2], ex[:, 1, 0, :], ALU.mult)
                    v.tensor_tensor(rk[:, 2, :], B[2], ex[:, 0, 1, :], ALU.mult).then_inc(s_kd, 1)
                    dve.wait_ge(s_dve, i)
                    for d in range(2):
                        for h in range(4):
                            i = v.tensor_scalar(kx[:, d, :, h, :], rk[:, 1 + 2 * d, :].rearrange("p (c j) -> p c j", j=32),
                                                C["head4"][:, h:h + 1], None, ALU.mult)
                    i.then_inc(s_kx, 1)
                    for h in range(2, 4):
                        dve.wait_ge(s_vxp, 4 * n + h + 1)
                        v.tensor_tensor(vx[:, 4 * h:4 * h + 4, :], B[6 + h % 2].rearrange("p (c k) -> p c k", c=4),
                                        C["vhead"].unsqueeze(1).broadcast_to([P, 4, P]), ALU.mult).then_inc(s_vx, 1)
                    dve.wait_ge(s_stp, n + 1)
                    v.tensor_tensor(st[:], B[1].rearrange("p (t c) -> p t c", t=GT),
                                    C["same8"].unsqueeze(1).broadcast_to([P, GT, P]), ALU.mult).then_inc(s_st, 1)
                    for m in range(2 * GT):
                        t, h = m // 2, m % 2
                        dve.wait_ge(s_ata, 8 * n + m + 1)
                        for q in (2 * h, 2 * h + 1):
                            d = at[m % 2][:, :, q % 2, 32 * q:32 * q + 64]
                            i = v.tensor_tensor(d, d, C["diag"].unsqueeze(1).broadcast_to([P, 4, 64]), ALU.mult)
                        i.then_inc(s_atd, 1)
                    dve.wait_ge(s_sd, n + 1)
                    then(v.reciprocal(rs[:], sd[:]))
                    then(v.tensor_tensor(nb[:], B[6], rs[:], ALU.mult))
                    then(v.tensor_scalar(xin[:], nb[:], lnwb[:, 0:1], lnwb[:, 1:2], ALU.mult, ALU.add))
                    dve.wait_ge(s_gs, n + 1)
                    v.tensor_tensor(yn[:], xin[:], gs[:], ALU.mult).then_inc(s_yn, 1)
                    dve.wait_ge(s_o, n + 1)
                    then(v.tensor_tensor(z[:], B[4].rearrange("p (t c) -> p t c", t=GT), xt[b][:], ALU.add))
                    for t in range(GT):
                        i = own.mark(v.bn_stats(bst[:, t, :], z[:, t, :]))
                    dve.wait_ge(s_dve, i)
                    for t in range(GT):
                        i = v.bn_aggr(mv[:, t, :], bst[:, t, :])
                    i.then_inc(s_z, 1)
                    dve.wait_ge(s_lsd, n + 1)
                    then(v.reciprocal(rsv[:], sdv[:]))
                    dve.wait_ge(s_x[b], 16 * it + 16)
                    for t in range(GT):
                        i = v.tensor_scalar(xo[b][:, t, :], z[:, t, :], mv[:, t, 0:1], rsv[:, t:t + 1],
                                            ALU.subtract, ALU.mult)
                    i.then_inc(s_xo, 1)


def moe_stage(nc, sem, tag, x_in, x_out, w, consts, topk, act_fn, gate_bias):
    where, ncon = constant_columns()
    NE, FC = 8, 4
    x_rows = x_in.rearrange("(g t p) c -> g p t c", t=GT, p=P)
    o_rows = x_out.rearrange("(g t p) c -> g p t c", t=GT, p=P)
    ctx = ExitStack()
    with ctx:
        def sb(name, shape, dt=F32):
            return ctx.enter_context(nc.sbuf_tensor(f"{tag}_{name}", shape, dt))

        con = sb("con", [P, ncon])
        C = {k: con[:, a:b] for k, (a, b) in where.items()}
        w1 = sb("w1", [P, NE, FC, P])
        w2 = sb("w2", [P, NE, FC, P])
        b1 = sb("b1", [P, NE, FC])
        b2 = sb("b2", [NE, P])
        gw = sb("gw", [P, NE])
        gb = sb("gb", [P, NE])
        eps = sb("eps", [P, 1])
        xt = [sb(f"xt{i}", [P, GT, P]) for i in range(2)]
        xo = [sb(f"xo{i}", [P, GT, P]) for i in range(2)]
        xT = sb("xT", [P, GTOK])
        lg = sb("lg", [P, GT, NE])
        mx = sb("mx", [P, GT])
        pr = sb("pr", [P, GT, NE])
        top = sb("top", [P, GT, 8])
        idx = sb("idx", [P, GT, 8], U32)
        idf = sb("idf", [P, GT, 8])
        wk = sb("wk", [P, GT, NE])
        wgt = sb("wgt", [P, GT, NE])
        wT = sb("wT", [NE, GTOK])
        h = [sb(f"h{i}", [P, FC, GTOK]) for i in range(2)]
        acc = sb("acc", [P, GT, P])
        bst = sb("bst", [P, GT, 6])
        mv = sb("mv", [P, GT, 2])
        sdv = sb("sdv", [P, GT])
        rsv = sb("rsv", [P, GT])
        B = [ctx.enter_context(nc.psum_tensor(f"{tag}_bank{i}", [P, GTOK], F32))[:, :] for i in range(8)]

        def s(name):
            return sem(f"{tag}_{name}")

        s_w, s_set, s_x, s_out, s_xo = s("weights_in"), s("constants_set"), [s("rows_in_0"), s("rows_in_1")], s("rows_out"), s("rows_ready")
        s_T, s_xT, s_lg, s_sh, s_pr = s("transposed"), s("channel_major"), s("logits"), s("logits_shifted"), s("exps")
        s_wg, s_wTp, s_wT, s_b2 = s("gates"), s("gates_transposed"), s("gates_by_expert"), s("bias_term")
        s_up, s_h, s_dn, s_acc = s("up"), s("hidden"), s("down"), s("accumulated")
        s_z, s_sd, s_dve = s("sum_stats"), s("sum_deviation"), s("vector_steps")

        block = ctx.enter_context(nc.Block())

        @block.sync
        def _(sp):
            loads = [(con[:], consts), (gw[:], w["gate_w"]), (w1[:], w["w1"]), (b1[:], w["b1"]),
                     (w2[:], w["w2"]), (b2[:], w["b2"])]
            if gate_bias:
                loads.append((gb[:], w["gate_b"].broadcast_to([P, NE])))
            for dst, src in loads:
                sp.dma_start(dst, src).then_inc(s_w, 16)
            stream_rows(sp, x_rows, o_rows, xt, xo, s_x, s_xo, s_out)
            sp.wait_ge(s_out, 16 * NG)

        NW = 16 * (6 + gate_bias)

        @block.gpsimd
        def _(pool):
            nc.gpsimd.memset(eps[:], LN_EPS).then_inc(s_set, 1)

        @block.tensor
        def _(pe):
            mm = nc.tensor.matmul
            pe.wait_ge(s_w, NW)
            with pe.Fori(0, NG // 2) as it:
                for b in range(2):
                    n = it * 2 + b
                    pe.wait_ge(s_x[b], 16 * it + 16)
                    for t in range(GT):
                        i = nc.tensor.transpose(B[0][:, t * P:(t + 1) * P], xt[b][:, t, :], C["ident"])
                    i.then_inc(s_T, 1)
                    pe.wait_ge(s_xT, n + 1)
                    for t in range(GT):
                        i = mm(B[7][:, t * NE:(t + 1) * NE], xT[:, t * P:(t + 1) * P], gw[:], start=True, stop=True)
                    i.then_inc(s_lg, 1)

                    def up(e):
                        for f in range(FC):
                            if e:
                                pe.wait_ge(s_h, FC * NE * n + FC * (e - 1) + f + 1)
                            mm(B[1 + f], w1[:, e, f, :], xT[:], start=True, stop=True).then_inc(s_up, 1)

                    def down(e):
                        pe.wait_ge(s_h, FC * NE * n + FC * e + FC)
                        if e >= 2:
                            pe.wait_ge(s_acc, NE * n + e - 1)
                        for t in range(GT):
                            for f in range(FC):
                                i = mm(B[5 + e % 2][:, t * P:(t + 1) * P], h[e % 2][:, f, t * P:(t + 1) * P],
                                       w2[:, e, f, :], start=(f == 0), stop=(f == FC - 1))
                        i.then_inc(s_dn, 1)

                    up(0)
                    up(1)
                    pe.wait_ge(s_wg, n + 1)
                    for t in range(GT):
                        i = nc.tensor.transpose(B[7][0:NE, t * P:(t + 1) * P], wgt[:, t, :], C["ident"])
                    i.then_inc(s_wTp, 1)
                    pe.wait_ge(s_wT, n + 1)
                    for t in range(GT):
                        i = mm(B[0][:, t * P:(t + 1) * P], wT[:, t * P:(t + 1) * P], b2[:], start=True, stop=True)
                    i.then_inc(s_b2, 1)
                    down(0)
                    for e in range(2, NE):
                        up(e)
                        down(e - 1)
                    down(NE - 1)

        @block.scalar
        def _(act):
            op = nc.scalar.activation
            act.wait_ge(s_w, NW)
            act.wait_ge(s_set, 1)
            with act.Fori(0, NG // 2) as it:
                for b in range(2):
                    n = it * 2 + b
                    act.wait_ge(s_T, n + 1)
                    op(xT[:], B[0], ACT.Copy).then_inc(s_xT, 1)
                    act.wait_ge(s_sh, n + 1)
                    op(pr[:], lg[:], ACT.Exp).then_inc(s_pr, 1)
                    for e in range(NE):
                        for f in range(FC):
                            act.wait_ge(s_up, FC * NE * n + FC * e + f + 1)
                            op(h[e % 2][:, f, :], B[1 + f], act_fn, bias=b1[:, e, f:f + 1]).then_inc(s_h, 1)
                        if e == 0:
                            act.wait_ge(s_wTp, n + 1)
                            op(wT[:], B[7][0:NE, :], ACT.Copy).then_inc(s_wT, 1)
                    act.wait_ge(s_z, n + 1)
                    op(sdv[:], mv[:, :, 1], ACT.Sqrt, bias=eps[:, 0:1]).then_inc(s_sd, 1)

        @block.vector
        def _(dve):
            v = nc.vector
            own = Steps(s_dve)
            dve.wait_ge(s_w, NW)

            def then(ins):
                dve.wait_ge(s_dve, own.mark(ins))

            with dve.Fori(0, NG // 2) as it:
                for b in range(2):
                    n = it * 2 + b
                    own.restart(dve)
                    dve.wait_ge(s_lg, n + 1)
                    raw = B[7][:, 0:GT * NE].rearrange("p (t e) -> p t e", t=GT)
                    if gate_bias:
                        then(v.tensor_tensor(lg[:], raw, gb[:].unsqueeze(1).broadcast_to([P, GT, NE]), ALU.add))
                    else:
                        then(v.tensor_copy(lg[:], raw))
                    then(v.tensor_reduce(mx[:], lg[:], AX_X, ALU.max))
                    v.tensor_tensor(lg[:], lg[:], mx[:].unsqueeze(2).broadcast_to([P, GT, NE]),
                                    ALU.subtract).then_inc(s_sh, 1)
                    dve.wait_ge(s_pr, n + 1)
                    then(v.tensor_reduce(mx[:], pr[:], AX_X, ALU.add))
                    then(v.reciprocal(mx[:], mx[:]))
                    then(v.tensor_tensor(pr[:], pr[:], mx[:].unsqueeze(2).broadcast_to([P, GT, NE]), ALU.mult))
                    for t in range(GT):
                        i = own.mark(v.max(top[:, t, :], pr[:, t, :]))
                    dve.wait_ge(s_dve, i)
                    for t in range(GT):
                        i = own.mark(v.max_index(idx[:, t, :], top[:, t, :], pr[:, t, :]))
                    dve.wait_ge(s_dve, i)
                    then(v.tensor_copy(idf[:], idx[:]))
                    for k in range(topk):
                        dst = (wgt, wk)[k]
                        for t in range(GT):
                            i = v.scalar_tensor_tensor(dst[:, t, :], C["experts"], idf[:, t, k:k + 1], pr[:, t, :],
                                                       ALU.is_equal, ALU.mult)
                            if k == topk - 1:
                                if topk == 1 and t == GT - 1:
                                    i.then_inc(s_wg, 1)
                                elif topk == 2:
                                    i = own.mark(i)
                    if topk == 2:
                        dve.wait_ge(s_dve, i)
                        v.tensor_tensor(wgt[:], wgt[:], wk[:], ALU.add).then_inc(s_wg, 1)
                    dve.wait_ge(s_wg, n + 1)
                    dve.wait_ge(s_b2, n + 1)
                    then(v.tensor_tensor(acc[:], B[0].rearrange("p (t c) -> p t c", t=GT), xt[b][:], ALU.add))
                    for e in range(NE):
                        dve.wait_ge(s_dn, NE * n + e + 1)
                        if e:
                            dve.wait_ge(s_acc, NE * n + e)
                        for t in range(GT):
                            i = v.scalar_tensor_tensor(acc[:, t, :], B[5 + e % 2][:, t * P:(t + 1) * P],
                                                       wgt[:, t, e:e + 1], acc[:, t, :], ALU.mult, ALU.add)
                        i.then_inc(s_acc, 1)
                    dve.wait_ge(s_acc, NE * n + NE)
                    for t in range(GT):
                        i = own.mark(v.bn_stats(bst[:, t, :], acc[:, t, :]))
                    dve.wait_ge(s_dve, i)
                    for t in range(GT):
                        i = v.bn_aggr(mv[:, t, :], bst[:, t, :])
                    i.then_inc(s_z, 1)
                    dve.wait_ge(s_sd, n + 1)
                    then(v.reciprocal(rsv[:], sdv[:]))
                    dve.wait_ge(s_x[b], 16 * it + 16)
                    for t in range(GT):
                        i = v.tensor_scalar(xo[b][:, t, :], acc[:, t, :], mv[:, t, 0:1], rsv[:, t:t + 1],
                                            ALU.subtract, ALU.mult)
                    i.then_inc(s_xo, 1)


NCH = SEQ // 32


def delta_project(nc, sem, keep, x_in, v_rows, s_rows, w, consts):
    where, ncon = constant_columns()
    x_tiles = x_in.rearrange("(g t p) c -> g p t c", t=GT, p=P)
    v_tiles = v_rows.rearrange("(g t p) c -> g p t c", t=GT, p=P)
    s_tiles = s_rows.rearrange("(g t p) c -> g p t c", t=GT, p=P)
    ctx = ExitStack()
    with ctx:
        def sb(name, shape, dt=F32):
            return ctx.enter_context(nc.sbuf_tensor("c_" + name, shape, dt))

        con = sb("con", [P, ncon])
        C = {k: con[:, a:b] for k, (a, b) in where.items()}
        wqkv = sb("wqkv", [P, 3, P])
        wb = sb("wb", [P, P])
        taps = sb("taps", [P, 3, 4])
        fir = sb("fir", [P, 3])
        eps = sb("eps", [P, 1])
        xt = [sb(f"xt{i}", [P, GT, P]) for i in range(2)]
        xT = sb("xT", [P, GTOK])
        pad = [sb(f"pad{i}", [P, GSEQ, SEQ + 3]) for i in range(3)]
        cv = [[sb(f"cv{i}{j}", [P, GTOK]) for j in range(2)] for i in range(3)]
        qk = [sb(f"qk{i}", [P, GTOK]) for i in range(2)]
        vs = sb("vs", [P, GSEQ, SEQ + 2])
        beta = sb("beta", [P, GTOK])
        sq = [sb(f"sq{i}", [P, GTOK]) for i in range(2)]
        sd = [sb(f"sd{i}", [P, GTOK]) for i in range(2)]
        kn = sb("kn", [P, GTOK])
        kq = sb("kq", [P, GTOK // 32, 2, 32])
        vb = sb("vb", [P, GTOK])
        kbs = sb("kbs", [P, GTOK])
        hs = [sb(f"hs{i}", [P, GTOK]) for i in range(3)]
        fa = [sb(f"fa{i}", [P, GTOK]) for i in range(2)]
        vt = sb("vt", [P, GT, P])
        ft = sb("ft", [P, GT, P])
        B = [ctx.enter_context(nc.psum_tensor(f"c_bank{i}", [P, GTOK], F32))[:, :] for i in range(8)]

        def s(name):
            return sem("delta_" + name)

        s_w, s_set, s_x, s_out = s("weights_in"), s("constants_set"), [s("rows_in_0"), s("rows_in_1")], s("rows_out")
        s_T, s_xT, s_p, s_pad, s_beta = s("transposed"), s("channel_major"), s("projected"), s("padded"), s("beta")
        s_cv, s_act, s_sq, s_ss, s_sd = s("convolved"), s("silu"), s("squared"), s("square_sums"), s("norms")
        s_n, s_kq, s_hs, s_keep = s("normalized"), s("score_operands"), s("head_rows"), s("kept")
        s_sc, s_m, s_fir, s_tp, s_rows = s("scores"), s("scores_masked"), s("short_fir"), s("value_rows"), s("value_rows_copied")
        s_dve = s("vector_steps")

        block = ctx.enter_context(nc.Block())
        one = lambda rows, n: rows[bass.ds(n, 1)].rearrange("g p t c -> (g p) t c")

        @block.sync
        def _(sp):
            for dst, src in [(con[:], consts), (wqkv[:], w["wqkv"]), (wb[:], w["wb"]), (taps[:], w["taps"]),
                             (fir[:], w["firs"])]:
                sp.dma_start(dst, src).then_inc(s_w, 16)

            def group(n, b, more):
                sp.wait_ge(s_out, 32 * n)
                if more:
                    sp.dma_start(xt[1 - b][:], one(x_tiles, n + 1)).then_inc(s_x[1 - b], 16)
                sp.wait_ge(s_rows, 2 * n + 2)
                sp.dma_start(one(v_tiles, n), vt[:]).then_inc(s_out, 16)
                sp.dma_start(one(s_tiles, n), ft[:]).then_inc(s_out, 16)

            sp.dma_start(xt[0][:], one(x_tiles, 0)).then_inc(s_x[0], 16)
            with sp.Fori(0, NG // 2 - 1) as it:
                for b in range(2):
                    group(it * 2 + b, b, True)
            group(NG - 2, 0, True)
            group(NG - 1, 1, False)
            sp.wait_ge(s_out, 32 * NG)

        @block.tensor
        def _(pe):
            mm = nc.tensor.matmul
            pe.wait_ge(s_w, 80)
            with pe.Fori(0, NG // 2) as it:
                for b in range(2):
                    n = it * 2 + b
                    pe.wait_ge(s_x[b], 16 * it + 16)
                    for t in range(GT):
                        i = nc.tensor.transpose(B[0][:, t * P:(t + 1) * P], xt[b][:, t, :], C["ident"])
                    i.then_inc(s_T, 1)
                    pe.wait_ge(s_xT, n + 1)
                    for k in range(3):
                        mm(B[1 + k], wqkv[:, k, :], xT[:], start=True, stop=True).then_inc(s_p, 1)
                    mm(B[4], wb[:], xT[:], start=True, stop=True).then_inc(s_p, 1)
                    for k in range(2):
                        pe.wait_ge(s_sq, 2 * n + k + 1)
                        mm(B[5 + k], C["same32"], sq[k][:], start=True, stop=True).then_inc(s_ss, 1)
                    for t in range(GT):
                        o = (t % 2) * P + 2
                        i = nc.tensor.transpose(B[7][:, t * P:(t + 1) * P], vs[:, t // 2, o:o + P], C["ident"])
                    i.then_inc(s_tp, 1)
                    pe.wait_ge(s_fir, n + 1)
                    for t in range(GT):
                        i = nc.tensor.transpose(B[0][:, t * P:(t + 1) * P], fa[0][:, t * P:(t + 1) * P], C["ident"])
                    i.then_inc(s_tp, 1)
                    pe.wait_ge(s_w, 80)
                    pe.wait_ge(s_kq, n + 1)
                    for c in range(GTOK // 32):
                        for h in range(4):
                            r = slice(32 * h, 32 * h + 32)
                            i = mm(B[1 + c // NCH][r, (c % NCH) * 64:(c % NCH) * 64 + 64], kn[r, 32 * c:32 * c + 32],
                                   kq[r, c].rearrange("p k c -> p (k c)"), start=True, stop=True,
                                   skip_group_check=True)
                        if c % NCH == NCH - 1:
                            i.then_inc(s_sc, 1)
                    pe.wait_ge(s_m, 2 * n + 2)
                    pe.wait_ge(s_rows, 2 * n + 2)

        @block.gpsimd
        def _(pool):
            nc.gpsimd.memset(eps[:], 1e-6).then_inc(s_set, 1)
            for k in range(3):
                nc.gpsimd.memset(pad[k][:, :, 0:3], 0.0).then_inc(s_set, 1)
            nc.gpsimd.memset(vs[:, :, 0:2], 0.0).then_inc(s_set, 1)
            with pool.Fori(0, NG) as n:
                seqs = bass.ds(n * GSEQ, GSEQ)
                view = lambda a: a.rearrange("p (s n c) -> p s n c", s=GSEQ, c=32)
                place = lambda a: a[:, :, seqs, :].rearrange("p n s c -> p s n c")
                pool.wait_ge(s_kq, n + 1)
                nc.gpsimd.tensor_copy(place(keep["q"]), kq[:, :, 1, :].rearrange("p (s n) c -> p s n c", s=GSEQ)
                                      ).then_inc(s_keep, 1)
                for k, name in enumerate(("k", "kb", "vb")):
                    pool.wait_ge(s_hs, 3 * n + k + 1)
                    nc.gpsimd.tensor_copy(place(keep[name]), view(hs[k][:])).then_inc(s_keep, 1)

        @block.scalar
        def _(act):
            op = nc.scalar.activation
            seqs = lambda a: a.rearrange("p (s t) -> p s t", s=GSEQ)
            act.wait_ge(s_w, 80)
            act.wait_ge(s_set, 5)
            with act.Fori(0, NG) as n:
                act.wait_ge(s_T, n + 1)
                op(xT[:], B[0], ACT.Copy).then_inc(s_xT, 1)
                for k in range(3):
                    act.wait_ge(s_p, 4 * n + k + 1)
                    op(pad[k][:, :, 3:SEQ + 3], seqs(B[1 + k]), ACT.Copy).then_inc(s_pad, 1)
                act.wait_ge(s_p, 4 * n + 4)
                op(beta[:], B[4], ACT.Sigmoid).then_inc(s_beta, 1)
                for k in range(3):
                    act.wait_ge(s_cv, 3 * n + k + 1)
                    op(seqs(qk[k][:]) if k < 2 else vs[:, :, 2:SEQ + 2], seqs(cv[k][1][:]), ACT.Silu).then_inc(s_act, 1)
                for k in range(2):
                    act.wait_ge(s_act, 3 * n + k + 1)
                    op(sq[k][:], qk[k][:], ACT.Square).then_inc(s_sq, 1)
                for k in range(2):
                    act.wait_ge(s_ss, 2 * n + k + 1)
                    op(sd[k][:], B[5 + k], ACT.Sqrt, bias=eps[:, 0:1]).then_inc(s_sd, 1)
                act.wait_ge(s_out, 32 * n)
                act.wait_ge(s_tp, 2 * n + 1)
                op(vt[:].rearrange("p t c -> p (t c)"), B[7], ACT.Copy).then_inc(s_rows, 1)
                act.wait_ge(s_tp, 2 * n + 2)
                op(ft[:].rearrange("p t c -> p (t c)"), B[0], ACT.Copy).then_inc(s_rows, 1)

        @block.vector
        def _(dve):
            v = nc.vector
            own = Steps(s_dve)
            seqs = lambda a: a.rearrange("p (s t) -> p s t", s=GSEQ)
            chunks = lambda a: a.rearrange("p (c j) -> p c j", j=32)
            dve.wait_ge(s_w, 80)
            dve.wait_ge(s_set, 5)

            def then(ins):
                dve.wait_ge(s_dve, own.mark(ins))

            with dve.Fori(0, NG) as n:
                own.restart(dve)
                tap = [0, 0, 0]
                for k in range(3):
                    dve.wait_ge(s_pad, 3 * n + k + 1)
                    tap[k] = own.mark(v.tensor_scalar(seqs(cv[k][0][:]), pad[k][:, :, 0:SEQ], taps[:, k, 0:1], None, ALU.mult))
                for j in range(1, 4):
                    for k in range(3):
                        dve.wait_ge(s_dve, tap[k])
                        ins = v.scalar_tensor_tensor(seqs(cv[k][j % 2][:]), pad[k][:, :, j:SEQ + j], taps[:, k, j:j + 1],
                                                     seqs(cv[k][1 - j % 2][:]), ALU.mult, ALU.add)
                        if j < 3:
                            tap[k] = own.mark(ins)
                        else:
                            ins.then_inc(s_cv, 1)
                dve.wait_ge(s_act, 3 * n + 3)
                then(v.tensor_scalar(seqs(fa[0][:]), vs[:, :, 0:SEQ], fir[:, 0:1], None, ALU.mult))
                then(v.scalar_tensor_tensor(seqs(fa[1][:]), vs[:, :, 1:SEQ + 1], fir[:, 1:2], seqs(fa[0][:]), ALU.mult, ALU.add))
                v.scalar_tensor_tensor(seqs(fa[0][:]), vs[:, :, 2:SEQ + 2], fir[:, 2:3], seqs(fa[1][:]),
                                       ALU.mult, ALU.add).then_inc(s_fir, 1)
                dve.wait_ge(s_beta, n + 1)
                i = own.mark(v.tensor_tensor(seqs(vb[:]), vs[:, :, 2:SEQ + 2], seqs(beta[:]), ALU.mult))
                for k in (1, 0):
                    dve.wait_ge(s_sd, 2 * n + k + 1)
                    then(v.reciprocal(cv[k][0][:], sd[k][:]))
                    if k:
                        then(v.tensor_tensor(kn[:], qk[1][:], cv[1][0][:], ALU.mult))
                        own_kb = own.mark(v.tensor_tensor(kbs[:], kn[:], beta[:], ALU.mult))
                        v.tensor_tensor(kq[:, :, 0, :], chunks(kn[:]), chunks(beta[:]), ALU.mult)
                    else:
                        v.tensor_tensor(kq[:, :, 1, :], chunks(qk[0][:]), chunks(cv[0][0][:]), ALU.mult).then_inc(s_kq, 1)
                dve.wait_ge(s_dve, own_kb)
                v.transpose(hs[0][:], kn[:]).then_inc(s_hs, 1)
                v.transpose(hs[1][:], kbs[:]).then_inc(s_hs, 1)
                v.transpose(hs[2][:], vb[:]).then_inc(s_hs, 1)
                for q in range(GSEQ):
                    dve.wait_ge(s_sc, 2 * n + q + 1)
                    sc = B[1 + q].rearrange("p (n k c) -> p n k c", n=NCH, k=2)
                    for k, (mask, dst) in enumerate((("strict", "A"), ("incl", "attn"))):
                        out = keep[dst][:, :, bass.ds(n * GSEQ + q, 1), :].rearrange("p n s c -> p n (s c)")
                        i = v.tensor_tensor(out, sc[:, :, k, :], C[mask].unsqueeze(1).broadcast_to([P, NCH, 32]), ALU.mult)
                    i.then_inc(s_m, 1)
                dve.wait_ge(s_keep, 4 * n + 4)


def delta_invert(nc, sem, keep, long_fir, v_rows, w, consts):
    where, ncon = constant_columns()
    NT, GC = TOK // P, 32
    v_tiles = v_rows.rearrange("(t p) c -> p t c", p=P)
    rev = w["firl"]
    span = rev.shape[1]
    ctx = ExitStack()
    with ctx:
        def sb(name, shape, dt=F32):
            return ctx.enter_context(nc.sbuf_tensor("i_" + name, shape, dt))

        con = sb("con", [P, ncon])
        C = {k: con[:, a:b] for k, (a, b) in where.items()}
        M = sb("M", [P, 32, 4, 32])
        tmp = [sb(f"tmp{i}", [P, 4096 // 8]) for i in range(2)]
        vtok = sb("vtok", [P, NT, P])
        toe = [sb(f"toe{i}", [P, GC, 192]) for i in range(1)]
        R = [ctx.enter_context(nc.psum_tensor(f"i_fir{i}", [P, 512], F32))[:, :] for i in range(4)]
        Q = [ctx.enter_context(nc.psum_tensor(f"i_bank{i}", [P, 512], F32))[:, :] for i in range(4)]

        def s(name):
            return sem("invert_" + name)

        s_flip, s_rev = s("flipped"), s("flipped_copied")
        s_w, s_v, s_toe, s_fir, s_long = s("constants_in"), s("values_in"), s("toeplitz_in"), s("fir"), s("fir_copied")
        s_at, s_M, s_done, s_ut, s_U, s_dve = s("chunks_transposed"), s("chunk_rows"), s("inverted"), s("back_transposed"), s("kept"), s("vector_steps")
        block = ctx.enter_context(nc.Block())

        @block.sync
        def _(sp):
            sp.dma_start(con[:], consts).then_inc(s_w, 16)
            sp.dma_start(vtok[:], v_tiles).then_inc(s_v, 16)
            for r in range(P // GC):
                if r:
                    sp.wait_ge(s_fir, 2 * r)
                src = bass.AP(rev.tensor, rev.offset + r * GC * span, [[1, P], [span, GC], [1, 192]])
                sp.dma_start(toe[0][:], src).then_inc(s_toe, 16)

        @block.tensor
        def _(pe):
            mm = nc.tensor.matmul
            pe.wait_ge(s_w, 16)
            A = keep["A"][:].rearrange("p n s c -> p (n s) c")
            for c in range(32):
                k = c // 4
                if c % 4 == 0 and k >= 4:
                    pe.wait_ge(s_M, k - 3)
                i = nc.tensor.transpose(Q[k % 4][:, (c % 4) * P:(c % 4 + 1) * P], A[:, :, c], C["ident"])
                if c % 4 == 3:
                    i.then_inc(s_at, 1)
            pe.wait_ge(s_v, 16)
            for k in range(8):
                if k >= 4:
                    pe.wait_ge(s_rev, k - 3)
                mm(R[k % 4], C["flip"], vtok[:, 4 * k:4 * k + 4, :].rearrange("p t c -> p (t c)"),
                   start=True, stop=True).then_inc(s_flip, 1)
            pe.wait_ge(s_rev, 8)
            for r in range(P // GC):
                pe.wait_ge(s_toe, 16 * r + 16)
                for half in range(2):
                    k = 2 * r + half
                    if k >= 4:
                        pe.wait_ge(s_long, k - 3)
                    for j in range(16):
                        ch, out = r * GC + half * 16 + j, R[k % 4][:, j * NT:(j + 1) * NT]
                        mm(out, toe[0][:, half * 16 + j, 0:P], vtok[:, :, ch], start=True, stop=False,
                           skip_group_check=True)
                        i = mm(out.rearrange("p (s t) -> p s t", t=2)[0:64, :, 1], toe[0][0:64, half * 16 + j, P:192],
                               vtok[0:64, :, ch].rearrange("p (s t) -> p s t", t=2)[:, :, 0],
                               start=False, stop=True, skip_group_check=True)
                    i.then_inc(s_fir, 1)
            pe.wait_ge(s_done, 1)
            for c in range(32):
                k = c // 4
                pe.wait_ge(s_M, 8)
                if c % 4 == 0 and k >= 4:
                    pe.wait_ge(s_U, k - 3)
                i = nc.tensor.transpose(Q[k % 4][:, (c % 4) * P:(c % 4 + 1) * P],
                                        M[:, c].rearrange("p h j -> p (h j)"), C["ident"])
                if c % 4 == 3:
                    i.then_inc(s_ut, 1)

        @block.scalar
        def _(act):
            op = nc.scalar.activation
            for k in range(8):
                act.wait_ge(s_at, k + 1)
                op(M[:, 4 * k:4 * k + 4].rearrange("p c h j -> p (c h j)"), Q[k % 4], ACT.Copy).then_inc(s_M, 1)
            for k in range(8):
                act.wait_ge(s_flip, k + 1)
                op(vtok[:, 4 * k:4 * k + 4, :].rearrange("p t c -> p (t c)"), R[k % 4], ACT.Copy).then_inc(s_rev, 1)
            for k in range(8):
                act.wait_ge(s_fir, k + 1)
                op(long_fir[:, :, 16 * k:16 * k + 16].rearrange("p t c -> p c t"),
                   R[k % 4].rearrange("p (c t) -> p c t", t=NT), ACT.Copy).then_inc(s_long, 1)
            U = keep["A"][:].rearrange("p n s c -> p c (n s)")
            for k in range(8):
                act.wait_ge(s_ut, k + 1)
                op(U[:, 4 * k:4 * k + 4, :], Q[k % 4].rearrange("p (c m) -> p c m", c=4), ACT.Copy).then_inc(s_U, 1)

        @block.vector
        def _(dve):
            v = nc.vector
            dve.wait_ge(s_M, 8)
            done = [0, 0]
            own = Steps(s_dve)
            for j in range(1, 31):
                rows = 31 - j
                for pair in range(2):
                    hh = slice(2 * pair, 2 * pair + 2)
                    t = tmp[pair][:, 0:rows * 2 * j].rearrange("p (i h c) -> p i h c", h=2, c=j)
                    if done[pair]:
                        dve.wait_ge(s_dve, done[pair])
                    done[pair] = own.mark(v.tensor_tensor(t, M[:, j + 1:32, hh, j:j + 1].broadcast_to([P, rows, 2, j]),
                                                 M[:, j:j + 1, hh, 0:j].broadcast_to([P, rows, 2, j]), ALU.mult))
                for pair in range(2):
                    hh = slice(2 * pair, 2 * pair + 2)
                    out = M[:, j + 1:32, hh, 0:j]
                    t = tmp[pair][:, 0:rows * 2 * j].rearrange("p (i h c) -> p i h c", h=2, c=j)
                    dve.wait_ge(s_dve, done[pair])
                    done[pair] = own.mark(v.tensor_tensor(out, out, t, ALU.add))
            dve.wait_ge(s_dve, done[1])
            flat = M[:].rearrange("p i h c -> p (i h c)")
            for h in range(4):
                i = v.memset(flat[:, h * 32:h * 32 + 31 * 129 + 1:129], 1.0)
            i.then_inc(s_done, 1)


def delta_recur(nc, sem, keep, oT):
    ctx = ExitStack()
    with ctx:
        def sb(name, shape, dt=F32):
            return ctx.enter_context(nc.sbuf_tensor("r_" + name, shape, dt))

        names = ("A", "kb", "vb", "k", "q", "attn")
        step = [{k: sb(f"{k}{i}", [P, NSEQ, 32]) for k in names} for i in range(2)]
        wn = sb("wn", [P, NSEQ, 32])
        ua = sb("ua", [P, NSEQ, 32])
        S = sb("S", [P, NSEQ, 32])
        Bank = [ctx.enter_context(nc.psum_tensor(f"r_bank{i}", [P, NSEQ, 32], F32)) for i in range(6)]
        Bu, Bw, Bo, Bs = Bank[0:2], Bank[2], Bank[3:5], Bank[5]

        def s(name):
            return sem("recur_" + name)

        s_in, s_set, s_w, s_wn, s_u, s_ua = [s("chunks_in_0"), s("chunks_in_1")], s("state_zero"), s("w"), s("w_copied"), s("u"), s("u_copied")
        s_S, s_Sc, s_o, s_oc = s("state"), s("state_copied"), s("o"), s("o_copied")
        block = ctx.enter_context(nc.Block())

        @block.sync
        def _(sp):
            def load(n, b):
                for k in names:
                    sp.dma_start(step[b][k][:], keep[k][:, n]).then_inc(s_in[b], 16)

            load(0, 0)
            load(1, 1)
            for n in range(2, NCH):
                sp.wait_ge(s_o, n - 1)
                load(n, n % 2)

        @block.tensor
        def _(pe):
            mm = nc.tensor.matmul

            def heads(out, lhsT, rhs, first, last, fresh=False):
                for q in range(NSEQ):
                    for h in range(4):
                        r = slice(32 * h, 32 * h + 32)
                        i = mm(out[r, q, :], lhsT[r, q, :], rhs[r, q, :], start=fresh and q == 0, stop=last,
                               skip_group_check=True)
                return i

            pe.wait_ge(s_set, 2)
            count, loaded = pe.alloc_register("steps"), pe.alloc_register("loads")
            pe.reg_mov(count, 0)
            pe.reg_mov(loaded, 0)
            with pe.Fori(0, NCH // 2) as it:
                for b in range(2):
                    pe.reg_add(count, count, 1)
                    if b == 0:
                        pe.reg_add(loaded, loaded, 96)
                    c = step[b]
                    pe.wait_ge(s_set, 2)
                    pe.wait_ge(s_in[b], loaded)
                    heads(Bw, c["kb"], c["A"], True, True, fresh=True).then_inc(s_w, 1)
                    heads(Bu[b], c["A"], c["vb"], True, False, fresh=True)
                    pe.wait_ge(s_set, 2)
                    pe.wait_ge(s_wn, count)
                    pe.wait_ge(s_Sc, count)
                    heads(Bu[b], wn, S, False, True).then_inc(s_u, 1)
                    heads(Bo[b], S, c["q"], True, False, fresh=True)
                    pe.wait_ge(s_set, 2)
                    pe.wait_ge(s_ua, count)
                    heads(Bs, c["k"], ua, True, True).then_inc(s_S, 1)
                    heads(Bo[b], ua, c["attn"], False, True).then_inc(s_o, 1)

        @block.scalar
        def _(act):
            op = nc.scalar.activation
            with act.Fori(0, NCH // 2) as it:
                for b in range(2):
                    n = it * 2 + b
                    act.wait_ge(s_w, n + 1)
                    op(wn[:], Bw[:], ACT.Copy, scale=-1.0).then_inc(s_wn, 1)
                    act.wait_ge(s_o, n + 1)
                    op(oT[:, bass.ds(n, 1)].rearrange("p n s c -> p (n s) c"), Bo[b][:], ACT.Copy).then_inc(s_oc, 1)

        @block.vector
        def _(dve):
            v = nc.vector
            v.memset(Bs[:], 0.0).then_inc(s_set, 1)
            v.memset(S[:], 0.0).then_inc(s_set, 1)
            dve.wait_ge(s_set, 2)
            v.tensor_copy(S[:], Bs[:]).then_inc(s_Sc, 1)
            with dve.Fori(0, NCH // 2) as it:
                for b in range(2):
                    n = it * 2 + b
                    dve.wait_ge(s_u, n + 1)
                    v.tensor_copy(ua[:], Bu[b][:]).then_inc(s_ua, 1)
                    dve.wait_ge(s_S, n + 1)
                    v.tensor_copy(S[:], Bs[:]).then_inc(s_Sc, 1)


def gate_stage(nc, sem, oT, long_fir, v_rows, s_rows, x_in, x_out, w, consts):
    where, ncon = constant_columns()
    NH, NA = 4, 4
    TH = GT * NH
    x_tiles = x_in.rearrange("(g t p) c -> g p t c", t=GT, p=P)
    o_tiles = x_out.rearrange("(g t p) c -> g p t c", t=GT, p=P)
    v_tiles = v_rows.rearrange("(g t p) c -> g p t c", t=GT, p=P)
    s_tiles = s_rows.rearrange("(g t p) c -> g p t c", t=GT, p=P)
    ctx = ExitStack()
    with ctx:
        def sb(name, shape, dt=F32):
            return ctx.enter_context(nc.sbuf_tensor("g_" + name, shape, dt))

        con = sb("con", [P, ncon])
        C = {k: con[:, a:b] for k, (a, b) in where.items()}
        g1 = sb("g1", [P, P])
        g1s = sb("g1s", [P, P])
        gb1 = sb("gb1", [P, 1])
        gw2 = sb("gw2", [P, NA])
        wid = sb("wid", [P, P])
        wo = sb("wo", [P, P])
        onw = sb("onw", [P, 1])
        par = sb("par", [P, 3, NH * NA])
        crl = sb("crl", [P, NH])
        alpha = sb("alpha", [P, NH])
        itemp = sb("itemp", [P, NH * NA])
        floor = sb("floor", [P, NH, NA])
        keepf = sb("keepf", [P, NH])
        res = sb("res", [P, NH])
        eps = sb("eps", [P, 1])
        xt = [sb(f"xt{i}", [P, GT, P]) for i in range(2)]
        xo = [sb(f"xo{i}", [P, GT, P]) for i in range(2)]
        X = [sb(f"X{i}", [P, NA, TH, 32]) for i in range(2)]
        xc = sb("xc", [P, NA, TH, 32])
        od = [sb(f"od{i}", [P, GSEQ, NCH, 32]) for i in range(2)]
        xT = sb("xT", [P, GTOK])
        ss = sb("ss", [P, 4, NA * TH])
        stt = sb("stt", [P, TH, 32])
        sT = sb("sT", [P, GTOK])
        hid = sb("hid", [P, NH, GTOK])
        lg = sb("lg", [P, TH, NA])
        mx = sb("mx", [P, TH])
        pr = sb("pr", [P, TH, NA])
        o = sb("o", [P, TH, 32])
        o2 = sb("o2", [P, TH, 32])
        oc = sb("oc", [P, GTOK])
        z = sb("z", [P, GT, P])
        bst = sb("bst", [P, GT, 6])
        mv = sb("mv", [P, GT, 2])
        sdv = sb("sdv", [P, GT])
        rsv = sb("rsv", [P, GT])
        B = [ctx.enter_context(nc.psum_tensor(f"g_bank{i}", [P, GTOK], F32))[:, :] for i in range(8)]

        def s(name):
            return sem("gate_" + name)

        s_w, s_set, s_x, s_out, s_xo = s("weights_in"), s("constants_set"), [s("rows_in_0"), s("rows_in_1")], s("rows_out"), s("rows_ready")
        s_pa, s_pv = s("parameters_scalar"), s("parameters_vector")
        s_od, s_T, s_xT, s_Xl, s_Xd = s("delta_copied"), s("transposed"), s("channel_major"), s("long_branch"), s("delta_branch")
        s_xc, s_sq, s_ms, s_l2, s_st = s("centered"), s("squared"), s("mean_squares"), s("norms"), s("stats")
        s_stp, s_sT, s_h, s_hid, s_lg = s("stats_transposed"), s("stats_copied"), s("hidden"), s("gelu"), s("logits")
        s_sh, s_ex, s_id, s_o, s_o2 = s("logits_shifted"), s("exps"), s("identity_branch"), s("mixed"), s("mixed_squared")
        s_rms, s_rsd, s_on, s_ot, s_oc = s("mixed_mean_square"), s("mixed_deviation"), s("normed"), s("normed_transposed"), s("normed_copied")
        s_pj, s_z, s_sd, s_dve = s("projected"), s("sum_stats"), s("sum_deviation"), s("vector_steps")
        block = ctx.enter_context(nc.Block())
        one = lambda rows, n: rows[bass.ds(n, 1)].rearrange("g p t c -> (g p) t c")
        NW = 16 * 13

        @block.sync
        def _(sp):
            bc = lambda a, k: a.broadcast_to([P, k])
            loads = [(con[:], consts), (g1[:], w["g1"]), (g1s[:], w["g1s"]), (gb1[:], w["gb1"]), (gw2[:], w["gw2"]),
                     (wid[:], w["wid"]), (wo[:], w["wo"]), (onw[:], w["onw"]), (par[:, 0], bc(w["gb2"], 16)),
                     (par[:, 1], bc(w["log_temp"], 16)), (par[:, 2], bc(w["floor"], 16)), (crl[:], bc(w["crl"], 4)),
                     (alpha[:], bc(w["alpha"], 4))]
            for dst, src in loads:
                sp.dma_start(dst, src).then_inc(s_w, 16)
            flat = lambda a: a.rearrange("p (t h) c -> p t (h c)", t=GT)

            def load(n, b):
                sp.dma_start(xt[b][:], one(x_tiles, n)).then_inc(s_x[b], 16)
                sp.dma_start(flat(X[b][:, 0]), one(s_tiles, n)).then_inc(s_x[b], 16)
                sp.dma_start(flat(X[b][:, 3]), one(v_tiles, n)).then_inc(s_x[b], 16)

            def group(n, b, more):
                sp.wait_ge(s_out, 16 * n)
                if more:
                    load(n + 1, 1 - b)
                sp.wait_ge(s_xo, n + 1)
                sp.dma_start(one(o_tiles, n), xo[b][:]).then_inc(s_out, 16)

            load(0, 0)
            with sp.Fori(0, NG // 2 - 1) as it:
                for b in range(2):
                    group(it * 2 + b, b, True)
            group(NG - 2, 0, True)
            group(NG - 1, 1, False)
            sp.wait_ge(s_out, 16 * NG)

        @block.gpsimd
        def _(pool):
            nc.gpsimd.memset(eps[:], LN_EPS).then_inc(s_set, 1)
            nc.gpsimd.memset(stt[:], 0.0).then_inc(s_set, 1)
            with pool.Fori(0, NG // 2) as it:
                for b in range(2):
                    n = it * 2 + b
                    pool.wait_ge(s_x[b], 48 * it + 48)
                    nc.gpsimd.tensor_copy(od[b][:], oT[:, :, bass.ds(n * GSEQ, GSEQ), :].rearrange("p n s c -> p s n c")
                                          ).then_inc(s_od, 1)
                    nc.gpsimd.tensor_copy(X[b][:, 1].rearrange("p (t h) c -> p t (h c)", t=GT),
                                          long_fir[:, bass.ds(n * GT, GT), :]).then_inc(s_Xl, 1)

        @block.tensor
        def _(pe):
            mm = nc.tensor.matmul
            pe.wait_ge(s_w, NW)
            pe.wait_ge(s_pv, 1)
            with pe.Fori(0, NG // 2) as it:
                for b in range(2):
                    n = it * 2 + b
                    tiles = [slice(t * P, (t + 1) * P) for t in range(GT)]
                    pe.wait_ge(s_x[b], 48 * it + 48)
                    for t in range(GT):
                        i = nc.tensor.transpose(B[0][:, tiles[t]], xt[b][:, t, :], C["ident"])
                    i.then_inc(s_T, 1)
                    pe.wait_ge(s_od, n + 1)
                    for t in range(GT):
                        i = nc.tensor.transpose(B[1][:, tiles[t]],
                                                od[b][:].rearrange("p s n c -> p (s n c)")[:, tiles[t]], C["ident"])
                    i.then_inc(s_T, 1)
                    pe.wait_ge(s_xT, n + 1)
                    for t in range(GT):
                        i = mm(B[2][:, tiles[t]], xT[:, tiles[t]], wid[:], start=True, stop=True)
                    i.then_inc(s_id, 1)
                    pe.wait_ge(s_st, n + 1)
                    stats = stt[:].rearrange("p (t h) k -> p t (h k)", t=GT)
                    for t in range(GT):
                        i = nc.tensor.transpose(B[3][:, tiles[t]], stats[:, t, :], C["ident"])
                    i.then_inc(s_stp, 1)
                    for h in range(NH):
                        mm(B[4 + h], g1[:], xT[:], start=True, stop=False)
                    pe.wait_ge(s_sT, n + 1)
                    for h in range(NH):
                        r = slice(32 * h, 32 * h + 32)
                        mm(B[4 + h], g1s[r, :], sT[r, :], start=False, stop=True).then_inc(s_h, 1)
                    for h in range(NH):
                        pe.wait_ge(s_hid, 4 * n + h + 1)
                        for t in range(GT):
                            i = mm(B[1][:, (t * NH + h) * NA:(t * NH + h + 1) * NA], hid[:, h, tiles[t]], gw2[:],
                                   start=True, stop=True)
                    i.then_inc(s_lg, 1)
                    pe.wait_ge(s_on, n + 1)
                    for t in range(GT):
                        i = nc.tensor.transpose(B[0][:, tiles[t]],
                                                o2[:].rearrange("p (t h) c -> p t (h c)", t=GT)[:, t, :], C["ident"])
                    i.then_inc(s_ot, 1)
                    pe.wait_ge(s_oc, n + 1)
                    for t in range(GT):
                        i = mm(B[3][:, tiles[t]], oc[:, tiles[t]], wo[:], start=True, stop=True)
                    i.then_inc(s_pj, 1)

        @block.scalar
        def _(act):
            op = nc.scalar.activation
            act.wait_ge(s_w, NW)
            act.wait_ge(s_set, 2)
            op(itemp[:], par[:, 1], ACT.Exp, scale=-1.0).then_inc(s_pa, 1)
            op(floor[:].rearrange("p h a -> p (h a)"), par[:, 2], ACT.Sigmoid).then_inc(s_pa, 1)
            op(res[:], crl[:], ACT.Sigmoid).then_inc(s_pa, 1)
            with act.Fori(0, NG // 2) as it:
                for b in range(2):
                    n = it * 2 + b
                    act.wait_ge(s_T, 2 * n + 1)
                    op(xT[:], B[0], ACT.Copy).then_inc(s_xT, 1)
                    act.wait_ge(s_T, 2 * n + 2)
                    op(X[b][:, 2].rearrange("p a c -> p (a c)"), B[1], ACT.Copy).then_inc(s_Xd, 1)
                    act.wait_ge(s_xc, n + 1)
                    op(xc[:], xc[:], ACT.Square).then_inc(s_sq, 1)
                    act.wait_ge(s_ms, n + 1)
                    op(stt[:].rearrange("p j (a k) -> p a j k", k=4)[:, 0:NA, :, 3],
                       ss[:, 3].rearrange("p (a j) -> p a j", a=NA), ACT.Sqrt, scale=32.0).then_inc(s_l2, 1)
                    act.wait_ge(s_stp, n + 1)
                    op(sT[:], B[3], ACT.Copy).then_inc(s_sT, 1)
                    for h in range(NH):
                        act.wait_ge(s_h, 4 * n + h + 1)
                        op(hid[:, h, :], B[4 + h], ACT.Gelu, bias=gb1[:, 0:1]).then_inc(s_hid, 1)
                    act.wait_ge(s_sh, n + 1)
                    op(pr[:], lg[:], ACT.Exp).then_inc(s_ex, 1)
                    act.wait_ge(s_o, n + 1)
                    op(o2[:], o[:], ACT.Square).then_inc(s_o2, 1)
                    act.wait_ge(s_rms, n + 1)
                    op(mx[:], mx[:], ACT.Sqrt, bias=eps[:, 0:1], scale=1.0 / 32).then_inc(s_rsd, 1)
                    act.wait_ge(s_ot, n + 1)
                    op(oc[:], B[0], ACT.Copy).then_inc(s_oc, 1)
                    act.wait_ge(s_z, n + 1)
                    op(sdv[:], mv[:, :, 1], ACT.Sqrt, bias=eps[:, 0:1]).then_inc(s_sd, 1)

        @block.vector
        def _(dve):
            v = nc.vector
            own = Steps(s_dve)

            def then(ins):
                dve.wait_ge(s_dve, own.mark(ins))

            dve.wait_ge(s_w, NW)
            dve.wait_ge(s_set, 2)
            dve.wait_ge(s_pa, 3)
            own.restart(dve)
            then(v.tensor_scalar(floor[:], floor[:], 0.05, None, ALU.mult))
            then(v.tensor_reduce(keepf[:], floor[:], AX_X, ALU.add))
            then(v.tensor_scalar(keepf[:], keepf[:], -1.0, 1.0, ALU.mult, ALU.add))
            then(v.tensor_tensor(floor[:, :, 0], floor[:, :, 0], res[:], ALU.add))
            then(v.tensor_tensor(wid[:].rearrange("p (h c) -> p h c", h=NH), wid[:].rearrange("p (h c) -> p h c", h=NH),
                                 alpha[:].unsqueeze(2).broadcast_to([P, NH, 32]), ALU.mult))
            v.tensor_scalar(wo[:], wo[:], onw[:, 0:1], None, ALU.mult).then_inc(s_pv, 1)
            dve.wait_ge(s_pv, 1)
            tiles4 = lambda a: a.unsqueeze(1).broadcast_to([P, GT, NH * NA])
            with dve.Fori(0, NG // 2) as it:
                for b in range(2):
                    n = it * 2 + b
                    own.restart(dve)
                    dve.wait_ge(s_x[b], 48 * it + 48)
                    dve.wait_ge(s_Xl, n + 1)
                    dve.wait_ge(s_Xd, n + 1)
                    x64 = X[b][:].rearrange("p a j c -> p (a j) c")
                    c64 = xc[:].rearrange("p a j c -> p (a j) c")
                    st4 = stt[:].rearrange("p j (a k) -> p a j k", k=4)[:, 0:NA]
                    by_a = lambda k: ss[:, k].rearrange("p (a j) -> p a j", a=NA)
                    then(v.tensor_reduce(ss[:, 0], x64, AX_X, ALU.add))
                    v.tensor_reduce(ss[:, 1], x64, AX_X, ALU.add, apply_absolute_value=True)
                    then(v.tensor_scalar(ss[:, 0], ss[:, 0], 1.0 / 32, None, ALU.mult))
                    v.tensor_tensor(c64, x64, ss[:, 0].unsqueeze(2).broadcast_to([P, NA * TH, 32]), ALU.subtract
                                    ).then_inc(s_xc, 1)
                    v.tensor_copy(st4[:, :, :, 0], by_a(0))
                    v.tensor_scalar(st4[:, :, :, 2], by_a(1), 1.0 / 32, None, ALU.mult)
                    then(v.tensor_tensor(ss[:, 3], ss[:, 0], ss[:, 0], ALU.mult))
                    dve.wait_ge(s_sq, n + 1)
                    then(v.tensor_reduce(ss[:, 2], c64, AX_X, ALU.add))
                    v.scalar_tensor_tensor(ss[:, 3], ss[:, 2], 1.0 / 32, ss[:, 3], ALU.mult, ALU.add).then_inc(s_ms, 1)
                    dve.wait_ge(s_l2, n + 1)
                    v.tensor_scalar(st4[:, :, :, 1], by_a(2), 1.0 / 32, None, ALU.mult).then_inc(s_st, 1)
                    dve.wait_ge(s_lg, n + 1)
                    then(v.tensor_tensor(lg[:].rearrange("p (t h) a -> p t (h a)", t=GT),
                                         B[1][:, 0:TH * NA].rearrange("p (t k) -> p t k", t=GT), tiles4(par[:, 0]), ALU.add))
                    then(v.tensor_tensor(lg[:].rearrange("p (t h) a -> p t (h a)", t=GT),
                                         lg[:].rearrange("p (t h) a -> p t (h a)", t=GT), tiles4(itemp[:]), ALU.mult))
                    then(v.tensor_reduce(mx[:], lg[:], AX_X, ALU.max))
                    wide = lambda a, k: a.unsqueeze(2).broadcast_to([P, TH, k])
                    v.tensor_tensor(lg[:], lg[:], wide(mx[:], NA), ALU.subtract).then_inc(s_sh, 1)
                    dve.wait_ge(s_ex, n + 1)
                    then(v.tensor_reduce(mx[:], pr[:], AX_X, ALU.add))
                    then(v.reciprocal(mx[:], mx[:]))
                    then(v.tensor_tensor(mx[:].rearrange("p (t h) -> p t h", t=GT), mx[:].rearrange("p (t h) -> p t h", t=GT),
                                         keepf[:].unsqueeze(1).broadcast_to([P, GT, NH]), ALU.mult))
                    then(v.tensor_tensor(pr[:], pr[:], wide(mx[:], NA), ALU.mult))
                    then(v.tensor_tensor(pr[:].rearrange("p (t h) a -> p t (h a)", t=GT),
                                         pr[:].rearrange("p (t h) a -> p t (h a)", t=GT),
                                         tiles4(floor[:].rearrange("p h a -> p (h a)")), ALU.add))
                    for a in range(NA):
                        i = own.mark(v.tensor_tensor(xc[:, a], X[b][:, a], wide(pr[:, :, a], 32), ALU.mult))
                    dve.wait_ge(s_dve, i)
                    then(v.tensor_reduce(o[:], xc[:].rearrange("p a j c -> p j c a"), AX_X, ALU.add))
                    dve.wait_ge(s_id, n + 1)
                    v.tensor_tensor(o[:], o[:], B[2].rearrange("p (j c) -> p j c", c=32), ALU.add).then_inc(s_o, 1)
                    dve.wait_ge(s_o2, n + 1)
                    v.tensor_reduce(mx[:], o2[:], AX_X, ALU.add).then_inc(s_rms, 1)
                    dve.wait_ge(s_rsd, n + 1)
                    then(v.reciprocal(mx[:], mx[:]))
                    v.tensor_tensor(o2[:], o[:], wide(mx[:], 32), ALU.mult).then_inc(s_on, 1)
                    dve.wait_ge(s_pj, n + 1)
                    then(v.tensor_tensor(z[:], B[3].rearrange("p (t c) -> p t c", t=GT), xt[b][:], ALU.add))
                    for t in range(GT):
                        i = own.mark(v.bn_stats(bst[:, t, :], z[:, t, :]))
                    dve.wait_ge(s_dve, i)
                    for t in range(GT):
                        i = v.bn_aggr(mv[:, t, :], bst[:, t, :])
                    i.then_inc(s_z, 1)
                    dve.wait_ge(s_sd, n + 1)
                    then(v.reciprocal(rsv[:], sdv[:]))
                    for t in range(GT):
                        i = v.tensor_scalar(xo[b][:, t, :], z[:, t, :], mv[:, t, 0:1], rsv[:, t:t + 1],
                                            ALU.subtract, ALU.mult)
                    i.then_inc(s_xo, 1)


def delta_stage(nc, sem, x_in, x_out, v_rows, s_rows, w, consts):
    with ExitStack() as ctx:
        def sb(name, shape):
            return ctx.enter_context(nc.sbuf_tensor("keep_" + name, shape, F32))

        long_fir = sb("long_fir", [P, TOK // P, P])
        oT = sb("oT", [P, NCH, NSEQ, 32])
        with ExitStack() as inner:
            keep = {k: inner.enter_context(nc.sbuf_tensor("keep_" + k, [P, NCH, NSEQ, 32], F32))
                    for k in ("A", "kb", "vb", "k", "q", "attn")}
            delta_project(nc, sem, keep, x_in, v_rows, s_rows, w, consts)
            delta_invert(nc, sem, keep, long_fir, v_rows, w, consts)
            delta_recur(nc, sem, keep, oT)
        gate_stage(nc, sem, oT, long_fir, v_rows, s_rows, x_in, x_out, w, consts)


def host_layout(inp):
    a = {k: np.asarray(v) for k, v in inp.items()}
    col = lambda v: v.reshape(-1, 1)
    L = "L0_attn_"
    d = {}
    d["a_maa"] = np.stack([a[L + "time_maa_" + c].reshape(-1) for c in "xwkvrg"], 1)
    d["a_maa_w1"] = a[L + "time_maa_w1"]
    d["a_maa_w2"] = a[L + "time_maa_w2"]
    d["a_dec_w1"] = a[L + "time_decay_w1"]
    d["a_dec_w2"] = a[L + "time_decay_w2"]
    d["a_decay"] = col(a[L + "time_decay"])
    d["a_wT"] = np.stack([a[L + "W_" + c].T for c in "rkvgo"], 1)
    d["a_lnwb"] = np.stack([a[L + "ln_w"], a[L + "ln_b"]], 1)
    for tag, L in (("b", "L0_ffn_"), ("d", "L1_ffn_")):
        d[tag + "_gate_w"] = a[L + "gate_w"].T if tag == "b" else a[L + "gate_w"]
        if tag == "d":
            d[tag + "_gate_b"] = a[L + "gate_b"].reshape(1, -1)
        d[tag + "_w1"] = a[L + "w1"].transpose(1, 0, 2).reshape(P, 8, 4, P)
        d[tag + "_b1"] = a[L + "b1"].reshape(8, 4, P).transpose(2, 0, 1)
        d[tag + "_w2"] = a[L + "w2"].reshape(8, 4, P, P).transpose(2, 0, 1, 3)
        d[tag + "_b2"] = a[L + "b2"]
    delta_layout(a, d)
    return d


def delta_layout(a, d):
    L = "L1_attn_"
    d["c_wqkv"] = np.stack([a[L + "W" + c] for c in "qkv"], 1)
    d["c_wb"] = np.repeat(a[L + "Wb"], 32, axis=1)
    d["c_taps"] = np.stack([a[L + "cw" + c] for c in "qkv"], 1)
    d["c_firs"] = a[L + "firs"].reshape(P, 3)
    firl = a[L + "firl"].reshape(P, 63)
    d["c_firl"] = np.concatenate([np.zeros((P, 127), firl.dtype), firl[:, ::-1], np.zeros((P, 129), firl.dtype)], 1)
    d["c_g1"] = a[L + "gW1"][:P]
    g1s = np.zeros((4, 32, P), a[L + "gW1"].dtype)
    g1s[:, :16] = a[L + "gW1"][P:]
    d["c_g1s"] = g1s.reshape(P, P)
    d["c_gb1"] = a[L + "gb1"].reshape(P, 1)
    d["c_gw2"] = a[L + "gW2"]
    d["c_wid"] = a[L + "Wid"]
    d["c_wo"] = a[L + "Wo"]
    d["c_onw"] = np.tile(a[L + "o_norm_w"], 4).reshape(P, 1)
    d["c_gb2"] = np.tile(a[L + "gb2"], 4).reshape(1, 16)
    d["c_log_temp"] = a[L + "log_temp"].reshape(1, 16)
    d["c_floor"] = a[L + "floor_param"].reshape(1, 16)
    d["c_crl"] = a[L + "conv_res_logit"].reshape(1, 4)
    d["c_alpha"] = a[L + "alpha_id"].reshape(1, 4)


def block_program(nc, ins, out, scratch):
    pick = lambda tag: {k[2:]: v for k, v in ins.items() if k.startswith(tag + "_")}
    x1, x2, x3, v_rows, s_rows = scratch
    def stage(build, *args):
        sems = []

        def sem(name):
            sems.append(nc.alloc_semaphore(name=name))
            return sems[-1]

        build(nc, sem, *args)
        nc.all_engine_barrier()
        nc.clear_and_free_semaphores(sems)
        nc.all_engine_barrier()

    stage(lion_stage, ins["x"], x1, pick("a"), ins["consts"])
    stage(moe_stage, "b", x1, x2, pick("b"), ins["consts"], 2, ACT.Relu, False)
    stage(delta_stage, x2, x3, v_rows, s_rows, pick("c"), ins["consts"])
    stage(moe_stage, "d", x3, out, pick("d"), ins["consts"], 1, ACT.Gelu, True)


def kernel(**inputs):
    import concourse.bacc as _bacc
    from concourse.bass_utils import run_bass_kernel_spmd as _run

    given = {k: np.asarray(v) for k, v in inputs.items()}
    nc = _bacc.Bacc("TRN2", target_bir_lowering=False, num_devices=1)
    laid = {"x": given["L0_attn_x"].reshape(TOK, P),
            "consts": np.concatenate(list(shape_constants().values()), 1)}
    laid.update(host_layout(given))
    arrays, ins = {}, {}
    for name, a in laid.items():
        a = np.ascontiguousarray(a)
        arrays["in_" + name] = a
        ins[name] = nc.dram_tensor("in_" + name, a.shape, mybir.dt.from_np(a.dtype), kind="ExternalInput").ap()
    out = nc.dram_tensor("out_rows", (TOK, P), F32, kind="ExternalOutput").ap()
    scratch = [nc.dram_tensor(f"rows_{i}", (TOK, P), F32, kind="Internal").ap() for i in range(5)]
    block_program(nc, ins, out, scratch)
    r = _run(nc, [arrays], core_ids=[0])
    return r.results[0]["out_rows"].reshape(NSEQ, SEQ, P)
```

```python
from contextlib import ExitStack

import numpy as np

import concourse.bass as bass
from concourse import mybir

F32 = mybir.dt.float32
U32 = mybir.dt.uint32
I32 = mybir.dt.int32
ALU = mybir.AluOpType
ACT = mybir.ActivationFunctionType
AX_X = mybir.AxisListType.X

P = 128
SEQ = 256
NSEQ = 16
TOK = NSEQ * SEQ
GT = 4
GTOK = GT * P
GSEQ = GTOK // SEQ
NG = TOK // GTOK
LN_EPS = 1e-5


class Steps:

    def __init__(self, sem):
        self.sem, self.n = sem, 0

    def restart(self, eng):
        eng.sem_clear(self.sem)
        self.n = 0

    def mark(self, ins):
        ins.then_inc(self.sem, 1)
        self.n += 1
        return self.n


def shape_constants():
    p = np.arange(P)
    c = {}
    c["ident"] = np.eye(P)
    c["flip"] = np.eye(P)[::-1]
    j, i = (p % 32)[:, None], np.arange(32)[None, :]
    c["diag"] = np.concatenate([i < j, i >= j], 1)
    c["heads16"] = (p // 8)[:, None] == np.arange(16)[None, :]
    c["vhead"] = (p // 32)[:, None] == ((p % 32) // 8)[None, :]
    c["same8"] = (p // 8)[:, None] == (p // 8)[None, :]
    c["mean8"] = c["same8"] / 8.0
    c["center8"] = np.eye(P) - c["mean8"]
    c["experts"] = np.broadcast_to(np.arange(8.0), (P, 8))
    c["before"] = p[:, None] < p[None, :]
    c["ones"] = np.ones((P, P))
    c["limits"] = np.broadcast_to(np.arange(TOK // P) * float(P), (P, TOK // P))
    c["tiles"] = np.broadcast_to(np.arange(80.0), (P, 80))
    c["repeat"] = np.concatenate([p[:, None] == 32 * q + (p % 32)[None, :] for q in range(4)], 1)
    c["strict"] = -1.0 * (i > j)
    c["incl"] = 1.0 * (i >= j)
    c["same32"] = (p // 32)[:, None] == (p // 32)[None, :]
    c["mean32"] = c["same32"] / 32.0
    c["heads32"] = (p // 32)[:, None] == np.arange(4)[None, :]
    return {k: v.astype(np.float32) for k, v in c.items()}


def constant_columns():
    at, where = 0, {}
    for k, v in shape_constants().items():
        where[k] = (at, at + v.shape[1])
        at += v.shape[1]
    return where, at


def stream_rows(sp, x_rows, o_rows, xt, xo, s_x, s_xo, s_out):
    one = lambda rows, n: rows[bass.ds(n, 1)].rearrange("g p t c -> (g p) t c")

    def group(n, b, more):
        sp.wait_ge(s_out, 16 * n)
        if more:
            sp.dma_start(xt[1 - b][:], one(x_rows, n + 1)).then_inc(s_x[1 - b], 16)
        sp.wait_ge(s_xo, n + 1)
        sp.dma_start(one(o_rows, n), xo[b][:]).then_inc(s_out, 16)

    sp.dma_start(xt[0][:], one(x_rows, 0)).then_inc(s_x[0], 16)
    with sp.Fori(0, NG // 2 - 1) as it:
        for b in range(2):
            group(it * 2 + b, b, True)
    group(NG - 2, 0, True)
    group(NG - 1, 1, False)


def lion_stage(nc, sem, x_in, x_out, w, consts):
    where, ncon = constant_columns()
    D_MIX, D_DECAY, NF = 32, 64, 5
    x_rows = x_in.rearrange("(g t p) c -> g p t c", t=GT, p=P)
    o_rows = x_out.rearrange("(g t p) c -> g p t c", t=GT, p=P)
    ctx = ExitStack()
    with ctx:
        def sb(name, shape, dt=F32):
            return ctx.enter_context(nc.sbuf_tensor("a_" + name, shape, dt))

        def bank(name, shape=(P, GTOK)):
            return ctx.enter_context(nc.psum_tensor("a_" + name, list(shape), F32))

        con = sb("con", [P, ncon])
        C = {k: con[:, a:b] for k, (a, b) in where.items()}
        maa = sb("maa", [P, 6])
        maa_w1 = sb("maa_w1", [P, NF * D_MIX])
        maa_w2 = sb("maa_w2", [P, NF, P])
        dec_w1 = sb("dec_w1", [P, D_DECAY])
        dec_w2 = sb("dec_w2", [D_DECAY, P])
        decay = sb("decay", [P, 1])
        wT = sb("wT", [P, 5, P])
        lnwb = sb("lnwb", [P, 2])
        eps = sb("eps", [P, 2])
        xt = [sb(f"xt{i}", [P, GT, P]) for i in range(2)]
        xp = sb("xp", [P, GSEQ, SEQ + 2])
        dx = sb("dx", [P, GTOK])
        nb = sb("nb", [P, GTOK])
        xin = sb("xin", [P, GTOK])
        hid1 = sb("hid1", [P, GTOK])
        hid2 = sb("hid2", [D_MIX, GTOK])
        xf = [sb(f"xf{i}", [P, GTOK]) for i in range(NF)]
        hdec = sb("hdec", [D_DECAY, GTOK])
        ew = sb("ew", [P, GTOK])
        ones = sb("ones", [P, SEQ])
        E = sb("E", [P, 2, GTOK])
        ex = sb("ex", [P, 2, 2, GTOK])
        rk = sb("rk", [P, 4, GTOK])
        kx = [sb(f"kx{i}", [P, 2, GTOK // 32, 4, 32]) for i in range(4)]
        vx = sb("vx", [P, GTOK // 32, P])
        vt = sb("vt", [P, GT, P])
        kt = sb("kt", [P, GT, P])
        st = sb("st", [P, GT, P])
        at = [sb(f"at{i}", [P, 4, 2, 160]) for i in range(2)]
        y = sb("y", [P, GTOK])
        sq = sb("sq", [P, GTOK])
        sd = sb("sd", [P, GTOK])
        rs = sb("rs", [P, GTOK])
        gs = sb("gs", [P, GTOK])
        yn = sb("yn", [P, GTOK])
        z = sb("z", [P, GT, P])
        bst = sb("bst", [P, GT, 6])
        mv = sb("mv", [P, GT, 2])
        sdv = sb("sdv", [P, GT])
        rsv = sb("rsv", [P, GT])
        xo = [sb(f"xo{i}", [P, GT, P]) for i in range(2)]
        S4 = bank("scores", (P, 4, GTOK))
        B = [S4[:, i, :] for i in range(4)] + [bank(f"b{i}")[:, :] for i in range(4, 8)]

        s_w, s_zero = sem("lion_weights_in"), sem("lion_constants_set")
        s_x = [sem(f"lion_rows_in_{i}") for i in range(2)]
        s_T, s_xp, s_xin = sem("lion_x_transposed"), sem("lion_x_channel_major"), sem("lion_mix_input")
        s_h, s_ht, s_mm = sem("lion_mix_hidden"), sem("lion_mix_tanh"), sem("lion_mix_factors")
        s_xf, s_hd, s_hdt = sem("lion_factor_inputs"), sem("lion_decay_hidden"), sem("lion_decay_tanh")
        s_wd, s_ew = sem("lion_decay_logits"), sem("lion_decay_exp")
        s_nf, s_ex = sem("lion_running_sums"), sem("lion_decay_factors")
        s_rk, s_g, s_gs = sem("lion_r_k_projected"), sem("lion_gate_projected"), sem("lion_gate_silu")
        s_v, s_vt = sem("lion_v_projected"), sem("lion_v_rows")
        s_vxp, s_vx = sem("lion_v_chunks_projected"), sem("lion_v_chunks")
        s_kd, s_ktp, s_kt = sem("lion_keys_scaled"), sem("lion_keys_transposed"), sem("lion_key_rows")
        s_kx = sem("lion_keys_spread")
        s_stp, s_st = sem("lion_states"), sem("lion_states_masked")
        s_sc, s_ata, s_atd = sem("lion_scores"), sem("lion_scores_copied"), sem("lion_diagonals_masked")
        s_y, s_ys, s_cen, s_sq = sem("lion_y"), sem("lion_y_copied"), sem("lion_y_centered"), sem("lion_y_squared")
        s_var, s_sd, s_yn = sem("lion_y_variance"), sem("lion_y_deviation"), sem("lion_y_gated")
        s_o, s_z, s_lsd, s_xo = sem("lion_projected"), sem("lion_sum_stats"), sem("lion_sum_deviation"), sem("lion_rows_ready")
        s_out = sem("lion_rows_out")
        s_dve, s_act = sem("lion_vector_steps"), sem("lion_scalar_steps")

        block = ctx.enter_context(nc.Block())

        @block.sync
        def _(sp):
            loads = [(con[:], consts), (maa[:], w["maa"]), (maa_w1[:], w["maa_w1"]),
                     (dec_w1[:], w["dec_w1"]), (dec_w2[:], w["dec_w2"]), (decay[:], w["decay"]),
                     (wT[:], w["wT"]), (lnwb[:], w["lnwb"])]
            for dst, src in loads:
                sp.dma_start(dst, src).then_inc(s_w, 16)
            sp.wait_ge(s_zero, 1)
            for f in range(NF):
                r = D_MIX * (f % 4)
                sp.dma_start(maa_w2[r:r + D_MIX, f, :], w["maa_w2"][f]).then_inc(s_w, 16)
            stream_rows(sp, x_rows, o_rows, xt, xo, s_x, s_xo, s_out)
            sp.wait_ge(s_out, 16 * NG)

        NW = 16 * (8 + NF)

        @block.tensor
        def _(pe):
            mm = nc.tensor.matmul
            pe.wait_ge(s_w, NW)
            pe.wait_ge(s_zero, 4)
            with pe.Fori(0, NG // 2) as it:
                for b in range(2):
                    n = it * 2 + b
                    pe.wait_ge(s_x[b], 16 * it + 16)
                    for t in range(GT):
                        i = nc.tensor.transpose(B[0][:, t * P:(t + 1) * P], xt[b][:, t, :], C["ident"])
                    i.then_inc(s_T, 1)
                    pe.wait_ge(s_xin, n + 1)
                    mm(B[1], maa_w1[:, 0:P], xin[:], start=True, stop=True)
                    mm(B[2][0:D_MIX, :], maa_w1[:, P:P + D_MIX], xin[:], start=True, stop=True).then_inc(s_h, 1)
                    pe.wait_ge(s_ht, n + 1)
                    for f in range(NF):
                        lhs, rhs = (maa_w2[:, f, :], hid1[:]) if f < 4 else (maa_w2[0:D_MIX, f, :], hid2[:])
                        mm(B[3 + f], lhs, rhs, start=True, stop=True).then_inc(s_mm, 1)
                    pe.wait_ge(s_xf, NF * n + 1)
                    mm(B[0][0:D_DECAY, :], dec_w1[:], xf[0][:], start=True, stop=True).then_inc(s_hd, 1)
                    pe.wait_ge(s_xf, NF * n + 2)
                    mm(B[3], wT[:, 1, :], xf[1][:], start=True, stop=True)
                    pe.wait_ge(s_hdt, n + 1)
                    mm(B[1], dec_w2[:], hdec[:], start=True, stop=True).then_inc(s_wd, 1)
                    pe.wait_ge(s_xf, NF * n + 3)
                    for t in range(GT):
                        i = mm(B[5][:, t * P:(t + 1) * P], xf[2][:, t * P:(t + 1) * P], wT[:, 2, :],
                               start=True, stop=True)
                    i.then_inc(s_v, 1)
                    pe.wait_ge(s_xf, NF * n + 4)
                    mm(B[2], wT[:, 0, :], xf[3][:], start=True, stop=True).then_inc(s_rk, 1)
                    pe.wait_ge(s_xf, NF * n + 5)
                    mm(B[4], wT[:, 3, :], xf[4][:], start=True, stop=True).then_inc(s_g, 1)
                    pe.wait_ge(s_vt, n + 1)
                    for c in range(GTOK // 32):
                        h = c // 4
                        if c % 4 == 0 and h >= 2:
                            pe.wait_ge(s_vx, 4 * n + h - 1)
                        i = mm(B[6 + h % 2][:, (c % 4) * P:(c % 4 + 1) * P],
                               C["repeat"][:, (c % 4) * P:(c % 4 + 1) * P], vt[:, h, :], start=True, stop=True)
                        if c % 4 == 3:
                            i.then_inc(s_vxp, 1)
                    pe.wait_ge(s_kd, n + 1)
                    for t in range(GT):
                        i = nc.tensor.transpose(B[0][:, t * P:(t + 1) * P],
                                                rk[:, 1 + 2 * (t % 2), t * P:(t + 1) * P], C["ident"])
                    i.then_inc(s_ktp, 1)
                    pe.wait_ge(s_kt, n + 1)
                    for t in range(GT):
                        i = mm(B[1][:, t * P:(t + 1) * P], kt[:, t ^ 1, :], vt[:, t ^ 1, :], start=True, stop=True)
                    i.then_inc(s_stp, 1)
                    pe.wait_ge(s_st, n + 1)

                    def attend(m):
                        t, h = m // 2, m % 2
                        pe.wait_ge(s_atd, 8 * n + m + 1)
                        if h == 0:
                            d = 2 * (1 - t % 2)
                            mm(B[5][:, t * P:(t + 1) * P], st[:, t, :], rk[:, d, t * P:(t + 1) * P],
                               start=(t == 0), stop=False, skip_group_check=True)
                        for g in range(4):
                            for q in (2 * h, 2 * h + 1):
                                k = 32 * q + 32
                                val = vx[:, 4 * t + q, 32 * g:32 * g + 32]
                                mm(B[5][32 * g:32 * g + 32, t * P:t * P + k], val, at[m % 2][:, g, q % 2, 0:k],
                                   start=False, stop=False, skip_group_check=True)
                                i = mm(B[5][32 * g:32 * g + 32, t * P + k - 32:(t + 1) * P], val,
                                       at[m % 2][:, g, q % 2, k:160],
                                       start=False, stop=(q == 3), skip_group_check=True)
                        if m == 7:
                            i.then_inc(s_y, 1)

                    for m in range(2 * GT):
                        t, h = m // 2, m % 2
                        if m % 4 == 0:
                            pe.wait_ge(s_kx, 4 * n + 2 * (m // 4) + 2)
                        if m:
                            pe.wait_ge(s_ata, 8 * n + m)
                        for g in range(4):
                            for q in (2 * h, 2 * h + 1):
                                o = (q % 2) * 160
                                keys = lambda d: kx[g][:, d, 4 * t + q].rearrange("p h j -> p (h j)")
                                mm(B[g][:, o + 32:o + 160], keys(0), rk[:, 0, t * P:(t + 1) * P],
                                   start=True, stop=True, skip_group_check=True)
                                i = mm(B[g][:, o:o + 32 * q + 32], keys(1),
                                       rk[:, 2, t * P:t * P + 32 * q + 32],
                                       start=True, stop=True, skip_group_check=True)
                        i.then_inc(s_sc, 1)
                        if m:
                            attend(m - 1)
                    attend(2 * GT - 1)
                    pe.wait_ge(s_ys, n + 1)
                    mm(B[6], C["center8"], y[:], start=True, stop=True).then_inc(s_cen, 1)
                    pe.wait_ge(s_sq, n + 1)
                    mm(B[7], C["mean8"], sq[:], start=True, stop=True).then_inc(s_var, 1)
                    pe.wait_ge(s_yn, n + 1)
                    for t in range(GT):
                        i = mm(B[4][:, t * P:(t + 1) * P], yn[:, t * P:(t + 1) * P], wT[:, 4, :], start=True, stop=True)
                    i.then_inc(s_o, 1)

        @block.gpsimd
        def _(pool):
            nc.gpsimd.memset(maa_w2[:], 0.0).then_inc(s_zero, 1)
            nc.gpsimd.memset(eps[:, 0:1], 64e-5).then_inc(s_zero, 1)
            nc.gpsimd.memset(eps[:, 1:2], LN_EPS).then_inc(s_zero, 1)
            nc.gpsimd.memset(ones[:], 1.0).then_inc(s_zero, 1)
            nc.gpsimd.memset(xp[:, :, 0:1], 0.0).then_inc(s_zero, 1)
            nc.gpsimd.memset(xp[:, :, SEQ + 1:SEQ + 2], 0.0).then_inc(s_zero, 1)

        @block.scalar
        def _(act):
            act.wait_ge(s_w, NW)
            act.wait_ge(s_zero, 6)
            op = nc.scalar.activation
            own = Steps(s_act)
            with act.Fori(0, NG // 2) as it:
                for b in range(2):
                    n = it * 2 + b
                    own.restart(act)
                    act.wait_ge(s_T, n + 1)
                    op(xp[:, :, 1:SEQ + 1], B[0].rearrange("p (s t) -> p s t", s=GSEQ), ACT.Copy).then_inc(s_xp, 1)
                    act.wait_ge(s_h, n + 1)
                    op(hid1[:], B[1], ACT.Tanh)
                    op(hid2[:], B[2][0:D_MIX, :], ACT.Tanh).then_inc(s_ht, 1)
                    act.wait_ge(s_hd, n + 1)
                    op(hdec[:], B[0][0:D_DECAY, :], ACT.Tanh).then_inc(s_hdt, 1)
                    act.wait_ge(s_wd, n + 1)
                    op(ew[:], B[1], ACT.Exp, bias=decay[:, 0:1]).then_inc(s_ew, 1)
                    act.wait_ge(s_v, n + 1)
                    op(vt[:].rearrange("p t c -> p (t c)"), B[5], ACT.Copy).then_inc(s_vt, 1)
                    act.wait_ge(s_nf, n + 1)
                    op(ex[:, 0, :, :], E[:], ACT.Exp).then_inc(s_ex, 1)
                    op(ex[:, 1, :, :], E[:], ACT.Exp, scale=-1.0).then_inc(s_ex, 1)
                    act.wait_ge(s_g, n + 1)
                    op(gs[:], B[4], ACT.Silu).then_inc(s_gs, 1)

                    def spread(half):
                        for h in range(16):
                            i = op(kx[h // 4][:, 1, 8 * half:8 * half + 8, h % 4, :],
                                   rk[:, 3, half * 256:half * 256 + 256].rearrange("p (c j) -> p c j", j=32),
                                   ACT.Copy, scale=C["heads16"][:, h:h + 1])
                        i.then_inc(s_kx, 1)

                    act.wait_ge(s_ktp, n + 1)
                    op(kt[:].rearrange("p t c -> p (t c)"), B[0], ACT.Copy).then_inc(s_kt, 1)
                    spread(0)
                    for m in range(2 * GT):
                        t, h = m // 2, m % 2
                        if m == 1:
                            spread(1)
                        act.wait_ge(s_sc, 8 * n + m + 1)
                        op(at[m % 2][:].rearrange("p g q k -> p g (q k)"), S4[:, :, 0:320], ACT.Copy).then_inc(s_ata, 1)
                    act.wait_ge(s_y, n + 1)
                    op(y[:], B[5], ACT.Copy).then_inc(s_ys, 1)
                    act.wait_ge(s_cen, n + 1)
                    op(sq[:], B[6], ACT.Square).then_inc(s_sq, 1)
                    act.wait_ge(s_var, n + 1)
                    act.wait_ge(s_act, own.mark(op(sd[:], B[7], ACT.Ln, bias=eps[:, 0:1])))
                    op(rs[:], sd[:], ACT.Exp, scale=-0.5).then_inc(s_sd, 1)
                    act.wait_ge(s_z, n + 1)
                    op(sdv[:], mv[:, :, 1], ACT.Sqrt, bias=eps[:, 1:2]).then_inc(s_lsd, 1)

        @block.vector
        def _(dve):
            v = nc.vector
            dve.wait_ge(s_w, NW)
            dve.wait_ge(s_zero, 6)
            own = Steps(s_dve)

            def then(ins):
                dve.wait_ge(s_dve, own.mark(ins))

            with dve.Fori(0, NG // 2) as it:
                for b in range(2):
                    n = it * 2 + b
                    own.restart(dve)
                    dve.wait_ge(s_xp, n + 1)
                    x3 = xp[:, :, 1:SEQ + 1]
                    seqs = lambda a: a.rearrange("p (s t) -> p s t", s=GSEQ)
                    then(v.tensor_tensor(seqs(nb[:]), xp[:, :, 0:SEQ], xp[:, :, 2:SEQ + 2], ALU.add))
                    then(v.scalar_tensor_tensor(seqs(dx[:]), seqs(nb[:]), 0.5, x3, ALU.mult, ALU.subtract))
                    v.scalar_tensor_tensor(seqs(xin[:]), seqs(dx[:]), maa[:, 0:1], x3, ALU.mult, ALU.add
                                           ).then_inc(s_xin, 1)
                    for f in range(NF):
                        dve.wait_ge(s_mm, NF * n + f + 1)
                        u = (nb, xin)[f % 2]
                        if f == 1:
                            dve.wait_ge(s_h, n + 1)
                        then(v.scalar_tensor_tensor(u[:], B[3 + f], maa[:, 1 + f:2 + f], dx[:], ALU.add, ALU.mult))
                        v.tensor_tensor(seqs(xf[f][:]), seqs(u[:]), x3, ALU.add).then_inc(s_xf, 1)
                    dve.wait_ge(s_ew, n + 1)
                    for s in range(GSEQ):
                        r = slice(s * SEQ, (s + 1) * SEQ)
                        i = own.mark(v.tensor_tensor_scan(E[:, 0, r], ones[:], ew[:, r], 0.0, ALU.mult, ALU.add))
                    dve.wait_ge(s_dve, i)
                    then(v.tensor_tensor(E[:, 1, :], E[:, 0, :], ew[:], ALU.subtract))
                    mid = sd[:, 0:2 * GSEQ]
                    then(v.tensor_copy(mid.rearrange("p (d s) -> p d s", d=2),
                                       E[:].rearrange("p d (s t) -> p d s t", s=GSEQ)[:, :, :, SEQ // 2]))
                    for d in range(2):
                        for s in range(GSEQ):
                            r = slice(s * SEQ, (s + 1) * SEQ)
                            i = own.mark(v.tensor_scalar(E[:, d, r], E[:, d, r], mid[:, 2 * d + s:2 * d + s + 1],
                                                         -60.0, ALU.subtract, ALU.max))
                    dve.wait_ge(s_dve, i)
                    v.tensor_scalar(E[:], E[:], 60.0, None, ALU.min).then_inc(s_nf, 1)
                    for h in range(2):
                        dve.wait_ge(s_vxp, 4 * n + h + 1)
                        v.tensor_tensor(vx[:, 4 * h:4 * h + 4, :], B[6 + h % 2].rearrange("p (c k) -> p c k", c=4),
                                        C["vhead"].unsqueeze(1).broadcast_to([P, 4, P]), ALU.mult).then_inc(s_vx, 1)
                    dve.wait_ge(s_ex, 2 * n + 2)
                    dve.wait_ge(s_rk, n + 1)
                    v.tensor_tensor(rk[:, 1, :], B[3], ex[:, 0, 0, :], ALU.mult)
                    i = own.mark(v.tensor_tensor(rk[:, 3, :], B[3], ex[:, 1, 1, :], ALU.mult))
                    v.tensor_tensor(rk[:, 0, :], B[2], ex[:, 1, 0, :], ALU.mult)
                    v.tensor_tensor(rk[:, 2, :], B[2], ex[:, 0, 1, :], ALU.mult).then_inc(s_kd, 1)
                    dve.wait_ge(s_dve, i)

                    def spread(half):
                        for h in range(16):
                            i = v.tensor_scalar(kx[h // 4][:, 0, 8 * half:8 * half + 8, h % 4, :],
                                                rk[:, 1, half * 256:half * 256 + 256].rearrange("p (c j) -> p c j", j=32),
                                                C["heads16"][:, h:h + 1], None, ALU.mult)
                        i.then_inc(s_kx, 1)

                    spread(0)
                    for h in range(2, 4):
                        dve.wait_ge(s_vxp, 4 * n + h + 1)
                        v.tensor_tensor(vx[:, 4 * h:4 * h + 4, :], B[6 + h % 2].rearrange("p (c k) -> p c k", c=4),
                                        C["vhead"].unsqueeze(1).broadcast_to([P, 4, P]), ALU.mult).then_inc(s_vx, 1)
                    dve.wait_ge(s_stp, n + 1)
                    v.tensor_tensor(st[:], B[1].rearrange("p (t c) -> p t c", t=GT),
                                    C["same8"].unsqueeze(1).broadcast_to([P, GT, P]), ALU.mult).then_inc(s_st, 1)
                    for m in range(2 * GT):
                        t, h = m // 2, m % 2
                        if m == 1:
                            spread(1)
                        dve.wait_ge(s_ata, 8 * n + m + 1)
                        for q in (2 * h, 2 * h + 1):
                            d = at[m % 2][:, :, q % 2, 32 * q:32 * q + 64]
                            i = v.tensor_tensor(d, d, C["diag"].unsqueeze(1).broadcast_to([P, 4, 64]), ALU.mult)
                        i.then_inc(s_atd, 1)
                    dve.wait_ge(s_sd, n + 1)
                    then(v.tensor_tensor(nb[:], B[6], rs[:], ALU.mult))
                    then(v.tensor_scalar(xin[:], nb[:], lnwb[:, 0:1], lnwb[:, 1:2], ALU.mult, ALU.add))
                    dve.wait_ge(s_gs, n + 1)
                    v.tensor_tensor(yn[:], xin[:], gs[:], ALU.mult).then_inc(s_yn, 1)
                    dve.wait_ge(s_o, n + 1)
                    then(v.tensor_tensor(z[:], B[4].rearrange("p (t c) -> p t c", t=GT), xt[b][:], ALU.add))
                    for t in range(GT):
                        i = own.mark(v.bn_stats(bst[:, t, :], z[:, t, :]))
                    dve.wait_ge(s_dve, i)
                    for t in range(GT):
                        i = v.bn_aggr(mv[:, t, :], bst[:, t, :])
                    i.then_inc(s_z, 1)
                    dve.wait_ge(s_lsd, n + 1)
                    then(v.reciprocal(rsv[:], sdv[:]))
                    dve.wait_ge(s_x[b], 16 * it + 16)
                    for t in range(GT):
                        i = v.tensor_scalar(xo[b][:, t, :], z[:, t, :], mv[:, t, 0:1], rsv[:, t:t + 1],
                                            ALU.subtract, ALU.mult)
                    i.then_inc(s_xo, 1)


NE, FC = 8, 4
RT = TOK // P


def expert_tiles(topk):
    most = TOK * topk // P + NE - 1
    return (most + 7) // 8 * 8


def moe_stage(nc, sem, tag, x_in, x_out, xs_rows, ys_rows, w, consts, topk, act_fn, gate_bias):
    where, ncon = constant_columns()
    NT = expert_tiles(topk)
    ctx = ExitStack()
    with ctx:
        def sb(name, shape, dt=F32):
            return ctx.enter_context(nc.sbuf_tensor(f"{tag}_{name}", shape, dt))

        k = {"C": {}, "sem": sem, "tag": tag, "NT": NT, "topk": topk}
        con = sb("con", [P, ncon])
        k["con"] = con
        k["C"] = {n: con[:, a:b] for n, (a, b) in where.items()}
        k["X"] = sb("X", [P, RT, P])
        k["w1"] = sb("w1", [P, NE, FC * P + FC])
        k["w2"] = sb("w2", [P, NE, FC, P])
        k["b2"] = sb("b2", [P, NE, P])
        k["top"] = sb("top", [P, RT, 8])
        k["slot"] = [sb(f"slot{i}", [P, RT], U32) for i in range(topk)]
        k["expert"] = sb("expert", [1, NT], I32)
        k["s_w"] = sem(f"{tag}_weights_in")
        moe_route(nc, k, x_in, xs_rows, w, consts, gate_bias)
        moe_experts(nc, k, xs_rows, ys_rows, act_fn)
        moe_combine(nc, k, ys_rows, x_out)


def moe_route(nc, k, x_in, xs_rows, w, consts, gate_bias):
    sem, tag, NT, topk, C, X, top, slot = (k[n] for n in ("sem", "tag", "NT", "topk", "C", "X", "top", "slot"))
    x_tiles = x_in.rearrange("(t p) c -> p t c", p=P)
    ctx = ExitStack()
    with ctx:
        def sb(name, shape, dt=F32):
            return ctx.enter_context(nc.sbuf_tensor(f"{tag}r_{name}", shape, dt))

        gw = sb("gw", [P, NE])
        gb = sb("gb", [P, NE])
        zero = sb("zero", [P, NT * P // 8])
        xT = [sb(f"xT{i}", [P, GTOK]) for i in range(2)]
        lg = sb("lg", [P, RT, NE])
        mx = sb("mx", [P, RT])
        pr = sb("pr", [P, RT, NE])
        idx = sb("idx", [P, RT, 8], U32)
        idf = sb("idf", [P, RT, 8])
        pick = [sb(f"pick{i}", [P, RT, NE]) for i in range(topk)]
        both = sb("both", [P, RT, NE])
        run = [sb(f"run{i}", [P, 16 + RT, NE]) for i in range(2)]
        over = sb("over", [P, NE, RT])
        base = [sb(f"base{i}", [P, 4 + NE]) for i in range(2)]
        place = sb("place", [P, RT, NE])
        mine = [sb(f"mine{i}", [P, RT, NE]) for i in range(topk)]
        pf = [sb(f"pf{i}", [P, RT]) for i in range(topk)]
        le = sb("le", [1, NT, NE - 1])
        ef = sb("ef", [1, NT])
        B = [ctx.enter_context(nc.psum_tensor(f"{tag}r_bank{i}", [P, GTOK], F32))[:, :] for i in range(4)]

        def s(name):
            return sem(f"{tag}_{name}")

        s_w, s_c, s_set = k["s_w"], s("constants_in"), s("constants_set")
        s_x = [s(f"rows_in_{i}") for i in range(4)]
        s_zero, s_T, s_xT, s_lg, s_sh, s_pr = s("zeros_out"), s("transposed"), s("channel_major"), s("logits"), s("logits_shifted"), s("exps")
        s_pick, s_cnt, s_slot, s_sc, s_dve = s("picks"), s("counts"), s("slots"), s("scattered"), s("vector_steps")
        block = ctx.enter_context(nc.Block())
        NC = 16 * (2 + gate_bias)

        @block.sync
        def _(sp):
            loads = [(k["con"][:], consts), (gw[:], w["gate_w"])]
            if gate_bias:
                loads.append((gb[:], w["gate_b"].broadcast_to([P, NE])))
            for q in range(4):
                sp.dma_start(X[:, 8 * q:8 * q + 8, :], x_tiles[:, 8 * q:8 * q + 8, :]).then_inc(s_x[q], 16)
                if q == 0:
                    for dst, src in loads:
                        sp.dma_start(dst, src).then_inc(s_c, 16)
            flat = xs_rows.rearrange("(p j) c -> p (j c)", p=P)
            sp.wait_ge(s_set, 3)
            for q in range(8):
                n = NT * P // 8
                sp.dma_start(flat[:, q * n:(q + 1) * n], zero[:]).then_inc(s_zero, 16)
            for e in range(NE):
                sp.dma_start(k["w1"][:, e, 0:FC * P], w["w1"][:, e].rearrange("p f c -> p (f c)")).then_inc(s_w, 16)
                sp.dma_start(k["w2"][:, e], w["w2"][:, e]).then_inc(s_w, 16)
            sp.dma_start(k["w1"][:, :, FC * P:], w["b1"]).then_inc(s_w, 16)
            sp.dma_start(k["b2"][:].rearrange("p e c -> p (e c)"),
                         w["b2"].rearrange("e c -> (e c)").unsqueeze(0).broadcast_to([P, NE * P])).then_inc(s_w, 16)

        @block.gpsimd
        def _(pool):
            nc.gpsimd.memset(zero[:], 0.0).then_inc(s_set, 1)
            for i in range(2):
                nc.gpsimd.memset(run[i][:, 0:16], 0.0).then_inc(s_set, 1)
            for i in range(2):
                nc.gpsimd.memset(base[i][:, 0:4], 0.0).then_inc(s_set, 1)
            pool.wait_ge(s_zero, 128)
            for i in range(topk):
                pool.wait_ge(s_slot, i + 1)
                for t in range(RT):
                    nc.gpsimd.indirect_dma_start(xs_rows, bass.IndirectOffsetOnAxis(ap=slot[i][:, t:t + 1], axis=0),
                                                 X[:, t, :], None).then_inc(s_sc, 16)
            pool.wait_ge(s_sc, 16 * topk * RT)

        @block.tensor
        def _(pe):
            mm = nc.tensor.matmul
            pe.wait_ge(s_c, NC)

            def logits(g):
                pe.wait_ge(s_xT, g + 1)
                for t in range(GT):
                    c = (g * GT + t) * NE
                    i = mm(B[2][:, c:c + NE], xT[g % 2][:, t * P:(t + 1) * P], gw[:], start=True, stop=True)
                return i

            for g in range(NG):
                if g % 2 == 0:
                    pe.wait_ge(s_x[g // 2], 16)
                for t in range(GT):
                    i = nc.tensor.transpose(B[g % 2][:, t * P:(t + 1) * P], X[:, g * GT + t, :], C["ident"])
                i.then_inc(s_T, 1)
                if g:
                    logits(g - 1).then_inc(s_lg, 1)
            logits(NG - 1).then_inc(s_lg, 1)
            pe.wait_ge(s_pick, 1)
            picks = both[:].rearrange("p t e -> p (t e)")
            mm(B[3][:, 0:RT * NE], C["before"], picks, start=True, stop=True)
            mm(B[3][:, RT * NE:], C["ones"], picks, start=True, stop=True).then_inc(s_cnt, 1)

        @block.scalar
        def _(act):
            op = nc.scalar.activation
            for g in range(NG):
                act.wait_ge(s_T, g + 1)
                if g >= 2:
                    act.wait_ge(s_lg, g - 1)
                op(xT[g % 2][:], B[g % 2], ACT.Copy).then_inc(s_xT, 1)
            act.wait_ge(s_sh, 1)
            op(pr[:], lg[:], ACT.Exp).then_inc(s_pr, 1)

        @block.vector
        def _(dve):
            v = nc.vector
            own = Steps(s_dve)

            def then(ins):
                dve.wait_ge(s_dve, own.mark(ins))

            per_tile = lambda a: a.unsqueeze(2).broadcast_to([P, RT, NE])
            dve.wait_ge(s_c, NC)
            dve.wait_ge(s_set, 5)
            dve.wait_ge(s_lg, NG)
            raw = B[2][:, 0:RT * NE].rearrange("p (t e) -> p t e", t=RT)
            if gate_bias:
                then(v.tensor_tensor(lg[:], raw, gb[:].unsqueeze(1).broadcast_to([P, RT, NE]), ALU.add))
            else:
                then(v.tensor_copy(lg[:], raw))
            then(v.tensor_reduce(mx[:], lg[:], AX_X, ALU.max))
            v.tensor_tensor(lg[:], lg[:], per_tile(mx[:]), ALU.subtract).then_inc(s_sh, 1)
            dve.wait_ge(s_pr, 1)
            then(v.tensor_reduce(mx[:], pr[:], AX_X, ALU.add))
            then(v.reciprocal(mx[:], mx[:]))
            then(v.tensor_tensor(pr[:], pr[:], per_tile(mx[:]), ALU.mult))
            for t in range(RT):
                i = own.mark(v.max(top[:, t, :], pr[:, t, :]))
            dve.wait_ge(s_dve, i)
            for t in range(RT):
                i = own.mark(v.max_index(idx[:, t, :], top[:, t, :], pr[:, t, :]))
            dve.wait_ge(s_dve, i)
            then(v.tensor_copy(idf[:], idx[:]))
            experts = C["experts"].unsqueeze(1).broadcast_to([P, RT, NE])
            for i in range(topk):
                ins = v.tensor_tensor(pick[i][:], experts, per_tile(idf[:, :, i]), ALU.is_equal)
                at = own.mark(ins)
            dve.wait_ge(s_dve, at)
            if topk == 2:
                v.tensor_tensor(both[:], pick[0][:], pick[1][:], ALU.add).then_inc(s_pick, 1)
            else:
                v.tensor_copy(both[:], pick[0][:]).then_inc(s_pick, 1)
            dve.wait_ge(s_cnt, 1)
            then(v.tensor_copy(run[0][:, 16:], B[3][:, RT * NE:].rearrange("p (t e) -> p t e", t=RT)))
            for q in range(5):
                a, b, d = run[q % 2], run[1 - q % 2], 1 << q
                then(v.tensor_tensor(b[:, 16:], a[:, 16:], a[:, 16 - d:16 + RT - d], ALU.add))
            sums = run[1]
            total = sums[:, 16 + RT - 1, :].unsqueeze(2).broadcast_to([P, NE, RT])
            then(v.tensor_tensor(over[:], total, C["limits"].unsqueeze(1).broadcast_to([P, NE, RT]), ALU.is_gt))
            then(v.tensor_reduce(base[0][:, 4:], over[:], AX_X, ALU.add))
            for q in range(3):
                a, b, d = base[q % 2], base[1 - q % 2], 1 << q
                then(v.tensor_tensor(b[:, 4:], a[:, 4:], a[:, 4 - d:4 + NE - d], ALU.add))
            starts = base[1][:, 3:3 + NE]
            then(v.scalar_tensor_tensor(place[:], starts.unsqueeze(1).broadcast_to([P, RT, NE]), float(P),
                                        sums[:, 15:15 + RT], ALU.mult, ALU.add))
            then(v.tensor_tensor(place[:], place[:], B[3][:, 0:RT * NE].rearrange("p (t e) -> p t e", t=RT), ALU.add))
            for i in range(topk):
                then(v.tensor_tensor(mine[i][:], pick[i][:], place[:], ALU.mult))
                then(v.tensor_reduce(pf[i][:], mine[i][:], AX_X, ALU.add))
                v.tensor_copy(slot[i][:], pf[i][:]).then_inc(s_slot, 1)
            then(v.tensor_tensor(le[:], base[1][0:1, 4:4 + NE - 1].unsqueeze(1).broadcast_to([1, NT, NE - 1]),
                                 C["tiles"][0:1, 0:NT].unsqueeze(2).broadcast_to([1, NT, NE - 1]), ALU.is_le))
            then(v.tensor_reduce(ef[:], le[:], AX_X, ALU.add))
            v.tensor_copy(k["expert"][:], ef[:]).then_inc(s_slot, 1)
            dve.wait_ge(s_slot, topk + 1)


def moe_experts(nc, k, xs_rows, ys_rows, act_fn):
    sem, tag, NT, C, w1, w2, b2, expert = (k[n] for n in ("sem", "tag", "NT", "C", "w1", "w2", "b2", "expert"))
    NI = NT // 8
    xs_tiles = xs_rows.rearrange("(g h t p) c -> g h p t c", h=2, t=GT, p=P)
    ys_tiles = ys_rows.rearrange("(g h t p) c -> g h p t c", h=2, t=GT, p=P)
    ctx = ExitStack()
    with ctx:
        def sb(name, shape, dt=F32):
            return ctx.enter_context(nc.sbuf_tensor(f"{tag}e_{name}", shape, dt))

        xs = [sb(f"xs{i}", [P, GT, P]) for i in range(2)]
        ys = [sb(f"ys{i}", [P, GT, P]) for i in range(2)]
        xT = [sb(f"xT{i}", [P, P]) for i in range(2)]
        cur = [sb(f"cur{i}", [P, FC * P + FC]) for i in range(2)]
        h = [sb(f"h{i}", [P, FC, P]) for i in range(2)]
        BT, BU, BY = [[ctx.enter_context(nc.psum_tensor(f"{tag}e_{n}{i}", [P, GTOK], F32))[:, :] for i in range(2)]
                      for n in ("turned", "up", "down")]

        def s(name):
            return sem(f"{tag}_{name}")

        s_in, s_st = [s("sorted_in_0"), s("sorted_in_1")], [s("results_out_0"), s("results_out_1")]
        s_T, s_xT, s_cur, s_up, s_h, s_dn, s_y = s("tile_transposed"), s("tile_channel_major"), s("tile_weights"), s("up"), s("hidden"), s("down"), s("results")
        s_w = k["s_w"]
        NW = 16 * (2 * NE + 2)
        block = ctx.enter_context(nc.Block())

        def after(eng, semaphore, count):
            if not isinstance(count, int) or count > 0:
                eng.wait_ge(semaphore, count)

        def rounds(eng, body):
            body(0, False)
            with eng.Fori(1, NI - 1) as g:
                body(g, False)
            body(NI - 1, True)

        @block.sync
        def _(sp):
            one = lambda rows, g, b: rows[bass.ds(g, 1), b].rearrange("g p t c -> (g p) t c")

            def body(g, last):
                for b in range(2):
                    done = g * 8 + 4 * b + 4
                    if not last:
                        sp.wait_ge(s_T, done)
                        sp.dma_start(xs[b][:], one(xs_tiles, g + 1, b)).then_inc(s_in[b], 16)
                    sp.wait_ge(s_y, done)
                    sp.dma_start(one(ys_tiles, g, b), ys[b][:]).then_inc(s_st[b], 16)

            for b in range(2):
                sp.dma_start(xs[b][:], one(xs_tiles, 0, b)).then_inc(s_in[b], 16)
            rounds(sp, body)
            for b in range(2):
                sp.wait_ge(s_st[b], 16 * NI)

        @block.tensor
        def _(pe):
            mm = nc.tensor.matmul

            def turn(g, u):
                if u % 4 == 0:
                    pe.wait_ge(s_in[u // 4], g * 16 + 16)
                nc.tensor.transpose(BT[u % 2][:, 0:P], xs[u // 4][:, u % 4, :], C["ident"]).then_inc(s_T, 1)

            def down(j, u, e):
                pe.wait_ge(s_h, j + 1)
                after(pe, s_y, j - 1)
                for f in range(FC):
                    i = mm(BY[u % 2][:, 0:P], h[u % 2][:, f, :], w2[:, bass.ds(e, 1), f, :].rearrange("p e c -> p (e c)"),
                           start=(f == 0), stop=(f == FC - 1))
                i.then_inc(s_dn, 1)

            pe.wait_ge(s_w, NW)
            turn(0, 0)

            def body(g, last):
                for u in range(8):
                    j = g * 8 + u
                    if u < 7:
                        turn(g, u + 1)
                    elif not last:
                        turn(g + 1, 0)
                    pe.wait_ge(s_cur, j + 1)
                    pe.wait_ge(s_xT, j + 1)
                    after(pe, s_h, j - 1)
                    for f in range(FC):
                        i = mm(BU[u % 2][:, f * P:(f + 1) * P], cur[u % 2][:, f * P:(f + 1) * P], xT[u % 2][:],
                               start=True, stop=True)
                    i.then_inc(s_up, 1)
                    if u or not isinstance(j, int) or j:
                        e = pe.value_load(expert[0:1, bass.ds(j - 1, 1)], min_val=0, max_val=NE - 1)
                        down(j - 1, (u - 1) % 8, e)

            rounds(pe, body)
            e = pe.value_load(expert[0:1, NT - 1:NT], min_val=0, max_val=NE - 1)
            down(NT - 1, 7, e)

        @block.scalar
        def _(act):
            op = nc.scalar.activation

            def body(g, last):
                for u in range(8):
                    j = g * 8 + u
                    act.wait_ge(s_up, j + 1)
                    after(act, s_dn, j - 1)
                    for f in range(FC):
                        i = op(h[u % 2][:, f, :], BU[u % 2][:, f * P:(f + 1) * P], act_fn,
                               bias=cur[u % 2][:, FC * P + f:FC * P + f + 1])
                    i.then_inc(s_h, 1)

            rounds(act, body)

        @block.vector
        def _(dve):
            v = nc.vector

            def fetch(j, u):
                e = dve.value_load(expert[0:1, bass.ds(j, 1)], min_val=0, max_val=NE - 1)
                after(dve, s_h, j - 1)
                v.tensor_scalar(cur[u % 2][:], w1[:, bass.ds(e, 1), :].rearrange("p e c -> p (e c)"),
                                1.0, None, ALU.mult).then_inc(s_cur, 1)

            def copy_x(j, u):
                dve.wait_ge(s_T, j + 1)
                v.tensor_copy(xT[u % 2][:], BT[u % 2][:, 0:P]).then_inc(s_xT, 1)

            def result(j, u, g):
                e = dve.value_load(expert[0:1, bass.ds(j, 1)], min_val=0, max_val=NE - 1)
                dve.wait_ge(s_dn, j + 1)
                if u % 4 == 0:
                    after(dve, s_st[u // 4], g * 16)
                v.tensor_tensor(ys[u // 4][:, u % 4, :], BY[u % 2][:, 0:P],
                                b2[:, bass.ds(e, 1), :].rearrange("p e c -> p (e c)"), ALU.add).then_inc(s_y, 1)

            dve.wait_ge(s_w, NW)
            fetch(0, 0)
            copy_x(0, 0)

            def body(g, last):
                for u in range(8):
                    j = g * 8 + u
                    if u < 7 or not last:
                        fetch(j + 1, (u + 1) % 8)
                        copy_x(j + 1, (u + 1) % 8)
                    if u:
                        result(j - 1, u - 1, g)
                    elif not isinstance(g, int) or g:
                        result(j - 1, 7, g - 1)

            rounds(dve, body)
            result(NT - 1, 7, NI - 1)


def moe_combine(nc, k, ys_rows, x_out):
    sem, tag, topk, X, top, slot = (k[n] for n in ("sem", "tag", "topk", "X", "top", "slot"))
    o_tiles = x_out.rearrange("(g t p) c -> g p t c", t=GT, p=P)
    ctx = ExitStack()
    with ctx:
        def sb(name, shape, dt=F32):
            return ctx.enter_context(nc.sbuf_tensor(f"{tag}c_{name}", shape, dt))

        eps = sb("eps", [P, 1])
        y = [sb(f"y{i}", [P, RT, P]) for i in range(topk)]
        bst = sb("bst", [P, RT, 6])
        mv = sb("mv", [P, RT, 2])
        sdv = sb("sdv", [P, RT])
        rsv = sb("rsv", [P, RT])

        def s(name):
            return sem(f"{tag}_{name}")

        s_set, s_y = s("eps_set"), [s(f"results_in_{g}") for g in range(NG)]
        s_z, s_sd, s_o, s_out, s_dve = s("sum_stats"), s("sum_deviation"), s("rows_ready"), s("rows_out"), s("combine_steps")
        block = ctx.enter_context(nc.Block())

        @block.gpsimd
        def _(pool):
            nc.gpsimd.memset(eps[:], LN_EPS).then_inc(s_set, 1)
            for g in range(NG):
                for t in range(g * GT, g * GT + GT):
                    for i in range(topk):
                        nc.gpsimd.indirect_dma_start(y[i][:, t, :], None, ys_rows,
                                                     bass.IndirectOffsetOnAxis(ap=slot[i][:, t:t + 1], axis=0)
                                                     ).then_inc(s_y[g], 16)

        @block.vector
        def _(dve):
            v = nc.vector
            own = Steps(s_dve)

            def finish(g):
                dve.wait_ge(s_sd, g + 1)
                r = slice(g * GT, g * GT + GT)
                dve.wait_ge(s_dve, own.mark(v.reciprocal(rsv[:, r], sdv[:, r])))
                for t in range(g * GT, g * GT + GT):
                    i = v.tensor_scalar(X[:, t, :], X[:, t, :], mv[:, t, 0:1], rsv[:, t:t + 1], ALU.subtract, ALU.mult)
                i.then_inc(s_o, 1)

            for g in range(NG):
                tiles = range(g * GT, g * GT + GT)
                dve.wait_ge(s_y[g], 16 * GT * topk)
                for i in range(topk):
                    for t in tiles:
                        at = own.mark(v.scalar_tensor_tensor(X[:, t, :], y[i][:, t, :], top[:, t, i:i + 1], X[:, t, :],
                                                             ALU.mult, ALU.add))
                    dve.wait_ge(s_dve, at)
                for t in tiles:
                    at = own.mark(v.bn_stats(bst[:, t, :], X[:, t, :]))
                dve.wait_ge(s_dve, at)
                for t in tiles:
                    i = v.bn_aggr(mv[:, t, :], bst[:, t, :])
                i.then_inc(s_z, 1)
                if g:
                    finish(g - 1)
            finish(NG - 1)

        @block.scalar
        def _(act):
            act.wait_ge(s_set, 1)
            for g in range(NG):
                r = slice(g * GT, g * GT + GT)
                act.wait_ge(s_z, g + 1)
                nc.scalar.activation(sdv[:, r], mv[:, r, 1], ACT.Sqrt, bias=eps[:, 0:1]).then_inc(s_sd, 1)

        @block.sync
        def _(sp):
            for g in range(NG):
                sp.wait_ge(s_o, g + 1)
                sp.dma_start(o_tiles[g], X[:, g * GT:g * GT + GT, :]).then_inc(s_out, 16)
            sp.wait_ge(s_out, 16 * NG)


NCH = SEQ // 32


def delta_project(nc, sem, keep, x_in, v_rows, s_rows, w, consts):
    where, ncon = constant_columns()
    x_tiles = x_in.rearrange("(g t p) c -> g p t c", t=GT, p=P)
    v_tiles = v_rows.rearrange("(g t p) c -> g p t c", t=GT, p=P)
    s_tiles = s_rows.rearrange("(g t p) c -> g p t c", t=GT, p=P)
    ctx = ExitStack()
    with ctx:
        def sb(name, shape, dt=F32):
            return ctx.enter_context(nc.sbuf_tensor("c_" + name, shape, dt))

        con = sb("con", [P, ncon])
        C = {k: con[:, a:b] for k, (a, b) in where.items()}
        wqkv = sb("wqkv", [P, 3, P])
        wb = sb("wb", [P, P])
        taps = sb("taps", [P, 3, 4])
        fir = sb("fir", [P, 3])
        eps = sb("eps", [P, 1])
        xt = [sb(f"xt{i}", [P, GT, P]) for i in range(2)]
        xT = sb("xT", [P, GTOK])
        pad = [sb(f"pad{i}", [P, GSEQ, SEQ + 3]) for i in range(3)]
        cv = [[sb(f"cv{i}{j}", [P, GTOK]) for j in range(2)] for i in range(3)]
        qk = [sb(f"qk{i}", [P, GTOK]) for i in range(2)]
        vs = sb("vs", [P, GSEQ, SEQ + 2])
        beta = sb("beta", [P, GTOK])
        sq = [sb(f"sq{i}", [P, GTOK]) for i in range(2)]
        sd = [sb(f"sd{i}", [P, GTOK]) for i in range(2)]
        kn = sb("kn", [P, GTOK])
        kq = sb("kq", [P, GTOK // 32, 2, 32])
        vb = sb("vb", [P, GTOK])
        kbs = sb("kbs", [P, GTOK])
        hs = [sb(f"hs{i}", [P, GTOK]) for i in range(3)]
        fa = [sb(f"fa{i}", [P, GTOK]) for i in range(2)]
        vt = sb("vt", [P, GT, P])
        ft = sb("ft", [P, GT, P])
        B = [ctx.enter_context(nc.psum_tensor(f"c_bank{i}", [P, GTOK], F32))[:, :] for i in range(8)]

        def s(name):
            return sem("delta_" + name)

        s_w, s_set, s_x, s_out = s("weights_in"), s("constants_set"), [s("rows_in_0"), s("rows_in_1")], s("rows_out")
        s_T, s_xT, s_p, s_pad, s_beta = s("transposed"), s("channel_major"), s("projected"), s("padded"), s("beta")
        s_cv, s_act, s_sq, s_ss, s_sd = s("convolved"), s("silu"), s("squared"), s("square_sums"), s("norms")
        s_n, s_kq, s_hs, s_keep = s("normalized"), s("score_operands"), s("head_rows"), s("kept")
        s_sc, s_m, s_fir, s_tp, s_rows = s("scores"), s("scores_masked"), s("short_fir"), s("value_rows"), s("value_rows_copied")
        s_ln, s_dve = s("logarithms"), s("vector_steps")

        block = ctx.enter_context(nc.Block())
        one = lambda rows, n: rows[bass.ds(n, 1)].rearrange("g p t c -> (g p) t c")

        def steps(eng, step):
            step(0, 0, 0, True, False)
            with eng.Fori(0, NG // 2 - 1) as it:
                step(it * 2 + 1, 1, it + 1, False, False)
                step(it * 2 + 2, 0, it + 1, False, False)
            step(NG - 1, 1, NG // 2, False, True)

        @block.sync
        def _(sp):
            for b in range(2):
                sp.dma_start(xt[b][:], one(x_tiles, b)).then_inc(s_x[b], 16)
            for dst, src in [(con[:], consts), (wqkv[:], w["wqkv"]), (wb[:], w["wb"]), (taps[:], w["taps"]),
                             (fir[:], w["firs"])]:
                sp.dma_start(dst, src).then_inc(s_w, 16)

            def group(n, b, more):
                if more:
                    sp.wait_ge(s_T, n + 1)
                    sp.dma_start(xt[b][:], one(x_tiles, n + 2)).then_inc(s_x[b], 16)
                sp.wait_ge(s_rows, 2 * n + 2)
                sp.dma_start(one(v_tiles, n), vt[:]).then_inc(s_out, 16)
                sp.dma_start(one(s_tiles, n), ft[:]).then_inc(s_out, 16)

            with sp.Fori(0, NG // 2 - 1) as it:
                for b in range(2):
                    group(it * 2 + b, b, True)
            group(NG - 2, 0, False)
            group(NG - 1, 1, False)
            sp.wait_ge(s_out, 32 * NG)

        @block.tensor
        def _(pe):
            mm = nc.tensor.matmul
            pe.wait_ge(s_w, 80)

            def project(m, b, r, first=False):
                pe.wait_ge(s_x[b], 16 * r + 16)
                for t in range(GT):
                    i = nc.tensor.transpose(B[0][:, t * P:(t + 1) * P], xt[b][:, t, :], C["ident"])
                i.then_inc(s_T, 1)
                pe.wait_ge(s_xT, m + 1)
                if not first:
                    pe.wait_ge(s_beta, m)
                for k in range(3):
                    mm(B[1 + k], wqkv[:, k, :], xT[:], start=True, stop=True).then_inc(s_p, 1)
                mm(B[4], wb[:], xT[:], start=True, stop=True).then_inc(s_p, 1)

            def step(n, b, r, first, last):
                if not first:
                    pe.wait_ge(s_m, 2 * n)
                for k in range(2):
                    pe.wait_ge(s_sq, 2 * n + k + 1)
                    mm(B[5 + k], C["same32"], sq[k][:], start=True, stop=True).then_inc(s_ss, 1)
                if not first:
                    pe.wait_ge(s_rows, 2 * n)
                for t in range(GT):
                    o = (t % 2) * P + 2
                    i = nc.tensor.transpose(B[7][:, t * P:(t + 1) * P], vs[:, t // 2, o:o + P], C["ident"])
                i.then_inc(s_tp, 1)
                if not last:
                    project(n + 1, 1 - b, r)
                pe.wait_ge(s_w, 80)
                pe.wait_ge(s_kq, n + 1)
                for c in range(GTOK // 32):
                    for h in range(4):
                        rows = slice(32 * h, 32 * h + 32)
                        i = mm(B[5 + c // NCH][rows, (c % NCH) * 64:(c % NCH) * 64 + 64], kn[rows, 32 * c:32 * c + 32],
                               kq[rows, c].rearrange("p k c -> p (k c)"), start=True, stop=True,
                               skip_group_check=True)
                    if c % NCH == NCH - 1:
                        i.then_inc(s_sc, 1)
                pe.wait_ge(s_fir, n + 1)
                pe.wait_ge(s_rows, 2 * n + 1)
                for t in range(GT):
                    i = nc.tensor.transpose(B[7][:, t * P:(t + 1) * P], fa[0][:, t * P:(t + 1) * P], C["ident"])
                i.then_inc(s_tp, 1)

            project(0, 0, 0, first=True)
            steps(pe, step)

        @block.gpsimd
        def _(pool):
            nc.gpsimd.memset(eps[:], 1e-6).then_inc(s_set, 1)
            for k in range(3):
                nc.gpsimd.memset(pad[k][:, :, 0:3], 0.0).then_inc(s_set, 1)
            nc.gpsimd.memset(vs[:, :, 0:2], 0.0).then_inc(s_set, 1)
            with pool.Fori(0, NG) as n:
                seqs = bass.ds(n * GSEQ, GSEQ)
                view = lambda a: a.rearrange("p (s n c) -> p s n c", s=GSEQ, c=32)
                place = lambda a: a[:, :, seqs, :].rearrange("p n s c -> p s n c")
                pool.wait_ge(s_kq, n + 1)
                nc.gpsimd.tensor_copy(place(keep["q"]), kq[:, :, 1, :].rearrange("p (s n) c -> p s n c", s=GSEQ)
                                      ).then_inc(s_keep, 1)
                for k, name in enumerate(("k", "kb", "vb")):
                    pool.wait_ge(s_hs, 3 * n + k + 1)
                    nc.gpsimd.tensor_copy(place(keep[name]), view(hs[k][:])).then_inc(s_keep, 1)

        @block.scalar
        def _(act):
            op = nc.scalar.activation
            seqs = lambda a: a.rearrange("p (s t) -> p s t", s=GSEQ)
            act.wait_ge(s_w, 80)
            act.wait_ge(s_set, 5)

            def copy_x(m):
                act.wait_ge(s_T, m + 1)
                op(xT[:], B[0], ACT.Copy).then_inc(s_xT, 1)

            def copy_projected(m):
                for k in range(3):
                    act.wait_ge(s_p, 4 * m + k + 1)
                    op(pad[k][:, :, 3:SEQ + 3], seqs(B[1 + k]), ACT.Copy).then_inc(s_pad, 1)

            def step_sizes(m):
                act.wait_ge(s_p, 4 * m + 4)
                op(beta[:], B[4], ACT.Sigmoid).then_inc(s_beta, 1)

            def step(n, b, r, first, last):
                for k in range(3):
                    act.wait_ge(s_cv, 3 * n + k + 1)
                    op(seqs(qk[k][:]) if k < 2 else vs[:, :, 2:SEQ + 2], seqs(cv[k][1][:]), ACT.Silu).then_inc(s_act, 1)
                for k in range(2):
                    act.wait_ge(s_act, 3 * n + k + 1)
                    op(sq[k][:], qk[k][:], ACT.Square).then_inc(s_sq, 1)
                for k in range(2):
                    act.wait_ge(s_ss, 2 * n + k + 1)
                    op(sq[k][:], B[5 + k], ACT.Ln, bias=eps[:, 0:1]).then_inc(s_ln, 1)
                for k in range(2):
                    act.wait_ge(s_ln, 2 * n + k + 1)
                    op(sd[k][:], sq[k][:], ACT.Exp, scale=-0.5).then_inc(s_sd, 1)
                if not last:
                    copy_x(n + 1)
                if not first:
                    act.wait_ge(s_out, 32 * n)
                act.wait_ge(s_tp, 2 * n + 1)
                op(vt[:].rearrange("p t c -> p (t c)"), B[7], ACT.Copy).then_inc(s_rows, 1)
                if not last:
                    copy_projected(n + 1)
                    act.wait_ge(s_kq, n + 1)
                    step_sizes(n + 1)
                act.wait_ge(s_tp, 2 * n + 2)
                op(ft[:].rearrange("p t c -> p (t c)"), B[7], ACT.Copy).then_inc(s_rows, 1)

            copy_x(0)
            copy_projected(0)
            step_sizes(0)
            steps(act, step)

        @block.vector
        def _(dve):
            v = nc.vector
            own = Steps(s_dve)
            seqs = lambda a: a.rearrange("p (s t) -> p s t", s=GSEQ)
            chunks = lambda a: a.rearrange("p (c j) -> p c j", j=32)
            dve.wait_ge(s_w, 80)
            dve.wait_ge(s_set, 5)

            def then(ins):
                dve.wait_ge(s_dve, own.mark(ins))

            def masks(n):
                for q in range(GSEQ):
                    dve.wait_ge(s_sc, 2 * n + q + 1)
                    sc = B[5 + q].rearrange("p (n k c) -> p n k c", n=NCH, k=2)
                    for k, (mask, dst) in enumerate((("strict", "A"), ("incl", "attn"))):
                        out = keep[dst][:, :, bass.ds(n * GSEQ + q, 1), :].rearrange("p n s c -> p n (s c)")
                        i = v.tensor_tensor(out, sc[:, :, k, :], C[mask].unsqueeze(1).broadcast_to([P, NCH, 32]), ALU.mult)
                    i.then_inc(s_m, 1)

            def step(n, b, r, first, last):
                own.restart(dve)
                tap = [0, 0, 0]
                for k in range(3):
                    dve.wait_ge(s_pad, 3 * n + k + 1)
                    tap[k] = own.mark(v.tensor_scalar(seqs(cv[k][0][:]), pad[k][:, :, 0:SEQ], taps[:, k, 0:1], None, ALU.mult))
                for j in range(1, 4):
                    for k in range(3):
                        dve.wait_ge(s_dve, tap[k])
                        ins = v.scalar_tensor_tensor(seqs(cv[k][j % 2][:]), pad[k][:, :, j:SEQ + j], taps[:, k, j:j + 1],
                                                     seqs(cv[k][1 - j % 2][:]), ALU.mult, ALU.add)
                        if j < 3:
                            tap[k] = own.mark(ins)
                        else:
                            ins.then_inc(s_cv, 1)
                if not first:
                    masks(n - 1)
                dve.wait_ge(s_act, 3 * n + 3)
                if not first:
                    dve.wait_ge(s_tp, 2 * n)
                then(v.tensor_scalar(seqs(fa[0][:]), vs[:, :, 0:SEQ], fir[:, 0:1], None, ALU.mult))
                then(v.scalar_tensor_tensor(seqs(fa[1][:]), vs[:, :, 1:SEQ + 1], fir[:, 1:2], seqs(fa[0][:]), ALU.mult, ALU.add))
                v.scalar_tensor_tensor(seqs(fa[0][:]), vs[:, :, 2:SEQ + 2], fir[:, 2:3], seqs(fa[1][:]),
                                       ALU.mult, ALU.add).then_inc(s_fir, 1)
                dve.wait_ge(s_beta, n + 1)
                if not first:
                    dve.wait_ge(s_keep, 4 * n)
                i = own.mark(v.tensor_tensor(seqs(vb[:]), vs[:, :, 2:SEQ + 2], seqs(beta[:]), ALU.mult))
                dve.wait_ge(s_sd, 2 * n + 2)
                own_kn = own.mark(v.tensor_tensor(kn[:], qk[1][:], sd[1][:], ALU.mult))
                v.tensor_tensor(kq[:, :, 1, :], chunks(qk[0][:]), chunks(sd[0][:]), ALU.mult)
                dve.wait_ge(s_dve, own_kn)
                own_kb = own.mark(v.tensor_tensor(kbs[:], kn[:], beta[:], ALU.mult))
                v.tensor_tensor(kq[:, :, 0, :], chunks(kn[:]), chunks(beta[:]), ALU.mult).then_inc(s_kq, 1)
                dve.wait_ge(s_dve, own_kb)
                v.transpose(hs[0][:], kn[:]).then_inc(s_hs, 1)
                v.transpose(hs[1][:], kbs[:]).then_inc(s_hs, 1)
                v.transpose(hs[2][:], vb[:]).then_inc(s_hs, 1)

            steps(dve, step)
            masks(NG - 1)
            dve.wait_ge(s_keep, 4 * NG)


def delta_invert(nc, sem, keep, long_fir, v_rows, w, consts):
    where, ncon = constant_columns()
    NT, GC = TOK // P, 16
    v_tiles = v_rows.rearrange("(s two p) c -> two p s c", two=2, p=P)
    rev = w["firl"]
    span = rev.shape[1]
    ctx = ExitStack()
    with ctx:
        def sb(name, shape, dt=F32):
            return ctx.enter_context(nc.sbuf_tensor("i_" + name, shape, dt))

        con = sb("con", [P, ncon])
        C = {k: con[:, a:b] for k, (a, b) in where.items()}
        M = sb("M", [P, 32, 4, 32])
        tmp = [sb(f"tmp{i}", [P, 4096 // 8]) for i in range(2)]
        vtok = sb("vtok", [P, NT, P])
        toe = [sb(f"toe{i}", [P, GC, 192]) for i in range(2)]
        turned = [sb(f"turned{i}", [P, 512]) for i in range(2)]
        R = [ctx.enter_context(nc.psum_tensor(f"i_fir{i}", [P, 512], F32))[:, :] for i in range(4)]
        Q = [ctx.enter_context(nc.psum_tensor(f"i_bank{i}", [P, 512], F32))[:, :] for i in range(4)]

        def s(name):
            return sem("invert_" + name)

        s_flip, s_rev = s("flipped"), s("flipped_copied")
        s_w, s_v, s_toe = s("constants_in"), s("values_in"), [s("toeplitz_in_0"), s("toeplitz_in_1")]
        s_fir, s_fc, s_ft, s_long = s("fir"), s("fir_copied"), s("fir_transposed"), s("fir_rows")
        s_at, s_M, s_done, s_ut, s_U, s_dve = s("chunks_transposed"), s("chunk_rows"), s("inverted"), s("back_transposed"), s("kept"), s("vector_steps")
        block = ctx.enter_context(nc.Block())

        @block.sync
        def _(sp):
            sp.dma_start(con[:], consts).then_inc(s_w, 16)
            for half in range(2):
                sp.dma_start(vtok[:, 16 * half:16 * half + 16], v_tiles[1 - half]).then_inc(s_v, 16)
            for r in range(P // GC):
                if r >= 2:
                    sp.wait_ge(s_fir, r - 1)
                src = bass.AP(rev.tensor, rev.offset + r * GC * span, [[1, P], [span, GC], [1, 192]])
                sp.dma_start(toe[r % 2][:], src).then_inc(s_toe[r % 2], 16)

        @block.tensor
        def _(pe):
            mm = nc.tensor.matmul
            pe.wait_ge(s_w, 16)
            A = keep["A"][:].rearrange("p n s c -> p (n s) c")
            for c in range(32):
                k = c // 4
                if c % 4 == 0 and k >= 4:
                    pe.wait_ge(s_M, k - 3)
                i = nc.tensor.transpose(Q[k % 4][:, (c % 4) * P:(c % 4 + 1) * P], A[:, :, c], C["ident"])
                if c % 4 == 3:
                    i.then_inc(s_at, 1)
            pe.wait_ge(s_v, 32)
            for k in range(8):
                if k >= 4:
                    pe.wait_ge(s_rev, k - 3)
                mm(R[k % 4], C["flip"], vtok[:, 4 * k:4 * k + 4, :].rearrange("p t c -> p (t c)"),
                   start=True, stop=True).then_inc(s_flip, 1)
            pe.wait_ge(s_rev, 8)
            def turn(r):
                pe.wait_ge(s_fc, r + 1)
                if r >= 2:
                    pe.wait_ge(s_long, r - 1)
                for j in range(4):
                    i = nc.tensor.transpose(R[2 + r % 2][:, j * P:(j + 1) * P], turned[r % 2][:, j * P:(j + 1) * P],
                                            C["ident"])
                i.then_inc(s_ft, 1)

            for r in range(P // GC):
                pe.wait_ge(s_toe[r % 2], 16 * (r // 2) + 16)
                if r >= 2:
                    pe.wait_ge(s_fc, r - 1)
                for j in range(GC):
                    ch, rows, at = r * GC + j, 32 * (j % 4), (j // 4) * P
                    mm(R[r % 2][rows:rows + 32, at:at + P], vtok[:, :, ch], toe[r % 2][:, j, 0:P],
                       start=True, stop=False, skip_group_check=True)
                    i = mm(R[r % 2][rows:rows + 16, at:at + 64], vtok[0:64, 16:32, ch], toe[r % 2][0:64, j, P:192],
                           start=False, stop=True, skip_group_check=True)
                i.then_inc(s_fir, 1)
                if r:
                    turn(r - 1)
            turn(P // GC - 1)
            pe.wait_ge(s_done, 1)
            for c in range(32):
                k = c // 4
                pe.wait_ge(s_M, 8)
                if c % 4 == 0 and k >= 4:
                    pe.wait_ge(s_U, k - 3)
                i = nc.tensor.transpose(Q[k % 4][:, (c % 4) * P:(c % 4 + 1) * P],
                                        M[:, c].rearrange("p h j -> p (h j)"), C["ident"])
                if c % 4 == 3:
                    i.then_inc(s_ut, 1)

        @block.scalar
        def _(act):
            op = nc.scalar.activation
            for k in range(8):
                act.wait_ge(s_at, k + 1)
                op(M[:, 4 * k:4 * k + 4].rearrange("p c h j -> p (c h j)"), Q[k % 4], ACT.Copy).then_inc(s_M, 1)
            for k in range(8):
                act.wait_ge(s_flip, k + 1)
                op(vtok[:, 4 * k:4 * k + 4, :].rearrange("p t c -> p (t c)"), R[k % 4], ACT.Copy).then_inc(s_rev, 1)

            def rows(r):
                act.wait_ge(s_ft, r + 1)
                for half in range(2):
                    out = long_fir[:, :, GC * r:GC * r + GC].rearrange("p (s two) c -> p two c s", two=2)[:, 1 - half]
                    i = op(out, R[2 + r % 2].rearrange("p (c h s) -> p h c s", h=2, s=16)[:, half], ACT.Copy)
                i.then_inc(s_long, 1)

            for r in range(P // GC):
                act.wait_ge(s_fir, r + 1)
                if r >= 2:
                    act.wait_ge(s_ft, r - 1)
                op(turned[r % 2][:], R[r % 2], ACT.Copy).then_inc(s_fc, 1)
                if r:
                    rows(r - 1)
            rows(P // GC - 1)
            U = keep["A"][:].rearrange("p n s c -> p c (n s)")
            for k in range(8):
                act.wait_ge(s_ut, k + 1)
                op(U[:, 4 * k:4 * k + 4, :], Q[k % 4].rearrange("p (c m) -> p c m", c=4), ACT.Copy).then_inc(s_U, 1)

        @block.vector
        def _(dve):
            v = nc.vector
            dve.wait_ge(s_M, 8)
            done = [0, 0]
            own = Steps(s_dve)
            for j in range(1, 31):
                rows = 31 - j
                for pair in range(2):
                    hh = slice(2 * pair, 2 * pair + 2)
                    t = tmp[pair][:, 0:rows * 2 * j].rearrange("p (i h c) -> p i h c", h=2, c=j)
                    if done[pair]:
                        dve.wait_ge(s_dve, done[pair])
                    done[pair] = own.mark(v.tensor_tensor(t, M[:, j + 1:32, hh, j:j + 1].broadcast_to([P, rows, 2, j]),
                                                 M[:, j:j + 1, hh, 0:j].broadcast_to([P, rows, 2, j]), ALU.mult))
                for pair in range(2):
                    hh = slice(2 * pair, 2 * pair + 2)
                    out = M[:, j + 1:32, hh, 0:j]
                    t = tmp[pair][:, 0:rows * 2 * j].rearrange("p (i h c) -> p i h c", h=2, c=j)
                    dve.wait_ge(s_dve, done[pair])
                    done[pair] = own.mark(v.tensor_tensor(out, out, t, ALU.add))
            dve.wait_ge(s_dve, done[1])
            flat = M[:].rearrange("p i h c -> p (i h c)")
            for h in range(4):
                i = v.memset(flat[:, h * 32:h * 32 + 31 * 129 + 1:129], 1.0)
            i.then_inc(s_done, 1)


def delta_recur(nc, sem, keep, oT):
    ctx = ExitStack()
    with ctx:
        def sb(name, shape, dt=F32):
            return ctx.enter_context(nc.sbuf_tensor("r_" + name, shape, dt))

        names = ("A", "kb", "vb", "k", "q", "attn")
        step = [{k: sb(f"{k}{i}", [P, NSEQ, 32]) for k in names} for i in range(2)]
        wn = sb("wn", [P, NSEQ, 32])
        ua = sb("ua", [P, NSEQ, 32])
        S = sb("S", [P, NSEQ, 32])
        Bank = [ctx.enter_context(nc.psum_tensor(f"r_bank{i}", [P, NSEQ, 32], F32)) for i in range(6)]
        Bu, Bw, Bo, Bs = Bank[0:2], Bank[2], Bank[3:5], Bank[5]

        def s(name):
            return sem("recur_" + name)

        s_in, s_set, s_w, s_wn, s_u, s_ua = [s("chunks_in_0"), s("chunks_in_1")], s("state_zero"), s("w"), s("w_copied"), s("u"), s("u_copied")
        s_S, s_Sc, s_o, s_oc = s("state"), s("state_copied"), s("o"), s("o_copied")
        block = ctx.enter_context(nc.Block())

        @block.sync
        def _(sp):
            def load(n, b):
                for k in names:
                    sp.dma_start(step[b][k][:], keep[k][:, n]).then_inc(s_in[b], 16)

            load(0, 0)
            load(1, 1)
            for n in range(2, NCH):
                sp.wait_ge(s_o, n - 1)
                load(n, n % 2)

        @block.tensor
        def _(pe):
            mm = nc.tensor.matmul

            def heads(out, lhsT, rhs, first, last, fresh=False):
                for q in range(NSEQ):
                    for h in range(4):
                        r = slice(32 * h, 32 * h + 32)
                        i = mm(out[r, q, :], lhsT[r, q, :], rhs[r, q, :], start=fresh and q == 0, stop=last,
                               skip_group_check=True)
                return i

            pe.wait_ge(s_set, 2)
            count, loaded = pe.alloc_register("steps"), pe.alloc_register("loads")
            pe.reg_mov(count, 0)
            pe.reg_mov(loaded, 0)
            with pe.Fori(0, NCH // 2) as it:
                for b in range(2):
                    pe.reg_add(count, count, 1)
                    if b == 0:
                        pe.reg_add(loaded, loaded, 96)
                    c = step[b]
                    pe.wait_ge(s_set, 2)
                    pe.wait_ge(s_in[b], loaded)
                    heads(Bw, c["kb"], c["A"], True, True, fresh=True).then_inc(s_w, 1)
                    heads(Bu[b], c["A"], c["vb"], True, False, fresh=True)
                    pe.wait_ge(s_set, 2)
                    pe.wait_ge(s_wn, count)
                    pe.wait_ge(s_Sc, count)
                    heads(Bu[b], wn, S, False, True).then_inc(s_u, 1)
                    heads(Bo[b], S, c["q"], True, False, fresh=True)
                    pe.wait_ge(s_set, 2)
                    pe.wait_ge(s_ua, count)
                    heads(Bs, c["k"], ua, True, True).then_inc(s_S, 1)
                    heads(Bo[b], ua, c["attn"], False, True).then_inc(s_o, 1)

        @block.scalar
        def _(act):
            op = nc.scalar.activation
            with act.Fori(0, NCH // 2) as it:
                for b in range(2):
                    n = it * 2 + b
                    act.wait_ge(s_w, n + 1)
                    op(wn[:], Bw[:], ACT.Copy, scale=-1.0).then_inc(s_wn, 1)
                    act.wait_ge(s_o, n + 1)
                    op(oT[:, bass.ds(n, 1)].rearrange("p n s c -> p (n s) c"), Bo[b][:], ACT.Copy).then_inc(s_oc, 1)

        @block.vector
        def _(dve):
            v = nc.vector
            v.memset(Bs[:], 0.0).then_inc(s_set, 1)
            v.memset(S[:], 0.0).then_inc(s_set, 1)
            dve.wait_ge(s_set, 2)
            v.tensor_copy(S[:], Bs[:]).then_inc(s_Sc, 1)
            with dve.Fori(0, NCH // 2) as it:
                for b in range(2):
                    n = it * 2 + b
                    dve.wait_ge(s_u, n + 1)
                    v.tensor_copy(ua[:], Bu[b][:]).then_inc(s_ua, 1)
                    dve.wait_ge(s_S, n + 1)
                    v.tensor_copy(S[:], Bs[:]).then_inc(s_Sc, 1)


def gate_stage(nc, sem, oT, long_fir, v_rows, s_rows, x_in, x_out, w, consts):
    where, ncon = constant_columns()
    NH, NA = 4, 4
    TH = GT * NH
    x_tiles = x_in.rearrange("(g t p) c -> g p t c", t=GT, p=P)
    o_tiles = x_out.rearrange("(g t p) c -> g p t c", t=GT, p=P)
    v_tiles = v_rows.rearrange("(g t p) c -> g p t c", t=GT, p=P)
    s_tiles = s_rows.rearrange("(g t p) c -> g p t c", t=GT, p=P)
    ctx = ExitStack()
    with ctx:
        def sb(name, shape, dt=F32):
            return ctx.enter_context(nc.sbuf_tensor("g_" + name, shape, dt))

        con = sb("con", [P, ncon])
        C = {k: con[:, a:b] for k, (a, b) in where.items()}
        g1 = sb("g1", [P, P])
        g1s = sb("g1s", [P, P])
        gb1 = sb("gb1", [P, 1])
        gw2 = sb("gw2", [P, NA])
        wid = sb("wid", [P, P])
        wo = sb("wo", [P, P])
        onw = sb("onw", [P, 1])
        par = sb("par", [P, 3, NH * NA])
        crl = sb("crl", [P, NH])
        alpha = sb("alpha", [P, NH])
        itemp = sb("itemp", [P, NH * NA])
        floor = sb("floor", [P, NH, NA])
        keepf = sb("keepf", [P, NH])
        res = sb("res", [P, NH])
        eps = sb("eps", [P, 1])
        xt = [sb(f"xt{i}", [P, GT, P]) for i in range(2)]
        xo = [sb(f"xo{i}", [P, GT, P]) for i in range(2)]
        X = [sb(f"X{i}", [P, NA, TH, 32]) for i in range(2)]
        xc = sb("xc", [P, NA, TH, 32])
        mix = sb("mix", [P, NA, TH, 32])
        od = [sb(f"od{i}", [P, GSEQ, NCH, 32]) for i in range(2)]
        xT = [sb(f"xT{i}", [P, GTOK]) for i in range(2)]
        ss = sb("ss", [P, 4, NA * TH])
        stt = sb("stt", [P, TH, 32])
        sT = sb("sT", [P, GTOK])
        hid = sb("hid", [P, NH, GTOK])
        lg = sb("lg", [P, TH, NA])
        mx = sb("mx", [P, TH])
        pr = sb("pr", [P, TH, NA])
        o = sb("o", [P, TH, 32])
        o2 = sb("o2", [P, TH, 32])
        oc = sb("oc", [P, GTOK])
        bst = sb("bst", [P, GT, 6])
        mv = sb("mv", [P, GT, 2])
        sdv = sb("sdv", [P, GT])
        rsv = sb("rsv", [P, GT])
        B = [ctx.enter_context(nc.psum_tensor(f"g_bank{i}", [P, GTOK], F32))[:, :] for i in range(8)]

        def s(name):
            return sem("gate_" + name)

        s_w, s_set, s_x, s_out, s_xo = s("weights_in"), s("constants_set"), [s("rows_in_0"), s("rows_in_1")], s("rows_out"), s("rows_ready")
        s_pa, s_pv = s("parameters_scalar"), s("parameters_vector")
        s_Td = s("delta_transposed")
        s_od, s_T, s_xT, s_Xl, s_Xd = s("delta_copied"), s("transposed"), s("channel_major"), s("long_branch"), s("delta_branch")
        s_xc, s_sq, s_ms, s_l2, s_st = s("centered"), s("squared"), s("mean_squares"), s("norms"), s("stats")
        s_stp, s_sT, s_h, s_hid, s_lg = s("stats_transposed"), s("stats_copied"), s("hidden"), s("gelu"), s("logits")
        s_sh, s_ex, s_id, s_o, s_o2 = s("logits_shifted"), s("exps"), s("identity_branch"), s("mixed"), s("mixed_squared")
        s_rms, s_rsd, s_on, s_ot, s_oc = s("mixed_mean_square"), s("mixed_deviation"), s("normed"), s("normed_transposed"), s("normed_copied")
        s_pj, s_z, s_sd, s_dve = s("projected"), s("sum_stats"), s("sum_deviation"), s("vector_steps")
        block = ctx.enter_context(nc.Block())
        one = lambda rows, n: rows[bass.ds(n, 1)].rearrange("g p t c -> (g p) t c")
        NW = 16 * 13

        def steps(eng, step):
            step(0, 0, 0, True, False)
            with eng.Fori(0, NG // 2 - 2) as it:
                step(it * 2 + 1, 1, it + 1, False, False)
                step(it * 2 + 2, 0, it + 1, False, False)
            for n in range(NG - 3, NG):
                step(n, n % 2, (n + 1) // 2, False, n == NG - 1)

        @block.sync
        def _(sp):
            bc = lambda a, k: a.broadcast_to([P, k])
            flat = lambda a: a.rearrange("p (t h) c -> p t (h c)", t=GT)

            def load(n, b):
                sp.dma_start(xt[b][:], one(x_tiles, n)).then_inc(s_x[b], 16)
                sp.dma_start(flat(X[b][:, 0]), one(s_tiles, n)).then_inc(s_x[b], 16)
                sp.dma_start(flat(X[b][:, 3]), one(v_tiles, n)).then_inc(s_x[b], 16)

            load(0, 0)
            load(1, 1)
            loads = [(con[:], consts), (g1[:], w["g1"]), (g1s[:], w["g1s"]), (gb1[:], w["gb1"]), (gw2[:], w["gw2"]),
                     (wid[:], w["wid"]), (wo[:], w["wo"]), (onw[:], w["onw"]), (par[:, 0], bc(w["gb2"], 16)),
                     (par[:, 1], bc(w["log_temp"], 16)), (par[:, 2], bc(w["floor"], 16)), (crl[:], bc(w["crl"], 4)),
                     (alpha[:], bc(w["alpha"], 4))]
            for dst, src in loads:
                sp.dma_start(dst, src).then_inc(s_w, 16)

            def step(n, b, more=True, first=False):
                if more:
                    sp.wait_ge(s_o, n + 1)
                    load(n + 2, b)
                if not first:
                    sp.wait_ge(s_out, 16 * n)
                sp.wait_ge(s_xo, n + 1)
                sp.dma_start(one(o_tiles, n), xo[b][:]).then_inc(s_out, 16)

            step(0, 0, first=True)
            step(1, 1)
            with sp.Fori(1, NG // 2 - 1) as it:
                for b in range(2):
                    step(it * 2 + b, b)
            step(NG - 2, 0, more=False)
            step(NG - 1, 1, more=False)
            sp.wait_ge(s_out, 16 * NG)

        @block.gpsimd
        def _(pool):
            nc.gpsimd.memset(eps[:], LN_EPS).then_inc(s_set, 1)
            nc.gpsimd.memset(stt[:], 0.0).then_inc(s_set, 1)

            def delta_rows(n, b):
                nc.gpsimd.tensor_copy(od[b][:], oT[:, :, bass.ds(n * GSEQ, GSEQ), :].rearrange("p n s c -> p s n c")
                                      ).then_inc(s_od, 1)

            def long_rows(n, b):
                nc.gpsimd.tensor_copy(X[b][:, 1].rearrange("p (t h) c -> p t (h c)", t=GT),
                                      long_fir[:, bass.ds(n * GT, GT), :]).then_inc(s_Xl, 1)

            def square(m):
                pool.wait_ge(s_xc, m + 1)
                nc.gpsimd.tensor_tensor(xc[:], xc[:], xc[:], ALU.mult).then_inc(s_sq, 1)

            delta_rows(0, 0)
            long_rows(0, 0)
            square(0)
            delta_rows(1, 1)
            long_rows(1, 1)

            def step(n, b, r, first, last):
                if not last:
                    square(n + 1)
                if not isinstance(n, int) or n < NG - 2:
                    pool.wait_ge(s_Td, n + 1)
                    delta_rows(n + 2, b)
                    pool.wait_ge(s_o, n + 1)
                    long_rows(n + 2, b)

            steps(pool, step)

        @block.tensor
        def _(pe):
            mm = nc.tensor.matmul
            tiles = [slice(t * P, (t + 1) * P) for t in range(GT)]
            pe.wait_ge(s_w, NW)
            pe.wait_ge(s_pv, 1)

            def turn_residual(m, b, r, first=False):
                pe.wait_ge(s_x[b], 48 * r + 48)
                if not first:
                    pe.wait_ge(s_xT, m)
                for t in range(GT):
                    i = nc.tensor.transpose(B[0][:, tiles[t]], xt[b][:, t, :], C["ident"])
                i.then_inc(s_T, 1)

            def turn_delta(m, b, first=False):
                pe.wait_ge(s_od, m + 1)
                if not first:
                    pe.wait_ge(s_Xd, m)
                for t in range(GT):
                    i = nc.tensor.transpose(B[1][:, tiles[t]],
                                            od[b][:].rearrange("p s n c -> p (s n c)")[:, tiles[t]], C["ident"])
                i.then_inc(s_Td, 1)

            def hidden_state(m, b):
                pe.wait_ge(s_xT, m + 1)
                for h in range(NH):
                    mm(B[4 + h], g1[:], xT[b][:], start=True, stop=False)

            def step(n, b, r, first, last):
                pe.wait_ge(s_st, n + 1)
                stats = stt[:].rearrange("p (t h) k -> p t (h k)", t=GT)
                for t in range(GT):
                    i = nc.tensor.transpose(B[3][:, tiles[t]], stats[:, t, :], C["ident"])
                i.then_inc(s_stp, 1)
                pe.wait_ge(s_sT, n + 1)
                for h in range(NH):
                    rows = slice(32 * h, 32 * h + 32)
                    mm(B[4 + h], g1s[rows, :], sT[rows, :], start=False, stop=True).then_inc(s_h, 1)
                for h in range(NH):
                    pe.wait_ge(s_hid, 4 * n + h + 1)
                    for t in range(GT):
                        i = mm(B[4][:, (t * NH + h) * NA:(t * NH + h + 1) * NA], hid[:, h, tiles[t]], gw2[:],
                               start=True, stop=True)
                i.then_inc(s_lg, 1)
                if not first:
                    pe.wait_ge(s_xo, n)
                for t in range(GT):
                    i = mm(B[2][:, tiles[t]], xT[b][:, tiles[t]], wid[:], start=True, stop=True)
                i.then_inc(s_id, 1)
                if not last:
                    turn_residual(n + 1, 1 - b, r)
                if not isinstance(n, int) or n < NG - 2:
                    turn_delta(n + 2, b)
                if not last:
                    pe.wait_ge(s_sh, n + 1)
                    hidden_state(n + 1, 1 - b)
                pe.wait_ge(s_on, n + 1)
                for t in range(GT):
                    i = nc.tensor.transpose(B[3][:, tiles[t]],
                                            o2[:].rearrange("p (t h) c -> p t (h c)", t=GT)[:, t, :], C["ident"])
                i.then_inc(s_ot, 1)
                pe.wait_ge(s_oc, n + 1)
                for t in range(GT):
                    mm(B[2][:, tiles[t]], oc[:, tiles[t]], wo[:], start=True, stop=False)
                    i = mm(B[2][:, tiles[t]], xT[b][:, tiles[t]], C["ident"], start=False, stop=True)
                i.then_inc(s_pj, 1)

            turn_residual(0, 0, 0, first=True)
            turn_delta(0, 0, first=True)
            turn_delta(1, 1)
            hidden_state(0, 0)
            steps(pe, step)

        @block.scalar
        def _(act):
            op = nc.scalar.activation
            act.wait_ge(s_w, NW)
            act.wait_ge(s_set, 2)
            op(itemp[:], par[:, 1], ACT.Exp, scale=-1.0).then_inc(s_pa, 1)
            op(floor[:].rearrange("p h a -> p (h a)"), par[:, 2], ACT.Sigmoid).then_inc(s_pa, 1)
            op(res[:], crl[:], ACT.Sigmoid).then_inc(s_pa, 1)

            def channel_major(m, b):
                act.wait_ge(s_T, m + 1)
                op(xT[b][:], B[0], ACT.Copy).then_inc(s_xT, 1)

            def delta_branch(m, b):
                act.wait_ge(s_Td, m + 1)
                op(X[b][:, 2].rearrange("p a c -> p (a c)"), B[1], ACT.Copy).then_inc(s_Xd, 1)

            def norms(m):
                act.wait_ge(s_ms, m + 1)
                op(stt[:].rearrange("p j (a k) -> p a j k", k=4)[:, 0:NA, :, 3],
                   ss[:, 3].rearrange("p (a j) -> p a j", a=NA), ACT.Sqrt, scale=32.0).then_inc(s_l2, 1)

            def sum_deviation(n):
                act.wait_ge(s_z, n + 1)
                op(sdv[:], mv[:, :, 1], ACT.Sqrt, bias=eps[:, 0:1]).then_inc(s_sd, 1)

            def step(n, b, r, first, last):
                act.wait_ge(s_stp, n + 1)
                op(sT[:], B[3], ACT.Copy).then_inc(s_sT, 1)
                for h in range(NH):
                    act.wait_ge(s_h, 4 * n + h + 1)
                    op(hid[:, h, :], B[4 + h], ACT.Gelu, bias=gb1[:, 0:1]).then_inc(s_hid, 1)
                if not first:
                    sum_deviation(n - 1)
                if not last:
                    norms(n + 1)
                act.wait_ge(s_sh, n + 1)
                op(pr[:], lg[:], ACT.Exp).then_inc(s_ex, 1)
                if not last:
                    if not first:
                        act.wait_ge(s_pj, n)
                    channel_major(n + 1, 1 - b)
                act.wait_ge(s_o, n + 1)
                op(o2[:], o[:], ACT.Square).then_inc(s_o2, 1)
                if not isinstance(n, int) or n < NG - 2:
                    delta_branch(n + 2, b)
                act.wait_ge(s_rms, n + 1)
                op(mx[:], mx[:], ACT.Sqrt, bias=eps[:, 0:1], scale=1.0 / 32).then_inc(s_rsd, 1)
                act.wait_ge(s_ot, n + 1)
                op(oc[:], B[3], ACT.Copy).then_inc(s_oc, 1)

            channel_major(0, 0)
            delta_branch(0, 0)
            delta_branch(1, 1)
            norms(0)
            steps(act, step)
            sum_deviation(NG - 1)

        @block.vector
        def _(dve):
            v = nc.vector
            own = Steps(s_dve)

            def then(ins):
                dve.wait_ge(s_dve, own.mark(ins))

            dve.wait_ge(s_w, NW)
            dve.wait_ge(s_set, 2)
            dve.wait_ge(s_pa, 3)
            own.restart(dve)
            then(v.tensor_scalar(floor[:], floor[:], 0.05, None, ALU.mult))
            then(v.tensor_reduce(keepf[:], floor[:], AX_X, ALU.add))
            then(v.tensor_scalar(keepf[:], keepf[:], -1.0, 1.0, ALU.mult, ALU.add))
            then(v.tensor_tensor(floor[:, :, 0], floor[:, :, 0], res[:], ALU.add))
            then(v.tensor_tensor(wid[:].rearrange("p (h c) -> p h c", h=NH), wid[:].rearrange("p (h c) -> p h c", h=NH),
                                 alpha[:].unsqueeze(2).broadcast_to([P, NH, 32]), ALU.mult))
            v.tensor_scalar(wo[:], wo[:], onw[:, 0:1], None, ALU.mult).then_inc(s_pv, 1)
            dve.wait_ge(s_pv, 1)
            tiles4 = lambda a: a.unsqueeze(1).broadcast_to([P, GT, NH * NA])
            wide = lambda a, k: a.unsqueeze(2).broadcast_to([P, TH, k])
            st4 = stt[:].rearrange("p j (a k) -> p a j k", k=4)[:, 0:NA]
            by_a = lambda k: ss[:, k].rearrange("p (a j) -> p a j", a=NA)
            c64 = xc[:].rearrange("p a j c -> p (a j) c")

            def center(m, b, r):
                x64 = X[b][:].rearrange("p a j c -> p (a j) c")
                dve.wait_ge(s_x[b], 48 * r + 48)
                dve.wait_ge(s_Xl, m + 1)
                dve.wait_ge(s_Xd, m + 1)
                i = own.mark(v.tensor_reduce(ss[:, 0], x64, AX_X, ALU.add))
                v.tensor_reduce(ss[:, 1], x64, AX_X, ALU.add, apply_absolute_value=True)
                dve.wait_ge(s_dve, i)
                then(v.tensor_scalar(ss[:, 0], ss[:, 0], 1.0 / 32, None, ALU.mult))
                v.tensor_tensor(c64, x64, ss[:, 0].unsqueeze(2).broadcast_to([P, NA * TH, 32]), ALU.subtract
                                ).then_inc(s_xc, 1)

            def squares(m, first=False):
                if not first:
                    dve.wait_ge(s_stp, m)
                v.tensor_copy(st4[:, :, :, 0], by_a(0))
                then(v.tensor_scalar(st4[:, :, :, 2], by_a(1), 1.0 / 32, None, ALU.mult))
                then(v.tensor_tensor(ss[:, 3], ss[:, 0], ss[:, 0], ALU.mult))
                dve.wait_ge(s_sq, m + 1)
                then(v.tensor_reduce(ss[:, 2], c64, AX_X, ALU.add))
                v.scalar_tensor_tensor(ss[:, 3], ss[:, 2], 1.0 / 32, ss[:, 3], ALU.mult, ALU.add).then_inc(s_ms, 1)

            def variances(m):
                dve.wait_ge(s_l2, m + 1)
                v.tensor_scalar(st4[:, :, :, 1], by_a(2), 1.0 / 32, None, ALU.mult).then_inc(s_st, 1)

            def layer_norm(n, b, first=False):
                z = B[2].rearrange("p (t c) -> p t c", t=GT)
                dve.wait_ge(s_pj, n + 1)
                for t in range(GT):
                    i = own.mark(v.bn_stats(bst[:, t, :], z[:, t, :]))
                dve.wait_ge(s_dve, i)
                for t in range(GT):
                    i = v.bn_aggr(mv[:, t, :], bst[:, t, :])
                i.then_inc(s_z, 1)
                dve.wait_ge(s_sd, n + 1)
                then(v.reciprocal(rsv[:], sdv[:]))
                if not first:
                    dve.wait_ge(s_out, 16 * n)
                for t in range(GT):
                    i = v.tensor_scalar(xo[b][:, t, :], z[:, t, :], mv[:, t, 0:1], rsv[:, t:t + 1],
                                        ALU.subtract, ALU.mult)
                i.then_inc(s_xo, 1)

            def step(n, b, r, first, last):
                own.restart(dve)
                if not last:
                    center(n + 1, 1 - b, r)
                if not first:
                    layer_norm(n - 1, 1 - b, first=isinstance(n, int) and n == 1)
                if not last:
                    squares(n + 1)
                dve.wait_ge(s_lg, n + 1)
                then(v.tensor_tensor(lg[:].rearrange("p (t h) a -> p t (h a)", t=GT),
                                     B[4][:, 0:TH * NA].rearrange("p (t k) -> p t k", t=GT), tiles4(par[:, 0]), ALU.add))
                then(v.tensor_tensor(lg[:].rearrange("p (t h) a -> p t (h a)", t=GT),
                                     lg[:].rearrange("p (t h) a -> p t (h a)", t=GT), tiles4(itemp[:]), ALU.mult))
                then(v.tensor_reduce(mx[:], lg[:], AX_X, ALU.max))
                v.tensor_tensor(lg[:], lg[:], wide(mx[:], NA), ALU.subtract).then_inc(s_sh, 1)
                dve.wait_ge(s_ex, n + 1)
                then(v.tensor_reduce(mx[:], pr[:], AX_X, ALU.add))
                then(v.reciprocal(mx[:], mx[:]))
                then(v.tensor_tensor(mx[:].rearrange("p (t h) -> p t h", t=GT), mx[:].rearrange("p (t h) -> p t h", t=GT),
                                     keepf[:].unsqueeze(1).broadcast_to([P, GT, NH]), ALU.mult))
                then(v.tensor_tensor(pr[:], pr[:], wide(mx[:], NA), ALU.mult))
                then(v.tensor_tensor(pr[:].rearrange("p (t h) a -> p t (h a)", t=GT),
                                     pr[:].rearrange("p (t h) a -> p t (h a)", t=GT),
                                     tiles4(floor[:].rearrange("p h a -> p (h a)")), ALU.add))
                for a in range(NA):
                    i = own.mark(v.tensor_tensor(mix[:, a], X[b][:, a], wide(pr[:, :, a], 32), ALU.mult))
                dve.wait_ge(s_dve, i)
                then(v.tensor_reduce(o[:], mix[:].rearrange("p a j c -> p j c a"), AX_X, ALU.add))
                dve.wait_ge(s_id, n + 1)
                v.tensor_tensor(o[:], o[:], B[2].rearrange("p (j c) -> p j c", c=32), ALU.add).then_inc(s_o, 1)
                if not last:
                    variances(n + 1)
                dve.wait_ge(s_o2, n + 1)
                v.tensor_reduce(mx[:], o2[:], AX_X, ALU.add).then_inc(s_rms, 1)
                dve.wait_ge(s_rsd, n + 1)
                then(v.reciprocal(mx[:], mx[:]))
                v.tensor_tensor(o2[:], o[:], wide(mx[:], 32), ALU.mult).then_inc(s_on, 1)

            center(0, 0, 0)
            squares(0, first=True)
            variances(0)
            steps(dve, step)
            own.restart(dve)
            layer_norm(NG - 1, 1)


def delta_stage(nc, sem, x_in, x_out, v_rows, s_rows, w, consts):
    with ExitStack() as ctx:
        def sb(name, shape):
            return ctx.enter_context(nc.sbuf_tensor("keep_" + name, shape, F32))

        long_fir = sb("long_fir", [P, TOK // P, P])
        oT = sb("oT", [P, NCH, NSEQ, 32])
        with ExitStack() as inner:
            keep = {k: inner.enter_context(nc.sbuf_tensor("keep_" + k, [P, NCH, NSEQ, 32], F32))
                    for k in ("A", "kb", "vb", "k", "q", "attn")}
            delta_project(nc, sem, keep, x_in, v_rows, s_rows, w, consts)
            delta_invert(nc, sem, keep, long_fir, v_rows, w, consts)
            delta_recur(nc, sem, keep, oT)
        gate_stage(nc, sem, oT, long_fir, v_rows, s_rows, x_in, x_out, w, consts)


def host_layout(inp):
    a = {k: np.asarray(v) for k, v in inp.items()}
    col = lambda v: v.reshape(-1, 1)
    L = "L0_attn_"
    d = {}
    d["a_maa"] = np.stack([a[L + "time_maa_" + c].reshape(-1) for c in "xwkvrg"], 1)
    d["a_maa_w1"] = a[L + "time_maa_w1"]
    d["a_maa_w2"] = a[L + "time_maa_w2"]
    d["a_dec_w1"] = a[L + "time_decay_w1"]
    d["a_dec_w2"] = a[L + "time_decay_w2"]
    d["a_decay"] = col(a[L + "time_decay"])
    d["a_wT"] = np.stack([a[L + "W_" + c].T for c in "rkvgo"], 1)
    d["a_lnwb"] = np.stack([a[L + "ln_w"], a[L + "ln_b"]], 1)
    for tag, L in (("b", "L0_ffn_"), ("d", "L1_ffn_")):
        d[tag + "_gate_w"] = a[L + "gate_w"].T if tag == "b" else a[L + "gate_w"]
        if tag == "d":
            d[tag + "_gate_b"] = a[L + "gate_b"].reshape(1, -1)
        d[tag + "_w1"] = a[L + "w1"].transpose(1, 0, 2).reshape(P, 8, 4, P)
        d[tag + "_b1"] = a[L + "b1"].reshape(8, 4, P).transpose(2, 0, 1)
        d[tag + "_w2"] = a[L + "w2"].reshape(8, 4, P, P).transpose(2, 0, 1, 3)
        d[tag + "_b2"] = a[L + "b2"]
    delta_layout(a, d)
    return d


def delta_layout(a, d):
    L = "L1_attn_"
    d["c_wqkv"] = np.stack([a[L + "W" + c] for c in "qkv"], 1)
    d["c_wb"] = np.repeat(a[L + "Wb"], 32, axis=1)
    d["c_taps"] = np.stack([a[L + "cw" + c] for c in "qkv"], 1)
    d["c_firs"] = a[L + "firs"].reshape(P, 3)
    firl = a[L + "firl"].reshape(P, 63)
    d["c_firl"] = np.concatenate([np.zeros((P, 127), firl.dtype), firl[:, ::-1], np.zeros((P, 129), firl.dtype)], 1)
    d["c_g1"] = a[L + "gW1"][:P]
    g1s = np.zeros((4, 32, P), a[L + "gW1"].dtype)
    g1s[:, :16] = a[L + "gW1"][P:]
    d["c_g1s"] = g1s.reshape(P, P)
    d["c_gb1"] = a[L + "gb1"].reshape(P, 1)
    d["c_gw2"] = a[L + "gW2"]
    d["c_wid"] = a[L + "Wid"]
    d["c_wo"] = a[L + "Wo"]
    d["c_onw"] = np.tile(a[L + "o_norm_w"], 4).reshape(P, 1)
    d["c_gb2"] = np.tile(a[L + "gb2"], 4).reshape(1, 16)
    d["c_log_temp"] = a[L + "log_temp"].reshape(1, 16)
    d["c_floor"] = a[L + "floor_param"].reshape(1, 16)
    d["c_crl"] = a[L + "conv_res_logit"].reshape(1, 4)
    d["c_alpha"] = a[L + "alpha_id"].reshape(1, 4)


def block_program(nc, ins, out, scratch):
    pick = lambda tag: {k[2:]: v for k, v in ins.items() if k.startswith(tag + "_")}
    x1, x2, x3, v_rows, s_rows, b_sorted, b_results, d_sorted, d_results = scratch
    def stage(build, *args):
        sems = []

        def sem(name):
            sems.append(nc.alloc_semaphore(name=name))
            return sems[-1]

        build(nc, sem, *args)
        nc.all_engine_barrier()
        nc.clear_and_free_semaphores(sems)
        nc.all_engine_barrier()

    stage(lion_stage, ins["x"], x1, pick("a"), ins["consts"])
    stage(moe_stage, "b", x1, x2, b_sorted, b_results, pick("b"), ins["consts"], 2, ACT.Relu, False)
    stage(delta_stage, x2, x3, v_rows, s_rows, pick("c"), ins["consts"])
    stage(moe_stage, "d", x3, out, d_sorted, d_results, pick("d"), ins["consts"], 1, ACT.Gelu, True)


def kernel(**inputs):
    import concourse.bacc as _bacc
    from concourse.bass_utils import run_bass_kernel_spmd as _run

    given = {k: np.asarray(v) for k, v in inputs.items()}
    nc = _bacc.Bacc("TRN2", target_bir_lowering=False, num_devices=1)
    laid = {"x": given["L0_attn_x"].reshape(TOK, P),
            "consts": np.concatenate(list(shape_constants().values()), 1)}
    laid.update(host_layout(given))
    arrays, ins = {}, {}
    for name, a in laid.items():
        a = np.ascontiguousarray(a)
        arrays["in_" + name] = a
        ins[name] = nc.dram_tensor("in_" + name, a.shape, mybir.dt.from_np(a.dtype), kind="ExternalInput").ap()
    out = nc.dram_tensor("out_rows", (TOK, P), F32, kind="ExternalOutput").ap()
    scratch = [nc.dram_tensor(f"rows_{i}", (TOK, P), F32, kind="Internal").ap() for i in range(5)]
    for tag, topk in (("b", 2), ("d", 1)):
        scratch += [nc.dram_tensor(f"{name}_{tag}", (expert_tiles(topk) * P, P), F32, kind="Internal").ap()
                    for name in ("sorted", "results")]
    block_program(nc, ins, out, scratch)
    r = _run(nc, [arrays], core_ids=[0])
    return r.results[0]["out_rows"].reshape(NSEQ, SEQ, P)
```

```python
from contextlib import ExitStack

import numpy as np

import concourse.bass as bass
from concourse import mybir

F32 = mybir.dt.float32
U32 = mybir.dt.uint32
I32 = mybir.dt.int32
ALU = mybir.AluOpType
ACT = mybir.ActivationFunctionType
AX_X = mybir.AxisListType.X

P = 128
SEQ = 256
NSEQ = 16
TOK = NSEQ * SEQ
GT = 4
GTOK = GT * P
GSEQ = GTOK // SEQ
NG = TOK // GTOK
LN_EPS = 1e-5


class Steps:

    def __init__(self, sem):
        self.sem, self.n = sem, 0

    def restart(self, eng):
        eng.sem_clear(self.sem)
        self.n = 0

    def mark(self, ins):
        ins.then_inc(self.sem, 1)
        self.n += 1
        return self.n


def shape_constants():
    p = np.arange(P)
    c = {}
    c["ident"] = np.eye(P)
    c["flip"] = np.eye(P)[::-1]
    j, i = (p % 32)[:, None], np.arange(32)[None, :]
    c["diag"] = np.concatenate([i < j, i >= j], 1)
    c["heads16"] = (p // 8)[:, None] == np.arange(16)[None, :]
    c["vhead"] = (p // 32)[:, None] == ((p % 32) // 8)[None, :]
    c["same8"] = (p // 8)[:, None] == (p // 8)[None, :]
    c["mean8"] = c["same8"] / 8.0
    c["center8"] = np.eye(P) - c["mean8"]
    c["experts"] = np.broadcast_to(np.arange(8.0), (P, 8))
    c["before"] = p[:, None] < p[None, :]
    c["ones"] = np.ones((P, P))
    c["limits"] = np.broadcast_to(np.arange(TOK // P) * float(P), (P, TOK // P))
    c["tiles"] = np.broadcast_to(np.arange(80.0), (P, 80))
    c["repeat"] = np.concatenate([p[:, None] == 32 * q + (p % 32)[None, :] for q in range(4)], 1)
    c["strict"] = -1.0 * (i > j)
    c["incl"] = 1.0 * (i >= j)
    c["same32"] = (p // 32)[:, None] == (p // 32)[None, :]
    c["mean32"] = c["same32"] / 32.0
    c["heads32"] = (p // 32)[:, None] == np.arange(4)[None, :]
    return {k: v.astype(np.float32) for k, v in c.items()}


def constant_columns():
    at, where = 0, {}
    for k, v in shape_constants().items():
        where[k] = (at, at + v.shape[1])
        at += v.shape[1]
    return where, at


def stream_rows(sp, x_rows, o_rows, xt, xo, s_x, s_xo, s_out):
    one = lambda rows, n: rows[bass.ds(n, 1)].rearrange("g p t c -> (g p) t c")

    def group(n, b, more, first=False):
        if not first:
            sp.wait_ge(s_out, 16 * n)
        if more:
            sp.dma_start(xt[1 - b][:], one(x_rows, n + 1)).then_inc(s_x[1 - b], 16)
        sp.wait_ge(s_xo, n + 1)
        sp.dma_start(one(o_rows, n), xo[b][:]).then_inc(s_out, 16)

    sp.dma_start(xt[0][:], one(x_rows, 0)).then_inc(s_x[0], 16)
    group(0, 0, True, first=True)
    group(1, 1, True)
    with sp.Fori(1, NG // 2 - 1) as it:
        for b in range(2):
            group(it * 2 + b, b, True)
    group(NG - 2, 0, True)
    group(NG - 1, 1, False)


def lion_stage(nc, sem, x_in, x_out, w, consts):
    where, ncon = constant_columns()
    D_MIX, D_DECAY, NF = 32, 64, 5
    SPLIT = 12
    x_rows = x_in.rearrange("(g t p) c -> g p t c", t=GT, p=P)
    o_rows = x_out.rearrange("(g t p) c -> g p t c", t=GT, p=P)
    ctx = ExitStack()
    with ctx:
        def sb(name, shape, dt=F32):
            return ctx.enter_context(nc.sbuf_tensor("a_" + name, shape, dt))

        def bank(name, shape=(P, GTOK)):
            return ctx.enter_context(nc.psum_tensor("a_" + name, list(shape), F32))

        con = sb("con", [P, ncon])
        C = {k: con[:, a:b] for k, (a, b) in where.items()}
        maa = sb("maa", [P, 6])
        maa_w1 = sb("maa_w1", [P, NF * D_MIX])
        maa_w2 = sb("maa_w2", [P, NF, P])
        dec_w1 = sb("dec_w1", [P, D_DECAY])
        dec_w2 = sb("dec_w2", [D_DECAY, P])
        decay = sb("decay", [P, 1])
        wT = sb("wT", [P, 5, P])
        lnwb = sb("lnwb", [P, 2])
        eps = sb("eps", [P, 2])
        xt = [sb(f"xt{i}", [P, GT, P]) for i in range(2)]
        xr = [sb(f"xr{i}", [P, GT, P]) for i in range(2)]
        xp = sb("xp", [P, GSEQ, SEQ + 2])
        dx = sb("dx", [P, GTOK])
        nb = sb("nb", [P, GTOK])
        xin = sb("xin", [P, GTOK])
        hid1 = sb("hid1", [P, GTOK])
        hid2 = sb("hid2", [D_MIX, GTOK])
        xf = [sb(f"xf{i}", [P, GTOK]) for i in range(NF)]
        hdec = sb("hdec", [D_DECAY, GTOK])
        ew = sb("ew", [P, GTOK])
        ones = sb("ones", [P, SEQ])
        E = sb("E", [P, 2, GTOK])
        ex = sb("ex", [P, 2, 2, GTOK])
        rk = [sb(f"rk{i}", [P, 4, GTOK]) for i in range(2)]
        kx = [sb(f"kx{i}", [P, 2, GTOK // 32, 4, 32]) for i in range(4)]
        vx = [sb(f"vx{i}", [P, GTOK // 32, P]) for i in range(2)]
        vt = sb("vt", [P, GT, P])
        kt = sb("kt", [P, GT, P])
        st = [sb(f"st{i}", [P, GT, P]) for i in range(2)]
        at = [sb(f"at{i}", [P, 4, 2, 160]) for i in range(2)]
        y = sb("y", [P, GTOK])
        sq = sb("sq", [P, GTOK])
        sd = sb("sd", [P, GTOK])
        rs = sb("rs", [P, GTOK])
        gs = [sb(f"gs{i}", [P, GTOK]) for i in range(2)]
        mid = sb("mid", [P, 2 * GSEQ])
        ya = sb("ya", [P, GTOK])
        yn = sb("yn", [P, GTOK])
        z = sb("z", [P, GT, P])
        bst = sb("bst", [P, GT, 6])
        mv = sb("mv", [P, GT, 2])
        sdv = sb("sdv", [P, GT])
        rsv = sb("rsv", [P, GT])
        xo = [sb(f"xo{i}", [P, GT, P]) for i in range(2)]
        S4 = bank("scores", (P, 4, GTOK))
        Y = bank("y_bank")[:, :]
        X0, X1, X2 = [bank(f"free{i}")[:, :] for i in range(3)]

        s_w, s_zero = sem("lion_weights_in"), sem("lion_constants_set")
        s_x = [sem(f"lion_rows_in_{i}") for i in range(2)]
        s_xr = [sem(f"lion_residual_in_{i}") for i in range(2)]
        s_T, s_xp, s_xin = sem("lion_x_transposed"), sem("lion_x_channel_major"), sem("lion_mix_input")
        s_h, s_ht, s_mm = sem("lion_mix_hidden"), sem("lion_mix_tanh"), sem("lion_mix_factors")
        s_xf, s_hd, s_hdt = sem("lion_factor_inputs"), sem("lion_decay_hidden"), sem("lion_decay_tanh")
        s_wd, s_ew = sem("lion_decay_logits"), sem("lion_decay_exp")
        s_nf, s_ex = sem("lion_running_sums"), sem("lion_decay_factors")
        s_rk, s_g, s_gs = sem("lion_r_k_projected"), sem("lion_gate_projected"), sem("lion_gate_silu")
        s_v, s_vt = sem("lion_v_projected"), sem("lion_v_rows")
        s_vxp, s_vx = sem("lion_v_chunks_projected"), sem("lion_v_chunks")
        s_kd, s_ktp, s_kt = sem("lion_keys_scaled"), sem("lion_keys_transposed"), sem("lion_key_rows")
        s_kx = sem("lion_keys_spread")
        s_stp, s_st = sem("lion_states"), sem("lion_states_masked")
        s_sc, s_ata, s_atd = sem("lion_scores"), sem("lion_scores_copied"), sem("lion_diagonals_masked")
        s_y, s_ys, s_cen, s_sq = sem("lion_y"), sem("lion_y_copied"), sem("lion_y_centered"), sem("lion_y_squared")
        s_var, s_sd, s_yn = sem("lion_y_variance"), sem("lion_y_deviation"), sem("lion_y_gated")
        s_o, s_z, s_lsd, s_xo = sem("lion_projected"), sem("lion_sum_stats"), sem("lion_sum_deviation"), sem("lion_rows_ready")
        s_out, s_lln = sem("lion_rows_out"), sem("lion_sum_logarithm")
        s_dve, s_act = sem("lion_vector_steps"), sem("lion_scalar_steps")

        block = ctx.enter_context(nc.Block())

        def steps(eng, step):
            step(0, 0, 0, True, False)
            with eng.Fori(0, NG // 2 - 1) as it:
                step(it * 2 + 1, 1, it + 1, False, False)
                step(it * 2 + 2, 0, it + 1, False, False)
            step(NG - 1, 1, NG // 2, False, True)

        @block.sync
        def _(sp):
            one = lambda rows, n: rows[bass.ds(n, 1)].rearrange("g p t c -> (g p) t c")
            sp.dma_start(xt[0][:], one(x_rows, 0)).then_inc(s_x[0], 16)
            loads = [(con[:], consts), (maa[:], w["maa"]), (maa_w1[:], w["maa_w1"]),
                     (dec_w1[:], w["dec_w1"]), (dec_w2[:], w["dec_w2"]), (decay[:], w["decay"]),
                     (wT[:], w["wT"]), (lnwb[:], w["lnwb"])]
            for dst, src in loads:
                sp.dma_start(dst, src).then_inc(s_w, 16)
            sp.wait_ge(s_zero, 1)
            for f in range(NF):
                r = D_MIX * (f % 4)
                sp.dma_start(maa_w2[r:r + D_MIX, f, :], w["maa_w2"][f]).then_inc(s_w, 16)
            sp.dma_start(xt[1][:], one(x_rows, 1)).then_inc(s_x[1], 16)
            for b in range(2):
                sp.dma_start(xr[b][:], one(x_rows, b)).then_inc(s_xr[b], 16)

            def step(n, b, first=False, more=True):
                if more:
                    sp.wait_ge(s_T, n + 1)
                    sp.dma_start(xt[b][:], one(x_rows, n + 2)).then_inc(s_x[b], 16)
                if not first:
                    sp.wait_ge(s_out, 16 * n)
                sp.wait_ge(s_xo, n + 1)
                sp.dma_start(one(o_rows, n), xo[b][:]).then_inc(s_out, 16)
                if more:
                    sp.dma_start(xr[b][:], one(x_rows, n + 2)).then_inc(s_xr[b], 16)

            step(0, 0, first=True)
            step(1, 1)
            with sp.Fori(1, NG // 2 - 1) as it:
                for b in range(2):
                    step(it * 2 + b, b)
            step(NG - 2, 0, more=False)
            step(NG - 1, 1, more=False)
            sp.wait_ge(s_out, 16 * NG)

        NW = 16 * (8 + NF)

        @block.tensor
        def _(pe):
            mm = nc.tensor.matmul
            pe.wait_ge(s_w, NW)
            pe.wait_ge(s_zero, 4)

            def next_group(slot, k, b, r, first=False):
                if slot == 0:
                    pe.wait_ge(s_x[b], 16 * r + 16)
                    if not first:
                        pe.wait_ge(s_sd, k - 1)
                    for t in range(GT):
                        i = nc.tensor.transpose(X0[:, t * P:(t + 1) * P], xt[b][:, t, :], C["ident"])
                    i.then_inc(s_T, 1)
                elif slot == 1:
                    pe.wait_ge(s_xin, k + 1)
                    mm(X1, maa_w1[:, 0:P], xin[:], start=True, stop=True)
                    mm(X2[0:D_MIX, :], maa_w1[:, P:P + D_MIX], xin[:], start=True, stop=True).then_inc(s_h, 1)
                elif slot == 2:
                    pe.wait_ge(s_ht, k + 1)
                    for f, bank_f in enumerate((X0, X1, X2)):
                        mm(bank_f, maa_w2[:, f, :], hid1[:], start=True, stop=True).then_inc(s_mm, 1)
                elif slot == 3:
                    pe.wait_ge(s_xf, NF * k + 1)
                    mm(X0, maa_w2[:, 3, :], hid1[:], start=True, stop=True).then_inc(s_mm, 1)
                    pe.wait_ge(s_xf, NF * k + 2)
                    mm(X1, maa_w2[0:D_MIX, 4, :], hid2[:], start=True, stop=True).then_inc(s_mm, 1)
                    pe.wait_ge(s_xf, NF * k + 3)
                    mm(X2[0:D_DECAY, :], dec_w1[:], xf[0][:], start=True, stop=True).then_inc(s_hd, 1)
                elif slot == 4:
                    pe.wait_ge(s_xf, NF * k + 5)
                    for t in range(GT):
                        i = mm(X1[:, t * P:(t + 1) * P], xf[2][:, t * P:(t + 1) * P], wT[:, 2, :],
                               start=True, stop=True)
                    i.then_inc(s_v, 1)
                    pe.wait_ge(s_hdt, k + 1)
                    mm(X0, dec_w2[:], hdec[:], start=True, stop=True).then_inc(s_wd, 1)
                elif slot in (5, 6):
                    pe.wait_ge(s_vt, k + 1)
                    for h in ((0, 1), (2, 3))[slot - 5]:
                        if h >= 2:
                            pe.wait_ge(s_vx, 4 * k + h - 1)
                        for c in range(4):
                            i = mm((X2, X1)[h % 2][:, c * P:(c + 1) * P], C["repeat"][:, c * P:(c + 1) * P],
                                   vt[:, h, :], start=True, stop=True)
                        i.then_inc(s_vxp, 1)
                    if slot == 5:
                        pe.wait_ge(s_ew, k + 1)
                        mm(X0, wT[:, 3, :], xf[4][:], start=True, stop=True).then_inc(s_g, 1)
                else:
                    pe.wait_ge(s_vx, 4 * k + 4)
                    mm(X1, wT[:, 1, :], xf[1][:], start=True, stop=True)
                    mm(X2, wT[:, 0, :], xf[3][:], start=True, stop=True).then_inc(s_rk, 1)

            def turn_keys(k, b):
                pe.wait_ge(s_gs, k + 1)
                pe.wait_ge(s_kd, k + 1)
                for t in range(GT):
                    i = nc.tensor.transpose(X0[:, t * P:(t + 1) * P],
                                            rk[b][:, 1 + 2 * (t % 2), t * P:(t + 1) * P], C["ident"])
                i.then_inc(s_ktp, 1)

            def states(k):
                pe.wait_ge(s_kt, k + 1)
                for t in range(GT):
                    i = mm(X1[:, t * P:(t + 1) * P], kt[:, t ^ 1, :], vt[:, t ^ 1, :], start=True, stop=True)
                i.then_inc(s_stp, 1)

            def project_out(n):
                pe.wait_ge(s_yn, n + 1)
                for t in range(GT):
                    i = mm(Y[:, t * P:(t + 1) * P], yn[:, t * P:(t + 1) * P], wT[:, 4, :], start=True, stop=True)
                i.then_inc(s_o, 1)

            def step(n, b, r, first, last):
                def attend(m):
                    t, h = m // 2, m % 2
                    if m == 0:
                        pe.wait_ge(s_st, n + 1)
                        if not first:
                            pe.wait_ge(s_z, n)
                    pe.wait_ge(s_atd, 8 * n + m + 1)
                    if h == 0:
                        d = 2 * (1 - t % 2)
                        mm(Y[:, t * P:(t + 1) * P], st[b][:, t, :], rk[b][:, d, t * P:(t + 1) * P],
                           start=(t == 0), stop=False, skip_group_check=True)
                    for g in range(4):
                        for q in (2 * h, 2 * h + 1):
                            k = 32 * q + 32
                            val = vx[b][:, 4 * t + q, 32 * g:32 * g + 32]
                            mm(Y[32 * g:32 * g + 32, t * P:t * P + k], val, at[m % 2][:, g, q % 2, 0:k],
                               start=False, stop=False, skip_group_check=True)
                            i = mm(Y[32 * g:32 * g + 32, t * P + k - 32:(t + 1) * P], val,
                                   at[m % 2][:, g, q % 2, k:160],
                                   start=False, stop=(q == 3), skip_group_check=True)
                    if m == 7:
                        i.then_inc(s_y, 1)

                for m in range(2 * GT):
                    t, h = m // 2, m % 2
                    if m % 4 == 0:
                        pe.wait_ge(s_kx, 4 * n + 2 * (m // 4) + 2)
                    if m:
                        pe.wait_ge(s_ata, 8 * n + m)
                    for g in range(4):
                        for q in (2 * h, 2 * h + 1):
                            o = (q % 2) * 160
                            keys = lambda d: kx[g][:, d, 4 * t + q].rearrange("p h j -> p (h j)")
                            mm(S4[:, g, o + 32:o + 160], keys(0), rk[b][:, 0, t * P:(t + 1) * P],
                               start=True, stop=True, skip_group_check=True)
                            i = mm(S4[:, g, o:o + 32 * q + 32], keys(1),
                                   rk[b][:, 2, t * P:t * P + 32 * q + 32],
                                   start=True, stop=True, skip_group_check=True)
                    i.then_inc(s_sc, 1)
                    if m == 0 and not first:
                        project_out(n - 1)
                    if m:
                        attend(m - 1)
                    if not last:
                        next_group(m, n + 1, 1 - b, r, first=first)
                attend(2 * GT - 1)
                if not last:
                    turn_keys(n + 1, 1 - b)
                pe.wait_ge(s_ys, n + 1)
                mm(X2, C["center8"], y[:], start=True, stop=True).then_inc(s_cen, 1)
                if not last:
                    states(n + 1)
                pe.wait_ge(s_sq, n + 1)
                mm(X0, C["mean8"], sq[:], start=True, stop=True).then_inc(s_var, 1)

            for slot in range(8):
                next_group(slot, 0, 0, 0, first=True)
            turn_keys(0, 0)
            states(0)
            steps(pe, step)
            project_out(NG - 1)

        @block.gpsimd
        def _(pool):
            nc.gpsimd.memset(maa_w2[:], 0.0).then_inc(s_zero, 1)
            nc.gpsimd.memset(eps[:, 0:1], 64e-5).then_inc(s_zero, 1)
            nc.gpsimd.memset(eps[:, 1:2], LN_EPS).then_inc(s_zero, 1)
            nc.gpsimd.memset(ones[:], 1.0).then_inc(s_zero, 1)
            nc.gpsimd.memset(xp[:, :, 0:1], 0.0).then_inc(s_zero, 1)
            nc.gpsimd.memset(xp[:, :, SEQ + 1:SEQ + 2], 0.0).then_inc(s_zero, 1)

        @block.scalar
        def _(act):
            act.wait_ge(s_w, NW)
            act.wait_ge(s_zero, 6)
            op = nc.scalar.activation
            own = Steps(s_act)

            def spread(half, b, first_head=0):
                for h in range(first_head, 16):
                    i = op(kx[h // 4][:, 1, 8 * half:8 * half + 8, h % 4, :],
                           rk[b][:, 3, half * 256:half * 256 + 256].rearrange("p (c j) -> p c j", j=32),
                           ACT.Copy, scale=C["heads16"][:, h:h + 1])
                i.then_inc(s_kx, 1)

            def next_group(slot, k, b):
                if slot == 0:
                    act.wait_ge(s_T, k + 1)
                    op(xp[:, :, 1:SEQ + 1], X0.rearrange("p (s t) -> p s t", s=GSEQ), ACT.Copy).then_inc(s_xp, 1)
                elif slot == 1:
                    act.wait_ge(s_h, k + 1)
                    op(hid1[:], X1, ACT.Tanh)
                    op(hid2[:], X2[0:D_MIX, :], ACT.Tanh).then_inc(s_ht, 1)
                elif slot == 3:
                    act.wait_ge(s_hd, k + 1)
                    op(hdec[:], X2[0:D_DECAY, :], ACT.Tanh).then_inc(s_hdt, 1)
                elif slot == 4:
                    act.wait_ge(s_v, k + 1)
                    op(vt[:].rearrange("p t c -> p (t c)"), X1, ACT.Copy).then_inc(s_vt, 1)
                    act.wait_ge(s_wd, k + 1)
                    op(ew[:], X0, ACT.Exp, bias=decay[:, 0:1]).then_inc(s_ew, 1)
                elif slot == 5:
                    act.wait_ge(s_nf, k + 1)
                    op(ex[:, 0, :, :], E[:], ACT.Exp).then_inc(s_ex, 1)
                    op(ex[:, 1, :, :], E[:], ACT.Exp, scale=-1.0).then_inc(s_ex, 1)
                elif slot == 6:
                    act.wait_ge(s_g, k + 1)
                    op(gs[b][:], X0, ACT.Silu).then_inc(s_gs, 1)

            def key_rows(k):
                act.wait_ge(s_ktp, k + 1)
                op(kt[:].rearrange("p t c -> p (t c)"), X0, ACT.Copy).then_inc(s_kt, 1)

            def sum_deviation(n):
                act.wait_ge(s_z, n + 1)
                op(sdv[:], mv[:, :, 1], ACT.Ln, bias=eps[:, 1:2]).then_inc(s_lln, 1)
                act.wait_ge(s_lln, n + 1)
                op(rsv[:], sdv[:], ACT.Exp, scale=-0.5).then_inc(s_lsd, 1)

            def step(n, b, r, first, last):
                own.restart(act)
                for m in range(2 * GT):
                    act.wait_ge(s_sc, 8 * n + m + 1)
                    op(at[m % 2][:].rearrange("p g q k -> p g (q k)"), S4[:, :, 0:320], ACT.Copy).then_inc(s_ata, 1)
                    if m == 1:
                        spread(1, b)
                    if not last:
                        next_group(m, n + 1, 1 - b)
                    if m == 1 and not first:
                        sum_deviation(n - 1)
                if not last:
                    key_rows(n + 1)
                act.wait_ge(s_y, n + 1)
                op(y[:], Y, ACT.Copy).then_inc(s_ys, 1)
                act.wait_ge(s_cen, n + 1)
                op(sq[:], X2, ACT.Square).then_inc(s_sq, 1)
                if not last:
                    spread(0, 1 - b, first_head=SPLIT)
                act.wait_ge(s_var, n + 1)
                act.wait_ge(s_act, own.mark(op(sd[:], X0, ACT.Ln, bias=eps[:, 0:1])))
                op(rs[:], sd[:], ACT.Exp, scale=-0.5).then_inc(s_sd, 1)

            for slot in range(8):
                next_group(slot, 0, 0)
            key_rows(0)
            spread(0, 0, first_head=SPLIT)
            steps(act, step)
            sum_deviation(NG - 1)

        @block.vector
        def _(dve):
            v = nc.vector
            dve.wait_ge(s_w, NW)
            dve.wait_ge(s_zero, 6)
            own = Steps(s_dve)
            x3 = xp[:, :, 1:SEQ + 1]
            seqs = lambda a: a.rearrange("p (s t) -> p s t", s=GSEQ)

            def then(ins):
                dve.wait_ge(s_dve, own.mark(ins))

            def spread(half, b):
                for d in range(2):
                    for h in range((16, 0 if half else SPLIT)[d]):
                        i = v.tensor_scalar(kx[h // 4][:, d, 8 * half:8 * half + 8, h % 4, :],
                                            rk[b][:, 1 + 2 * d, half * 256:half * 256 + 256].rearrange(
                                                "p (c j) -> p c j", j=32),
                                            C["heads16"][:, h:h + 1], None, ALU.mult)
                i.then_inc(s_kx, 1)

            def factor(f, k):
                dve.wait_ge(s_mm, NF * k + f + 1)
                u = (nb, xin)[f % 2]
                then(v.scalar_tensor_tensor(u[:], (X0, X1, X2, X0, X1)[f], maa[:, 1 + f:2 + f], dx[:], ALU.add, ALU.mult))
                v.tensor_tensor(seqs(xf[f][:]), seqs(u[:]), x3, ALU.add).then_inc(s_xf, 1)

            def next_group(slot, k, b):
                if slot == 0:
                    dve.wait_ge(s_xp, k + 1)
                    then(v.tensor_tensor(seqs(nb[:]), xp[:, :, 0:SEQ], xp[:, :, 2:SEQ + 2], ALU.add))
                    then(v.scalar_tensor_tensor(seqs(dx[:]), seqs(nb[:]), 0.5, x3, ALU.mult, ALU.subtract))
                    v.scalar_tensor_tensor(seqs(xin[:]), seqs(dx[:]), maa[:, 0:1], x3, ALU.mult, ALU.add
                                           ).then_inc(s_xin, 1)
                elif slot == 2:
                    for f in range(3):
                        factor(f, k)
                elif slot == 3:
                    for f in (3, 4):
                        factor(f, k)
                elif slot == 4:
                    dve.wait_ge(s_ew, k + 1)
                    for s in range(GSEQ):
                        r = slice(s * SEQ, (s + 1) * SEQ)
                        i = own.mark(v.tensor_tensor_scan(E[:, 0, r], ones[:], ew[:, r], 0.0, ALU.mult, ALU.add))
                    dve.wait_ge(s_dve, i)
                    then(v.tensor_tensor(E[:, 1, :], E[:, 0, :], ew[:], ALU.subtract))
                    then(v.tensor_copy(mid[:].rearrange("p (d s) -> p d s", d=2),
                                       E[:].rearrange("p d (s t) -> p d s t", s=GSEQ)[:, :, :, SEQ // 2]))
                    for d in range(2):
                        for s in range(GSEQ):
                            r = slice(s * SEQ, (s + 1) * SEQ)
                            i = own.mark(v.tensor_scalar(E[:, d, r], E[:, d, r], mid[:, 2 * d + s:2 * d + s + 1],
                                                         -60.0, ALU.subtract, ALU.max))
                    dve.wait_ge(s_dve, i)
                    v.tensor_scalar(E[:], E[:], 60.0, None, ALU.min).then_inc(s_nf, 1)
                elif slot in (5, 6):
                    for h in ((0, 1), (2, 3))[slot - 5]:
                        dve.wait_ge(s_vxp, 4 * k + h + 1)
                        v.tensor_tensor(vx[b][:, 4 * h:4 * h + 4, :], (X2, X1)[h % 2].rearrange("p (c k) -> p c k", c=4),
                                        C["vhead"].unsqueeze(1).broadcast_to([P, 4, P]), ALU.mult).then_inc(s_vx, 1)
                elif slot == 7:
                    dve.wait_ge(s_ex, 2 * k + 2)
                    dve.wait_ge(s_rk, k + 1)
                    then(v.tensor_tensor(rk[b][:, 1, :], X1, ex[:, 0, 0, :], ALU.mult))
                    v.tensor_tensor(rk[b][:, 3, :], X1, ex[:, 1, 1, :], ALU.mult)
                    v.tensor_tensor(rk[b][:, 0, :], X2, ex[:, 1, 0, :], ALU.mult)
                    v.tensor_tensor(rk[b][:, 2, :], X2, ex[:, 0, 1, :], ALU.mult).then_inc(s_kd, 1)

            def state_mask(k, b):
                dve.wait_ge(s_stp, k + 1)
                v.tensor_tensor(st[b][:], X1.rearrange("p (t c) -> p t c", t=GT),
                                C["same8"].unsqueeze(1).broadcast_to([P, GT, P]), ALU.mult).then_inc(s_st, 1)

            def sums(n, b, r):
                dve.wait_ge(s_xr[b], 16 * r + 16)
                dve.wait_ge(s_o, n + 1)
                then(v.tensor_tensor(z[:], Y.rearrange("p (t c) -> p t c", t=GT), xr[b][:], ALU.add))
                for t in range(GT):
                    i = own.mark(v.bn_stats(bst[:, t, :], z[:, t, :]))
                dve.wait_ge(s_dve, i)
                for t in range(GT):
                    i = v.bn_aggr(mv[:, t, :], bst[:, t, :])
                i.then_inc(s_z, 1)

            def norm(n, b, first=False):
                dve.wait_ge(s_lsd, n + 1)
                if not first:
                    dve.wait_ge(s_out, 16 * n)
                for t in range(GT):
                    i = v.tensor_scalar(xo[b][:, t, :], z[:, t, :], mv[:, t, 0:1], rsv[:, t:t + 1],
                                        ALU.subtract, ALU.mult)
                i.then_inc(s_xo, 1)

            def step(n, b, r, first, last):
                own.restart(dve)
                for m in range(2 * GT):
                    t, h = m // 2, m % 2
                    dve.wait_ge(s_ata, 8 * n + m + 1)
                    for q in (2 * h, 2 * h + 1):
                        d = at[m % 2][:, :, q % 2, 32 * q:32 * q + 64]
                        i = v.tensor_tensor(d, d, C["diag"].unsqueeze(1).broadcast_to([P, 4, 64]), ALU.mult)
                    i.then_inc(s_atd, 1)
                    if m == 0 and not first:
                        sums(n - 1, 1 - b, r - 1)
                    if m == 1:
                        spread(1, b)
                    if not last:
                        next_group(m, n + 1, 1 - b)
                    if m == 1 and not first:
                        norm(n - 1, 1 - b, first=isinstance(n, int) and n == 1)
                if not last:
                    dve.wait_ge(s_kd, n + 2)
                    spread(0, 1 - b)
                    state_mask(n + 1, 1 - b)
                dve.wait_ge(s_sd, n + 1)
                then(v.tensor_tensor(ya[:], X2, rs[:], ALU.mult))
                then(v.tensor_scalar(ya[:], ya[:], lnwb[:, 0:1], lnwb[:, 1:2], ALU.mult, ALU.add))
                v.tensor_tensor(yn[:], ya[:], gs[b][:], ALU.mult).then_inc(s_yn, 1)

            own.restart(dve)
            for slot in range(8):
                next_group(slot, 0, 0)
            dve.wait_ge(s_kd, 1)
            spread(0, 0)
            state_mask(0, 0)
            steps(dve, step)
            own.restart(dve)
            sums(NG - 1, 1, NG // 2 - 1)
            norm(NG - 1, 1)


NE, FC = 8, 4
RT = TOK // P


LT = (RT + NE - 1 + 7) // 8 * 8


def expert_tiles(topk):
    return topk * LT


def moe_stage(nc, sem, tag, x_in, x_out, xs_rows, ys_rows, w, consts, topk, act_fn, gate_bias):
    where, ncon = constant_columns()
    NT = expert_tiles(topk)
    ctx = ExitStack()
    with ctx:
        def sb(name, shape, dt=F32):
            return ctx.enter_context(nc.sbuf_tensor(f"{tag}_{name}", shape, dt))

        k = {"C": {}, "sem": sem, "tag": tag, "NT": NT, "topk": topk}
        con = sb("con", [P, ncon])
        k["con"] = con
        k["C"] = {n: con[:, a:b] for n, (a, b) in where.items()}
        k["X"] = sb("X", [P, RT, P])
        k["w1"] = sb("w1", [P, NE, FC * P + FC])
        k["w2"] = sb("w2", [P, NE, FC, P])
        k["b2"] = sb("b2", [P, NE, P])
        k["top"] = sb("top", [P, RT, 8])
        k["slot"] = [sb(f"slot{i}", [P, RT], U32) for i in range(topk)]
        k["expert"] = sb("expert", [1, NT], I32)
        k["y"] = [sb(f"y{i}", [P, RT, P]) for i in range(topk)]
        k["s_w"] = sem(f"{tag}_weights_in")
        moe_route(nc, k, x_in, xs_rows, w, consts, gate_bias)
        moe_experts(nc, k, xs_rows, ys_rows, act_fn)
        moe_combine(nc, k, ys_rows, x_out)


def moe_route(nc, k, x_in, xs_rows, w, consts, gate_bias):
    sem, tag, NT, topk, C, X, top, slot = (k[n] for n in ("sem", "tag", "NT", "topk", "C", "X", "top", "slot"))
    x_tiles = x_in.rearrange("(t p) c -> p t c", p=P)
    ctx = ExitStack()
    with ctx:
        def sb(name, shape, dt=F32):
            return ctx.enter_context(nc.sbuf_tensor(f"{tag}r_{name}", shape, dt))

        gw = sb("gw", [P, NE])
        gb = sb("gb", [P, NE])
        zero = sb("zero", [P, LT * P // 4])
        xT = [sb(f"xT{i}", [P, GTOK]) for i in range(2)]
        lg = sb("lg", [P, RT, NE])
        mx = sb("mx", [P, RT])
        pr = sb("pr", [P, RT, NE])
        idx = sb("idx", [P, RT, 8], U32)
        idf = sb("idf", [P, RT, 8])
        NL = topk * NE
        pick = sb("pick", [P, RT, NL])
        run = [sb(f"run{i}", [P, 16 + RT, NL]) for i in range(2)]
        over = sb("over", [P, NL, RT])
        base = [sb(f"base{i}", [P, topk, 4 + NE]) for i in range(2)]
        place = sb("place", [P, RT, NL])
        mine = [sb(f"mine{i}", [P, RT, NE]) for i in range(topk)]
        pf = [sb(f"pf{i}", [P, RT]) for i in range(topk)]
        le = [sb(f"le{i}", [1, LT, NE - 1]) for i in range(topk)]
        ef = sb("ef", [1, NT])
        B = [ctx.enter_context(nc.psum_tensor(f"{tag}r_bank{i}", [P, GTOK], F32))[:, :] for i in range(4)]

        def s(name):
            return sem(f"{tag}_{name}")

        s_w, s_c, s_set = k["s_w"], s("constants_in"), s("constants_set")
        s_x = [s(f"rows_in_{i}") for i in range(4)]
        s_zero, s_T, s_xT, s_lg, s_sh, s_pr = s("zeros_out"), s("transposed"), s("channel_major"), s("logits"), s("logits_shifted"), s("exps")
        s_pick, s_cnt, s_slot, s_sc, s_dve = s("picks"), s("counts"), s("slots"), s("scattered"), s("vector_steps")
        block = ctx.enter_context(nc.Block())
        NC = 16 * (2 + gate_bias)

        @block.sync
        def _(sp):
            loads = [(k["con"][:], consts), (gw[:], w["gate_w"])]
            if gate_bias:
                loads.append((gb[:], w["gate_b"].broadcast_to([P, NE])))
            for q in range(4):
                sp.dma_start(X[:, 8 * q:8 * q + 8, :], x_tiles[:, 8 * q:8 * q + 8, :]).then_inc(s_x[q], 16)
                if q == 0:
                    for dst, src in loads:
                        sp.dma_start(dst, src).then_inc(s_c, 16)
            sp.wait_ge(s_set, 3)
            for rows in xs_rows:
                flat = rows.rearrange("(p j) c -> p (j c)", p=P)
                for q in range(4):
                    n = LT * P // 4
                    sp.dma_start(flat[:, q * n:(q + 1) * n], zero[:]).then_inc(s_zero, 16)
            for e in range(NE):
                sp.dma_start(k["w1"][:, e, 0:FC * P], w["w1"][:, e].rearrange("p f c -> p (f c)")).then_inc(s_w, 16)
                sp.dma_start(k["w2"][:, e], w["w2"][:, e]).then_inc(s_w, 16)
            sp.dma_start(k["w1"][:, :, FC * P:], w["b1"]).then_inc(s_w, 16)
            sp.dma_start(k["b2"][:].rearrange("p e c -> p (e c)"),
                         w["b2"].rearrange("e c -> (e c)").unsqueeze(0).broadcast_to([P, NE * P])).then_inc(s_w, 16)

        @block.gpsimd
        def _(pool):
            nc.gpsimd.memset(zero[:], 0.0).then_inc(s_set, 1)
            for i in range(2):
                nc.gpsimd.memset(run[i][:, 0:16], 0.0).then_inc(s_set, 1)
            for i in range(2):
                nc.gpsimd.memset(base[i][:, :, 0:4], 0.0).then_inc(s_set, 1)
            pool.wait_ge(s_zero, 64 * topk)
            pool.wait_ge(s_slot, 1)
            for t in range(RT):
                nc.gpsimd.indirect_dma_start(xs_rows[0], bass.IndirectOffsetOnAxis(ap=slot[0][:, t:t + 1], axis=0),
                                             X[:, t, :], None).then_inc(s_sc, 16)
            pool.wait_ge(s_sc, 16 * RT)

        @block.tensor
        def _(pe):
            mm = nc.tensor.matmul
            pe.wait_ge(s_c, NC)

            def logits(g):
                pe.wait_ge(s_xT, g + 1)
                for t in range(GT):
                    c = (g * GT + t) * NE
                    i = mm(B[2][:, c:c + NE], xT[g % 2][:, t * P:(t + 1) * P], gw[:], start=True, stop=True)
                return i

            for g in range(NG):
                if g % 2 == 0:
                    pe.wait_ge(s_x[g // 2], 16)
                for t in range(GT):
                    i = nc.tensor.transpose(B[g % 2][:, t * P:(t + 1) * P], X[:, g * GT + t, :], C["ident"])
                i.then_inc(s_T, 1)
                if g:
                    logits(g - 1).then_inc(s_lg, 1)
            logits(NG - 1).then_inc(s_lg, 1)
            pe.wait_ge(s_pick, topk)
            picks = pick[:].rearrange("p t e -> p (t e)")
            mm(B[3][:, 0:RT * NL], C["before"], picks, start=True, stop=True)
            mm(B[0][:, 0:RT * NL], C["ones"], picks, start=True, stop=True).then_inc(s_cnt, 1)

        @block.scalar
        def _(act):
            op = nc.scalar.activation
            for g in range(NG):
                act.wait_ge(s_T, g + 1)
                if g >= 2:
                    act.wait_ge(s_lg, g - 1)
                op(xT[g % 2][:], B[g % 2], ACT.Copy).then_inc(s_xT, 1)
            act.wait_ge(s_sh, 1)
            op(pr[:], lg[:], ACT.Exp).then_inc(s_pr, 1)

        @block.vector
        def _(dve):
            v = nc.vector
            own = Steps(s_dve)

            def then(ins):
                dve.wait_ge(s_dve, own.mark(ins))

            per_tile = lambda a: a.unsqueeze(2).broadcast_to([P, RT, NE])
            dve.wait_ge(s_c, NC)
            dve.wait_ge(s_set, 5)
            dve.wait_ge(s_lg, NG)
            raw = B[2][:, 0:RT * NE].rearrange("p (t e) -> p t e", t=RT)
            if gate_bias:
                then(v.tensor_tensor(lg[:], raw, gb[:].unsqueeze(1).broadcast_to([P, RT, NE]), ALU.add))
            else:
                then(v.tensor_copy(lg[:], raw))
            then(v.tensor_reduce(mx[:], lg[:], AX_X, ALU.max))
            v.tensor_tensor(lg[:], lg[:], per_tile(mx[:]), ALU.subtract).then_inc(s_sh, 1)
            dve.wait_ge(s_pr, 1)
            then(v.tensor_reduce(mx[:], pr[:], AX_X, ALU.add))
            then(v.reciprocal(mx[:], mx[:]))
            then(v.tensor_tensor(pr[:], pr[:], per_tile(mx[:]), ALU.mult))
            for t in range(RT):
                i = own.mark(v.max(top[:, t, :], pr[:, t, :]))
            dve.wait_ge(s_dve, i)
            for t in range(RT):
                i = own.mark(v.max_index(idx[:, t, :], top[:, t, :], pr[:, t, :]))
            dve.wait_ge(s_dve, i)
            then(v.tensor_copy(idf[:], idx[:]))
            experts = C["experts"].unsqueeze(1).broadcast_to([P, RT, NE])
            for i in range(topk):
                v.tensor_tensor(pick[:, :, i * NE:(i + 1) * NE], experts, per_tile(idf[:, :, i]), ALU.is_equal
                                ).then_inc(s_pick, 1)
            by_pair = lambda a: a.rearrange("p (t e) -> p t e", t=RT)
            dve.wait_ge(s_cnt, 1)
            then(v.tensor_copy(run[0][:, 16:], by_pair(B[0][:, 0:RT * NL])))
            for q in range(5):
                a, b, d = run[q % 2], run[1 - q % 2], 1 << q
                then(v.tensor_tensor(b[:, 16:], a[:, 16:], a[:, 16 - d:16 + RT - d], ALU.add))
            sums = run[1]
            total = sums[:, 16 + RT - 1, :].unsqueeze(2).broadcast_to([P, NL, RT])
            then(v.tensor_tensor(over[:], total, C["limits"].unsqueeze(1).broadcast_to([P, NL, RT]), ALU.is_gt))
            then(v.tensor_reduce(base[0][:, :, 4:], over[:].rearrange("p (k e) t -> p k e t", e=NE), AX_X, ALU.add))
            for q in range(3):
                a, b, d = base[q % 2], base[1 - q % 2], 1 << q
                then(v.tensor_tensor(b[:, :, 4:], a[:, :, 4:], a[:, :, 4 - d:4 + NE - d], ALU.add))
            for i in range(topk):
                own_pairs = slice(i * NE, (i + 1) * NE)
                starts = base[1][:, i, 3:3 + NE]
                at = own.mark(v.scalar_tensor_tensor(place[:, :, own_pairs], starts.unsqueeze(1).broadcast_to([P, RT, NE]),
                                                     float(P), sums[:, 15:15 + RT, own_pairs], ALU.mult, ALU.add))
            dve.wait_ge(s_dve, at)
            then(v.tensor_tensor(place[:], place[:], by_pair(B[3][:, 0:RT * NL]), ALU.add))
            for i in range(topk):
                own_pairs = slice(i * NE, (i + 1) * NE)
                then(v.tensor_tensor(mine[i][:], pick[:, :, own_pairs], place[:, :, own_pairs], ALU.mult))
                then(v.tensor_reduce(pf[i][:], mine[i][:], AX_X, ALU.add))
                v.tensor_copy(slot[i][:], pf[i][:]).then_inc(s_slot, 1)
            for i in range(topk):
                then(v.tensor_tensor(le[i][:], base[1][0:1, i, 4:4 + NE - 1].unsqueeze(1).broadcast_to([1, LT, NE - 1]),
                                     C["tiles"][0:1, 0:LT].unsqueeze(2).broadcast_to([1, LT, NE - 1]), ALU.is_le))
                then(v.tensor_reduce(ef[:, i * LT:(i + 1) * LT], le[i][:], AX_X, ALU.add))
            v.tensor_copy(k["expert"][:], ef[:]).then_inc(s_slot, 1)
            dve.wait_ge(s_slot, topk + 1)


def moe_experts(nc, k, xs_rows, ys_rows, act_fn):
    sem, tag, NT, C, w1, w2, b2, expert = (k[n] for n in ("sem", "tag", "NT", "C", "w1", "w2", "b2", "expert"))
    NI, NI1 = NT // 8, LT // 8
    topk, X, slot, y = (k[n] for n in ("topk", "X", "slot", "y"))
    xs_tiles, ys_tiles = [[rows.rearrange("(g h t p) c -> g h p t c", h=2, t=GT, p=P) for rows in lists]
                          for lists in (xs_rows, ys_rows)]
    ctx = ExitStack()
    with ctx:
        def sb(name, shape, dt=F32):
            return ctx.enter_context(nc.sbuf_tensor(f"{tag}e_{name}", shape, dt))

        xs = [sb(f"xs{i}", [P, GT, P]) for i in range(2)]
        ys = [sb(f"ys{i}", [P, GT, P]) for i in range(2)]
        xT = [sb(f"xT{i}", [P, P]) for i in range(2)]
        cur = [sb(f"cur{i}", [P, FC * P + FC]) for i in range(2)]
        h = [sb(f"h{i}", [P, FC, P]) for i in range(2)]
        BT, BU, BY = [[ctx.enter_context(nc.psum_tensor(f"{tag}e_{n}{i}", [P, GTOK], F32))[:, :] for i in range(2)]
                      for n in ("turned", "up", "down")]

        def s(name):
            return sem(f"{tag}_{name}")

        s_in, s_st = [s("sorted_in_0"), s("sorted_in_1")], [s("results_out_0"), s("results_out_1")]
        s_T, s_xT, s_cur, s_up, s_h, s_dn, s_y = s("tile_transposed"), s("tile_channel_major"), s("tile_weights"), s("up"), s("hidden"), s("down"), s("results")
        s_sc, s_y0 = s("second_choices_scattered"), s("first_results_in")
        s_w = k["s_w"]
        NW = 16 * (2 * NE + 2)
        block = ctx.enter_context(nc.Block())

        def after(eng, semaphore, count):
            if not isinstance(count, int) or count > 0:
                eng.wait_ge(semaphore, count)

        def rounds(eng, body):
            body(0, False, 0)
            for i in range(topk):
                with eng.Fori(max(i * NI1, 1), (i + 1) * NI1 - 1) as g:
                    body(g, False, i)
                body((i + 1) * NI1 - 1, i == topk - 1, i)

        @block.gpsimd
        def _(pool):
            if topk == 2:
                for t in range(RT):
                    nc.gpsimd.indirect_dma_start(xs_rows[1], bass.IndirectOffsetOnAxis(ap=slot[1][:, t:t + 1], axis=0),
                                                 X[:, t, :], None).then_inc(s_sc, 16)
                for b in range(2):
                    pool.wait_ge(s_st[b], 16 * NI1)
                for t in range(RT):
                    nc.gpsimd.indirect_dma_start(y[0][:, t, :], None, ys_rows[0],
                                                 bass.IndirectOffsetOnAxis(ap=slot[0][:, t:t + 1], axis=0)
                                                 ).then_inc(s_y0, 16)
                pool.wait_ge(s_y0, 16 * RT)

        @block.sync
        def _(sp):
            one = lambda rows, g, b: rows[bass.ds(g, 1), b].rearrange("g p t c -> (g p) t c")

            def body(g, last, i):
                for b in range(2):
                    done = g * 8 + 4 * b + 4
                    if not last:
                        ends = isinstance(g, int) and g == NI1 * (i + 1) - 1
                        if ends and b == 0:
                            sp.wait_ge(s_sc, 16 * RT)
                        sp.wait_ge(s_T, done)
                        rows = one(xs_tiles[i + 1], 0, b) if ends else one(xs_tiles[i], g + 1 - i * NI1, b)
                        sp.dma_start(xs[b][:], rows).then_inc(s_in[b], 16)
                    sp.wait_ge(s_y, done)
                    sp.dma_start(one(ys_tiles[i], g - i * NI1, b), ys[b][:]).then_inc(s_st[b], 16)

            for b in range(2):
                sp.dma_start(xs[b][:], one(xs_tiles[0], 0, b)).then_inc(s_in[b], 16)
            rounds(sp, body)
            for b in range(2):
                sp.wait_ge(s_st[b], 16 * NI)

        @block.tensor
        def _(pe):
            mm = nc.tensor.matmul

            def turn(g, u):
                if u % 4 == 0:
                    pe.wait_ge(s_in[u // 4], g * 16 + 16)
                nc.tensor.transpose(BT[u % 2][:, 0:P], xs[u // 4][:, u % 4, :], C["ident"]).then_inc(s_T, 1)

            def down(j, u, e):
                pe.wait_ge(s_h, j + 1)
                after(pe, s_y, j - 1)
                for f in range(FC):
                    i = mm(BY[u % 2][:, 0:P], h[u % 2][:, f, :], w2[:, bass.ds(e, 1), f, :].rearrange("p e c -> p (e c)"),
                           start=(f == 0), stop=(f == FC - 1))
                i.then_inc(s_dn, 1)

            pe.wait_ge(s_w, NW)
            turn(0, 0)

            def body(g, last, i):
                for u in range(8):
                    j = g * 8 + u
                    if u < 7:
                        turn(g, u + 1)
                    elif not last:
                        turn(g + 1, 0)
                    pe.wait_ge(s_cur, j + 1)
                    pe.wait_ge(s_xT, j + 1)
                    after(pe, s_h, j - 1)
                    for f in range(FC):
                        i = mm(BU[u % 2][:, f * P:(f + 1) * P], cur[u % 2][:, f * P:(f + 1) * P], xT[u % 2][:],
                               start=True, stop=True)
                    i.then_inc(s_up, 1)
                    if u or not isinstance(j, int) or j:
                        e = pe.value_load(expert[0:1, bass.ds(j - 1, 1)], min_val=0, max_val=NE - 1)
                        down(j - 1, (u - 1) % 8, e)

            rounds(pe, body)
            e = pe.value_load(expert[0:1, NT - 1:NT], min_val=0, max_val=NE - 1)
            down(NT - 1, 7, e)

        @block.scalar
        def _(act):
            op = nc.scalar.activation

            def body(g, last, i):
                for u in range(8):
                    j = g * 8 + u
                    act.wait_ge(s_up, j + 1)
                    after(act, s_dn, j - 1)
                    for f in range(FC):
                        i = op(h[u % 2][:, f, :], BU[u % 2][:, f * P:(f + 1) * P], act_fn,
                               bias=cur[u % 2][:, FC * P + f:FC * P + f + 1])
                    i.then_inc(s_h, 1)

            rounds(act, body)

        @block.vector
        def _(dve):
            v = nc.vector

            def fetch(j, u):
                e = dve.value_load(expert[0:1, bass.ds(j, 1)], min_val=0, max_val=NE - 1)
                after(dve, s_h, j - 1)
                v.tensor_scalar(cur[u % 2][:], w1[:, bass.ds(e, 1), :].rearrange("p e c -> p (e c)"),
                                1.0, None, ALU.mult).then_inc(s_cur, 1)

            def copy_x(j, u):
                dve.wait_ge(s_T, j + 1)
                v.tensor_copy(xT[u % 2][:], BT[u % 2][:, 0:P]).then_inc(s_xT, 1)

            def result(j, u, g):
                e = dve.value_load(expert[0:1, bass.ds(j, 1)], min_val=0, max_val=NE - 1)
                dve.wait_ge(s_dn, j + 1)
                if u % 4 == 0:
                    after(dve, s_st[u // 4], g * 16)
                v.tensor_tensor(ys[u // 4][:, u % 4, :], BY[u % 2][:, 0:P],
                                b2[:, bass.ds(e, 1), :].rearrange("p e c -> p (e c)"), ALU.add).then_inc(s_y, 1)

            dve.wait_ge(s_w, NW)
            fetch(0, 0)
            copy_x(0, 0)

            def body(g, last, i):
                for u in range(8):
                    j = g * 8 + u
                    if u < 7 or not last:
                        fetch(j + 1, (u + 1) % 8)
                        copy_x(j + 1, (u + 1) % 8)
                    if u:
                        result(j - 1, u - 1, g)
                    elif not isinstance(g, int) or g:
                        result(j - 1, 7, g - 1)

            rounds(dve, body)
            result(NT - 1, 7, NI - 1)


def moe_combine(nc, k, ys_rows, x_out):
    sem, tag, topk, X, top, slot = (k[n] for n in ("sem", "tag", "topk", "X", "top", "slot"))
    o_tiles = x_out.rearrange("(g t p) c -> g p t c", t=GT, p=P)
    ctx = ExitStack()
    with ctx:
        def sb(name, shape, dt=F32):
            return ctx.enter_context(nc.sbuf_tensor(f"{tag}c_{name}", shape, dt))

        eps = sb("eps", [P, 1])
        y = k["y"]
        bst = sb("bst", [P, RT, 6])
        mv = sb("mv", [P, RT, 2])
        sdv = sb("sdv", [P, RT])
        rsv = sb("rsv", [P, RT])

        def s(name):
            return sem(f"{tag}_{name}")

        s_set, s_y = s("eps_set"), [s(f"results_in_{g}") for g in range(NG)]
        s_z, s_sd, s_o, s_out, s_dve = s("sum_stats"), s("sum_deviation"), s("rows_ready"), s("rows_out"), s("combine_steps")
        block = ctx.enter_context(nc.Block())

        @block.gpsimd
        def _(pool):
            nc.gpsimd.memset(eps[:], LN_EPS).then_inc(s_set, 1)
            for g in range(NG):
                for t in range(g * GT, g * GT + GT):
                    nc.gpsimd.indirect_dma_start(y[topk - 1][:, t, :], None, ys_rows[topk - 1],
                                                 bass.IndirectOffsetOnAxis(ap=slot[topk - 1][:, t:t + 1], axis=0)
                                                 ).then_inc(s_y[g], 16)

        @block.vector
        def _(dve):
            v = nc.vector
            own = Steps(s_dve)

            def finish(g):
                dve.wait_ge(s_sd, g + 1)
                r = slice(g * GT, g * GT + GT)
                dve.wait_ge(s_dve, own.mark(v.reciprocal(rsv[:, r], sdv[:, r])))
                for t in range(g * GT, g * GT + GT):
                    i = v.tensor_scalar(X[:, t, :], X[:, t, :], mv[:, t, 0:1], rsv[:, t:t + 1], ALU.subtract, ALU.mult)
                i.then_inc(s_o, 1)

            for g in range(NG):
                tiles = range(g * GT, g * GT + GT)
                dve.wait_ge(s_y[g], 16 * GT)
                for i in range(topk):
                    for t in tiles:
                        at = own.mark(v.scalar_tensor_tensor(X[:, t, :], y[i][:, t, :], top[:, t, i:i + 1], X[:, t, :],
                                                             ALU.mult, ALU.add))
                    dve.wait_ge(s_dve, at)
                for t in tiles:
                    at = own.mark(v.bn_stats(bst[:, t, :], X[:, t, :]))
                dve.wait_ge(s_dve, at)
                for t in tiles:
                    i = v.bn_aggr(mv[:, t, :], bst[:, t, :])
                i.then_inc(s_z, 1)
                if g:
                    finish(g - 1)
            finish(NG - 1)

        @block.scalar
        def _(act):
            act.wait_ge(s_set, 1)
            for g in range(NG):
                r = slice(g * GT, g * GT + GT)
                act.wait_ge(s_z, g + 1)
                nc.scalar.activation(sdv[:, r], mv[:, r, 1], ACT.Sqrt, bias=eps[:, 0:1]).then_inc(s_sd, 1)

        @block.sync
        def _(sp):
            for g in range(NG):
                sp.wait_ge(s_o, g + 1)
                sp.dma_start(o_tiles[g], X[:, g * GT:g * GT + GT, :]).then_inc(s_out, 16)
            sp.wait_ge(s_out, 16 * NG)


NCH = SEQ // 32


def delta_project(nc, sem, keep, x_in, v_rows, s_rows, w, consts):
    where, ncon = constant_columns()
    x_tiles = x_in.rearrange("(g t p) c -> g p t c", t=GT, p=P)
    v_tiles = v_rows.rearrange("(g t p) c -> g p t c", t=GT, p=P)
    s_tiles = s_rows.rearrange("(g t p) c -> g p t c", t=GT, p=P)
    ctx = ExitStack()
    with ctx:
        def sb(name, shape, dt=F32):
            return ctx.enter_context(nc.sbuf_tensor("c_" + name, shape, dt))

        con = sb("con", [P, ncon])
        C = {k: con[:, a:b] for k, (a, b) in where.items()}
        wqkv = sb("wqkv", [P, 3, P])
        wb = sb("wb", [P, P])
        taps = sb("taps", [P, 3, 4])
        fir = sb("fir", [P, 3])
        eps = sb("eps", [P, 1])
        xt = [sb(f"xt{i}", [P, GT, P]) for i in range(2)]
        xT = sb("xT", [P, GTOK])
        pad = [sb(f"pad{i}", [P, GSEQ, SEQ + 3]) for i in range(3)]
        cv = [[sb(f"cv{i}{j}", [P, GTOK]) for j in range(2)] for i in range(3)]
        qk = [sb(f"qk{i}", [P, GTOK]) for i in range(2)]
        vs = sb("vs", [P, GSEQ, SEQ + 2])
        beta = sb("beta", [P, GTOK])
        sq = [sb(f"sq{i}", [P, GTOK]) for i in range(2)]
        sd = [sb(f"sd{i}", [P, GTOK]) for i in range(2)]
        kn = sb("kn", [P, GTOK])
        kq = sb("kq", [P, GTOK // 32, 2, 32])
        vb = sb("vb", [P, GTOK])
        kbs = sb("kbs", [P, GTOK])
        hs = [sb(f"hs{i}", [P, GTOK]) for i in range(3)]
        fa = [sb(f"fa{i}", [P, GTOK]) for i in range(2)]
        vt = sb("vt", [P, GT, P])
        ft = sb("ft", [P, GT, P])
        B = [ctx.enter_context(nc.psum_tensor(f"c_bank{i}", [P, GTOK], F32))[:, :] for i in range(8)]

        def s(name):
            return sem("delta_" + name)

        s_w, s_set, s_x, s_out = s("weights_in"), s("constants_set"), [s("rows_in_0"), s("rows_in_1")], s("rows_out")
        s_T, s_xT, s_p, s_pad, s_beta = s("transposed"), s("channel_major"), s("projected"), s("padded"), s("beta")
        s_cv, s_act, s_sq, s_ss, s_sd = s("convolved"), s("silu"), s("squared"), s("square_sums"), s("norms")
        s_n, s_kq, s_hs, s_keep = s("normalized"), s("score_operands"), s("head_rows"), s("kept")
        s_sc, s_m, s_fir, s_tp, s_rows = s("scores"), s("scores_masked"), s("short_fir"), s("value_rows"), s("value_rows_copied")
        s_ln, s_dve = s("logarithms"), s("vector_steps")

        block = ctx.enter_context(nc.Block())
        one = lambda rows, n: rows[bass.ds(n, 1)].rearrange("g p t c -> (g p) t c")

        def steps(eng, step):
            step(0, 0, 0, True, False)
            with eng.Fori(0, NG // 2 - 1) as it:
                step(it * 2 + 1, 1, it + 1, False, False)
                step(it * 2 + 2, 0, it + 1, False, False)
            step(NG - 1, 1, NG // 2, False, True)

        @block.sync
        def _(sp):
            for b in range(2):
                sp.dma_start(xt[b][:], one(x_tiles, b)).then_inc(s_x[b], 16)
            for dst, src in [(con[:], consts), (wqkv[:], w["wqkv"]), (wb[:], w["wb"]), (taps[:], w["taps"]),
                             (fir[:], w["firs"])]:
                sp.dma_start(dst, src).then_inc(s_w, 16)

            def group(n, b, more):
                if more:
                    sp.wait_ge(s_T, n + 1)
                    sp.dma_start(xt[b][:], one(x_tiles, n + 2)).then_inc(s_x[b], 16)
                sp.wait_ge(s_rows, 2 * n + 2)
                sp.dma_start(one(v_tiles, n), vt[:]).then_inc(s_out, 16)
                sp.dma_start(one(s_tiles, n), ft[:]).then_inc(s_out, 16)

            with sp.Fori(0, NG // 2 - 1) as it:
                for b in range(2):
                    group(it * 2 + b, b, True)
            group(NG - 2, 0, False)
            group(NG - 1, 1, False)
            sp.wait_ge(s_out, 32 * NG)

        @block.tensor
        def _(pe):
            mm = nc.tensor.matmul
            pe.wait_ge(s_w, 80)

            def project(m, b, r, first=False):
                pe.wait_ge(s_x[b], 16 * r + 16)
                for t in range(GT):
                    i = nc.tensor.transpose(B[0][:, t * P:(t + 1) * P], xt[b][:, t, :], C["ident"])
                i.then_inc(s_T, 1)
                pe.wait_ge(s_xT, m + 1)
                if not first:
                    pe.wait_ge(s_beta, m)
                for k in range(3):
                    mm(B[1 + k], wqkv[:, k, :], xT[:], start=True, stop=True).then_inc(s_p, 1)
                mm(B[4], wb[:], xT[:], start=True, stop=True).then_inc(s_p, 1)

            def step(n, b, r, first, last):
                if not first:
                    pe.wait_ge(s_m, 2 * n)
                for k in range(2):
                    pe.wait_ge(s_sq, 2 * n + k + 1)
                    mm(B[5 + k], C["same32"], sq[k][:], start=True, stop=True).then_inc(s_ss, 1)
                if not first:
                    pe.wait_ge(s_rows, 2 * n)
                for t in range(GT):
                    o = (t % 2) * P + 2
                    i = nc.tensor.transpose(B[7][:, t * P:(t + 1) * P], vs[:, t // 2, o:o + P], C["ident"])
                i.then_inc(s_tp, 1)
                if not last:
                    project(n + 1, 1 - b, r)
                pe.wait_ge(s_w, 80)
                pe.wait_ge(s_kq, n + 1)
                for c in range(GTOK // 32):
                    for h in range(4):
                        rows = slice(32 * h, 32 * h + 32)
                        i = mm(B[5 + c // NCH][rows, (c % NCH) * 64:(c % NCH) * 64 + 64], kn[rows, 32 * c:32 * c + 32],
                               kq[rows, c].rearrange("p k c -> p (k c)"), start=True, stop=True,
                               skip_group_check=True)
                    if c % NCH == NCH - 1:
                        i.then_inc(s_sc, 1)
                pe.wait_ge(s_fir, n + 1)
                pe.wait_ge(s_rows, 2 * n + 1)
                for t in range(GT):
                    i = nc.tensor.transpose(B[7][:, t * P:(t + 1) * P], fa[0][:, t * P:(t + 1) * P], C["ident"])
                i.then_inc(s_tp, 1)

            project(0, 0, 0, first=True)
            steps(pe, step)

        @block.gpsimd
        def _(pool):
            nc.gpsimd.memset(eps[:], 1e-6).then_inc(s_set, 1)
            for k in range(3):
                nc.gpsimd.memset(pad[k][:, :, 0:3], 0.0).then_inc(s_set, 1)
            nc.gpsimd.memset(vs[:, :, 0:2], 0.0).then_inc(s_set, 1)
            with pool.Fori(0, NG) as n:
                seqs = bass.ds(n * GSEQ, GSEQ)
                view = lambda a: a.rearrange("p (s n c) -> p s n c", s=GSEQ, c=32)
                place = lambda a: a[:, :, seqs, :].rearrange("p n s c -> p s n c")
                pool.wait_ge(s_kq, n + 1)
                nc.gpsimd.tensor_copy(place(keep["q"]), kq[:, :, 1, :].rearrange("p (s n) c -> p s n c", s=GSEQ)
                                      ).then_inc(s_keep, 1)
                for k, name in enumerate(("k", "kb", "vb")):
                    pool.wait_ge(s_hs, 3 * n + k + 1)
                    nc.gpsimd.tensor_copy(place(keep[name]), view(hs[k][:])).then_inc(s_keep, 1)

        @block.scalar
        def _(act):
            op = nc.scalar.activation
            seqs = lambda a: a.rearrange("p (s t) -> p s t", s=GSEQ)
            act.wait_ge(s_w, 80)
            act.wait_ge(s_set, 5)

            def copy_x(m):
                act.wait_ge(s_T, m + 1)
                op(xT[:], B[0], ACT.Copy).then_inc(s_xT, 1)

            def copy_projected(m):
                for k in range(3):
                    act.wait_ge(s_p, 4 * m + k + 1)
                    op(pad[k][:, :, 3:SEQ + 3], seqs(B[1 + k]), ACT.Copy).then_inc(s_pad, 1)

            def step_sizes(m):
                act.wait_ge(s_p, 4 * m + 4)
                op(beta[:], B[4], ACT.Sigmoid).then_inc(s_beta, 1)

            def step(n, b, r, first, last):
                for k in range(3):
                    act.wait_ge(s_cv, 3 * n + k + 1)
                    op(seqs(qk[k][:]) if k < 2 else vs[:, :, 2:SEQ + 2], seqs(cv[k][1][:]), ACT.Silu).then_inc(s_act, 1)
                for k in range(2):
                    act.wait_ge(s_act, 3 * n + k + 1)
                    op(sq[k][:], qk[k][:], ACT.Square).then_inc(s_sq, 1)
                for k in range(2):
                    act.wait_ge(s_ss, 2 * n + k + 1)
                    op(sq[k][:], B[5 + k], ACT.Ln, bias=eps[:, 0:1]).then_inc(s_ln, 1)
                for k in range(2):
                    act.wait_ge(s_ln, 2 * n + k + 1)
                    op(sd[k][:], sq[k][:], ACT.Exp, scale=-0.5).then_inc(s_sd, 1)
                if not last:
                    copy_x(n + 1)
                if not first:
                    act.wait_ge(s_out, 32 * n)
                act.wait_ge(s_tp, 2 * n + 1)
                op(vt[:].rearrange("p t c -> p (t c)"), B[7], ACT.Copy).then_inc(s_rows, 1)
                if not last:
                    copy_projected(n + 1)
                    act.wait_ge(s_kq, n + 1)
                    step_sizes(n + 1)
                act.wait_ge(s_tp, 2 * n + 2)
                op(ft[:].rearrange("p t c -> p (t c)"), B[7], ACT.Copy).then_inc(s_rows, 1)

            copy_x(0)
            copy_projected(0)
            step_sizes(0)
            steps(act, step)

        @block.vector
        def _(dve):
            v = nc.vector
            own = Steps(s_dve)
            seqs = lambda a: a.rearrange("p (s t) -> p s t", s=GSEQ)
            chunks = lambda a: a.rearrange("p (c j) -> p c j", j=32)
            dve.wait_ge(s_w, 80)
            dve.wait_ge(s_set, 5)

            def then(ins):
                dve.wait_ge(s_dve, own.mark(ins))

            def masks(n):
                for q in range(GSEQ):
                    dve.wait_ge(s_sc, 2 * n + q + 1)
                    sc = B[5 + q].rearrange("p (n k c) -> p n k c", n=NCH, k=2)
                    for k, (mask, dst) in enumerate((("strict", "A"), ("incl", "attn"))):
                        out = keep[dst][:, :, bass.ds(n * GSEQ + q, 1), :].rearrange("p n s c -> p n (s c)")
                        i = v.tensor_tensor(out, sc[:, :, k, :], C[mask].unsqueeze(1).broadcast_to([P, NCH, 32]), ALU.mult)
                    i.then_inc(s_m, 1)

            def step(n, b, r, first, last):
                own.restart(dve)
                tap = [0, 0, 0]
                for k in range(3):
                    dve.wait_ge(s_pad, 3 * n + k + 1)
                    tap[k] = own.mark(v.tensor_scalar(seqs(cv[k][0][:]), pad[k][:, :, 0:SEQ], taps[:, k, 0:1], None, ALU.mult))
                for j in range(1, 4):
                    for k in range(3):
                        dve.wait_ge(s_dve, tap[k])
                        ins = v.scalar_tensor_tensor(seqs(cv[k][j % 2][:]), pad[k][:, :, j:SEQ + j], taps[:, k, j:j + 1],
                                                     seqs(cv[k][1 - j % 2][:]), ALU.mult, ALU.add)
                        if j < 3:
                            tap[k] = own.mark(ins)
                        else:
                            ins.then_inc(s_cv, 1)
                if not first:
                    masks(n - 1)
                dve.wait_ge(s_act, 3 * n + 3)
                if not first:
                    dve.wait_ge(s_tp, 2 * n)
                then(v.tensor_scalar(seqs(fa[0][:]), vs[:, :, 0:SEQ], fir[:, 0:1], None, ALU.mult))
                then(v.scalar_tensor_tensor(seqs(fa[1][:]), vs[:, :, 1:SEQ + 1], fir[:, 1:2], seqs(fa[0][:]), ALU.mult, ALU.add))
                v.scalar_tensor_tensor(seqs(fa[0][:]), vs[:, :, 2:SEQ + 2], fir[:, 2:3], seqs(fa[1][:]),
                                       ALU.mult, ALU.add).then_inc(s_fir, 1)
                dve.wait_ge(s_beta, n + 1)
                if not first:
                    dve.wait_ge(s_keep, 4 * n)
                i = own.mark(v.tensor_tensor(seqs(vb[:]), vs[:, :, 2:SEQ + 2], seqs(beta[:]), ALU.mult))
                dve.wait_ge(s_sd, 2 * n + 2)
                own_kn = own.mark(v.tensor_tensor(kn[:], qk[1][:], sd[1][:], ALU.mult))
                v.tensor_tensor(kq[:, :, 1, :], chunks(qk[0][:]), chunks(sd[0][:]), ALU.mult)
                dve.wait_ge(s_dve, own_kn)
                own_kb = own.mark(v.tensor_tensor(kbs[:], kn[:], beta[:], ALU.mult))
                v.tensor_tensor(kq[:, :, 0, :], chunks(kn[:]), chunks(beta[:]), ALU.mult).then_inc(s_kq, 1)
                dve.wait_ge(s_dve, own_kb)
                v.transpose(hs[0][:], kn[:]).then_inc(s_hs, 1)
                v.transpose(hs[1][:], kbs[:]).then_inc(s_hs, 1)
                v.transpose(hs[2][:], vb[:]).then_inc(s_hs, 1)

            steps(dve, step)
            masks(NG - 1)
            dve.wait_ge(s_keep, 4 * NG)


def delta_invert(nc, sem, keep, long_fir, v_rows, w, consts):
    where, ncon = constant_columns()
    NT, GC = TOK // P, 16
    v_tiles = v_rows.rearrange("(s two p) c -> two p s c", two=2, p=P)
    rev = w["firl"]
    span = rev.shape[1]
    ctx = ExitStack()
    with ctx:
        def sb(name, shape, dt=F32):
            return ctx.enter_context(nc.sbuf_tensor("i_" + name, shape, dt))

        con = sb("con", [P, ncon])
        C = {k: con[:, a:b] for k, (a, b) in where.items()}
        M = sb("M", [P, 32, 4, 32])
        tmp = [sb(f"tmp{i}", [P, 4096 // 8]) for i in range(2)]
        vtok = sb("vtok", [P, NT, P])
        toe = [sb(f"toe{i}", [P, GC, 192]) for i in range(2)]
        turned = [sb(f"turned{i}", [P, 512]) for i in range(2)]
        R = [ctx.enter_context(nc.psum_tensor(f"i_fir{i}", [P, 512], F32))[:, :] for i in range(4)]
        Q = [ctx.enter_context(nc.psum_tensor(f"i_bank{i}", [P, 512], F32))[:, :] for i in range(4)]

        def s(name):
            return sem("invert_" + name)

        s_flip, s_rev = s("flipped"), s("flipped_copied")
        s_w, s_v, s_toe = s("constants_in"), s("values_in"), [s("toeplitz_in_0"), s("toeplitz_in_1")]
        s_fir, s_fc, s_ft, s_long = s("fir"), s("fir_copied"), s("fir_transposed"), s("fir_rows")
        s_at, s_M, s_done, s_ut, s_U, s_dve = s("chunks_transposed"), s("chunk_rows"), s("inverted"), s("back_transposed"), s("kept"), s("vector_steps")
        block = ctx.enter_context(nc.Block())

        @block.sync
        def _(sp):
            sp.dma_start(con[:], consts).then_inc(s_w, 16)
            for half in range(2):
                sp.dma_start(vtok[:, 16 * half:16 * half + 16], v_tiles[1 - half]).then_inc(s_v, 16)
            for r in range(P // GC):
                if r >= 2:
                    sp.wait_ge(s_fir, r - 1)
                src = bass.AP(rev.tensor, rev.offset + r * GC * span, [[1, P], [span, GC], [1, 192]])
                sp.dma_start(toe[r % 2][:], src).then_inc(s_toe[r % 2], 16)

        @block.tensor
        def _(pe):
            mm = nc.tensor.matmul
            pe.wait_ge(s_w, 16)
            A = keep["A"][:].rearrange("p n s c -> p (n s) c")
            for c in range(32):
                k = c // 4
                if c % 4 == 0 and k >= 4:
                    pe.wait_ge(s_M, k - 3)
                i = nc.tensor.transpose(Q[k % 4][:, (c % 4) * P:(c % 4 + 1) * P], A[:, :, c], C["ident"])
                if c % 4 == 3:
                    i.then_inc(s_at, 1)
            pe.wait_ge(s_v, 32)
            for k in range(8):
                if k >= 4:
                    pe.wait_ge(s_rev, k - 3)
                mm(R[k % 4], C["flip"], vtok[:, 4 * k:4 * k + 4, :].rearrange("p t c -> p (t c)"),
                   start=True, stop=True).then_inc(s_flip, 1)
            pe.wait_ge(s_rev, 8)
            def turn(r):
                pe.wait_ge(s_fc, r + 1)
                if r >= 2:
                    pe.wait_ge(s_long, r - 1)
                for j in range(4):
                    i = nc.tensor.transpose(R[2 + r % 2][:, j * P:(j + 1) * P], turned[r % 2][:, j * P:(j + 1) * P],
                                            C["ident"])
                i.then_inc(s_ft, 1)

            for r in range(P // GC):
                pe.wait_ge(s_toe[r % 2], 16 * (r // 2) + 16)
                if r >= 2:
                    pe.wait_ge(s_fc, r - 1)
                for j in range(GC):
                    ch, rows, at = r * GC + j, 32 * (j % 4), (j // 4) * P
                    mm(R[r % 2][rows:rows + 32, at:at + P], vtok[:, :, ch], toe[r % 2][:, j, 0:P],
                       start=True, stop=False, skip_group_check=True)
                    i = mm(R[r % 2][rows:rows + 16, at:at + 64], vtok[0:64, 16:32, ch], toe[r % 2][0:64, j, P:192],
                           start=False, stop=True, skip_group_check=True)
                i.then_inc(s_fir, 1)
                if r:
                    turn(r - 1)
            turn(P // GC - 1)
            pe.wait_ge(s_done, 1)
            for c in range(32):
                k = c // 4
                pe.wait_ge(s_M, 8)
                if c % 4 == 0 and k >= 4:
                    pe.wait_ge(s_U, k - 3)
                i = nc.tensor.transpose(Q[k % 4][:, (c % 4) * P:(c % 4 + 1) * P],
                                        M[:, c].rearrange("p h j -> p (h j)"), C["ident"])
                if c % 4 == 3:
                    i.then_inc(s_ut, 1)

        @block.scalar
        def _(act):
            op = nc.scalar.activation
            for k in range(8):
                act.wait_ge(s_at, k + 1)
                op(M[:, 4 * k:4 * k + 4].rearrange("p c h j -> p (c h j)"), Q[k % 4], ACT.Copy).then_inc(s_M, 1)
            for k in range(8):
                act.wait_ge(s_flip, k + 1)
                op(vtok[:, 4 * k:4 * k + 4, :].rearrange("p t c -> p (t c)"), R[k % 4], ACT.Copy).then_inc(s_rev, 1)

            def rows(r):
                act.wait_ge(s_ft, r + 1)
                for half in range(2):
                    out = long_fir[:, :, GC * r:GC * r + GC].rearrange("p (s two) c -> p two c s", two=2)[:, 1 - half]
                    i = op(out, R[2 + r % 2].rearrange("p (c h s) -> p h c s", h=2, s=16)[:, half], ACT.Copy)
                i.then_inc(s_long, 1)

            for r in range(P // GC):
                act.wait_ge(s_fir, r + 1)
                if r >= 2:
                    act.wait_ge(s_ft, r - 1)
                op(turned[r % 2][:], R[r % 2], ACT.Copy).then_inc(s_fc, 1)
                if r:
                    rows(r - 1)
            rows(P // GC - 1)
            U = keep["A"][:].rearrange("p n s c -> p c (n s)")
            for k in range(8):
                act.wait_ge(s_ut, k + 1)
                op(U[:, 4 * k:4 * k + 4, :], Q[k % 4].rearrange("p (c m) -> p c m", c=4), ACT.Copy).then_inc(s_U, 1)

        @block.vector
        def _(dve):
            v = nc.vector
            dve.wait_ge(s_M, 8)
            done = [0, 0]
            own = Steps(s_dve)
            for j in range(1, 31):
                rows = 31 - j
                for pair in range(2):
                    hh = slice(2 * pair, 2 * pair + 2)
                    t = tmp[pair][:, 0:rows * 2 * j].rearrange("p (i h c) -> p i h c", h=2, c=j)
                    if done[pair]:
                        dve.wait_ge(s_dve, done[pair])
                    done[pair] = own.mark(v.tensor_tensor(t, M[:, j + 1:32, hh, j:j + 1].broadcast_to([P, rows, 2, j]),
                                                 M[:, j:j + 1, hh, 0:j].broadcast_to([P, rows, 2, j]), ALU.mult))
                for pair in range(2):
                    hh = slice(2 * pair, 2 * pair + 2)
                    out = M[:, j + 1:32, hh, 0:j]
                    t = tmp[pair][:, 0:rows * 2 * j].rearrange("p (i h c) -> p i h c", h=2, c=j)
                    dve.wait_ge(s_dve, done[pair])
                    done[pair] = own.mark(v.tensor_tensor(out, out, t, ALU.add))
            dve.wait_ge(s_dve, done[1])
            flat = M[:].rearrange("p i h c -> p (i h c)")
            for h in range(4):
                i = v.memset(flat[:, h * 32:h * 32 + 31 * 129 + 1:129], 1.0)
            i.then_inc(s_done, 1)


def delta_recur(nc, sem, keep, oT):
    ctx = ExitStack()
    with ctx:
        def sb(name, shape, dt=F32):
            return ctx.enter_context(nc.sbuf_tensor("r_" + name, shape, dt))

        names = ("A", "kb", "vb", "k", "q", "attn")
        step = [{k: sb(f"{k}{i}", [P, NSEQ, 32]) for k in names} for i in range(2)]
        wn = sb("wn", [P, NSEQ, 32])
        ua = sb("ua", [P, NSEQ, 32])
        S = sb("S", [P, NSEQ, 32])
        Bank = [ctx.enter_context(nc.psum_tensor(f"r_bank{i}", [P, NSEQ, 32], F32)) for i in range(6)]
        Bu, Bw, Bo, Bs = Bank[0:2], Bank[2], Bank[3:5], Bank[5]

        def s(name):
            return sem("recur_" + name)

        s_in, s_set, s_w, s_wn, s_u, s_ua = [s("chunks_in_0"), s("chunks_in_1")], s("state_zero"), s("w"), s("w_copied"), s("u"), s("u_copied")
        s_S, s_Sc, s_o, s_oc = s("state"), s("state_copied"), s("o"), s("o_copied")
        block = ctx.enter_context(nc.Block())

        @block.sync
        def _(sp):
            def load(n, b):
                for k in names:
                    sp.dma_start(step[b][k][:], keep[k][:, n]).then_inc(s_in[b], 16)

            load(0, 0)
            load(1, 1)
            for n in range(2, NCH):
                sp.wait_ge(s_o, n - 1)
                load(n, n % 2)

        @block.tensor
        def _(pe):
            mm = nc.tensor.matmul

            def heads(out, lhsT, rhs, first, last, fresh=False):
                for q in range(NSEQ):
                    for h in range(4):
                        r = slice(32 * h, 32 * h + 32)
                        i = mm(out[r, q, :], lhsT[r, q, :], rhs[r, q, :], start=fresh and q == 0, stop=last,
                               skip_group_check=True)
                return i

            pe.wait_ge(s_set, 2)
            count, loaded = pe.alloc_register("steps"), pe.alloc_register("loads")
            pe.reg_mov(count, 0)
            pe.reg_mov(loaded, 0)
            with pe.Fori(0, NCH // 2) as it:
                for b in range(2):
                    pe.reg_add(count, count, 1)
                    if b == 0:
                        pe.reg_add(loaded, loaded, 96)
                    c = step[b]
                    pe.wait_ge(s_set, 2)
                    pe.wait_ge(s_in[b], loaded)
                    heads(Bw, c["kb"], c["A"], True, True, fresh=True).then_inc(s_w, 1)
                    heads(Bu[b], c["A"], c["vb"], True, False, fresh=True)
                    pe.wait_ge(s_set, 2)
                    pe.wait_ge(s_wn, count)
                    pe.wait_ge(s_Sc, count)
                    heads(Bu[b], wn, S, False, True).then_inc(s_u, 1)
                    heads(Bo[b], S, c["q"], True, False, fresh=True)
                    pe.wait_ge(s_set, 2)
                    pe.wait_ge(s_ua, count)
                    heads(Bs, c["k"], ua, True, True).then_inc(s_S, 1)
                    heads(Bo[b], ua, c["attn"], False, True).then_inc(s_o, 1)

        @block.scalar
        def _(act):
            op = nc.scalar.activation
            with act.Fori(0, NCH // 2) as it:
                for b in range(2):
                    n = it * 2 + b
                    act.wait_ge(s_w, n + 1)
                    op(wn[:], Bw[:], ACT.Copy, scale=-1.0).then_inc(s_wn, 1)
                    act.wait_ge(s_o, n + 1)
                    op(oT[:, bass.ds(n, 1)].rearrange("p n s c -> p (n s) c"), Bo[b][:], ACT.Copy).then_inc(s_oc, 1)

        @block.vector
        def _(dve):
            v = nc.vector
            v.memset(Bs[:], 0.0).then_inc(s_set, 1)
            v.memset(S[:], 0.0).then_inc(s_set, 1)
            dve.wait_ge(s_set, 2)
            v.tensor_copy(S[:], Bs[:]).then_inc(s_Sc, 1)
            with dve.Fori(0, NCH // 2) as it:
                for b in range(2):
                    n = it * 2 + b
                    dve.wait_ge(s_u, n + 1)
                    v.tensor_copy(ua[:], Bu[b][:]).then_inc(s_ua, 1)
                    dve.wait_ge(s_S, n + 1)
                    v.tensor_copy(S[:], Bs[:]).then_inc(s_Sc, 1)


def gate_stage(nc, sem, oT, long_fir, v_rows, s_rows, x_in, x_out, w, consts):
    where, ncon = constant_columns()
    NH, NA = 4, 4
    TH = GT * NH
    x_tiles = x_in.rearrange("(g t p) c -> g p t c", t=GT, p=P)
    o_tiles = x_out.rearrange("(g t p) c -> g p t c", t=GT, p=P)
    v_tiles = v_rows.rearrange("(g t p) c -> g p t c", t=GT, p=P)
    s_tiles = s_rows.rearrange("(g t p) c -> g p t c", t=GT, p=P)
    ctx = ExitStack()
    with ctx:
        def sb(name, shape, dt=F32):
            return ctx.enter_context(nc.sbuf_tensor("g_" + name, shape, dt))

        con = sb("con", [P, ncon])
        C = {k: con[:, a:b] for k, (a, b) in where.items()}
        g1 = sb("g1", [P, P])
        g1s = sb("g1s", [P, P])
        gb1 = sb("gb1", [P, 1])
        gw2 = sb("gw2", [P, NA])
        wid = sb("wid", [P, P])
        wo = sb("wo", [P, P])
        onw = sb("onw", [P, 1])
        par = sb("par", [P, 3, NH * NA])
        crl = sb("crl", [P, NH])
        alpha = sb("alpha", [P, NH])
        itemp = sb("itemp", [P, NH * NA])
        floor = sb("floor", [P, NH, NA])
        keepf = sb("keepf", [P, NH])
        res = sb("res", [P, NH])
        eps = sb("eps", [P, 1])
        xt = [sb(f"xt{i}", [P, GT, P]) for i in range(2)]
        xo = [sb(f"xo{i}", [P, GT, P]) for i in range(2)]
        X = [sb(f"X{i}", [P, NA, TH, 32]) for i in range(2)]
        xc = sb("xc", [P, NA, TH, 32])
        mix = sb("mix", [P, NA, TH, 32])
        od = [sb(f"od{i}", [P, GSEQ, NCH, 32]) for i in range(2)]
        xT = [sb(f"xT{i}", [P, GTOK]) for i in range(2)]
        ss = sb("ss", [P, 4, NA * TH])
        stt = sb("stt", [P, TH, 32])
        sT = sb("sT", [P, GTOK])
        hid = sb("hid", [P, NH, GTOK])
        lg = sb("lg", [P, TH, NA])
        mx = sb("mx", [P, TH])
        pr = sb("pr", [P, TH, NA])
        o = sb("o", [P, TH, 32])
        o2 = sb("o2", [P, TH, 32])
        oc = sb("oc", [P, GTOK])
        bst = sb("bst", [P, GT, 6])
        mv = sb("mv", [P, GT, 2])
        sdv = sb("sdv", [P, GT])
        rsv = sb("rsv", [P, GT])
        B = [ctx.enter_context(nc.psum_tensor(f"g_bank{i}", [P, GTOK], F32))[:, :] for i in range(8)]

        def s(name):
            return sem("gate_" + name)

        s_w, s_set, s_x, s_out, s_xo = s("weights_in"), s("constants_set"), [s("rows_in_0"), s("rows_in_1")], s("rows_out"), s("rows_ready")
        s_pa, s_pv = s("parameters_scalar"), s("parameters_vector")
        s_Td = s("delta_transposed")
        s_od, s_T, s_xT, s_Xl, s_Xd = s("delta_copied"), s("transposed"), s("channel_major"), s("long_branch"), s("delta_branch")
        s_xc, s_sq, s_ms, s_l2, s_st = s("centered"), s("squared"), s("mean_squares"), s("norms"), s("stats")
        s_stp, s_sT, s_h, s_hid, s_lg = s("stats_transposed"), s("stats_copied"), s("hidden"), s("gelu"), s("logits")
        s_sh, s_ex, s_id, s_o, s_o2 = s("logits_shifted"), s("exps"), s("identity_branch"), s("mixed"), s("mixed_squared")
        s_rms, s_rsd, s_on, s_ot, s_oc = s("mixed_mean_square"), s("mixed_deviation"), s("normed"), s("normed_transposed"), s("normed_copied")
        s_pj, s_z, s_sd, s_dve = s("projected"), s("sum_stats"), s("sum_deviation"), s("vector_steps")
        block = ctx.enter_context(nc.Block())
        one = lambda rows, n: rows[bass.ds(n, 1)].rearrange("g p t c -> (g p) t c")
        NW = 16 * 13

        def steps(eng, step):
            step(0, 0, 0, True, False)
            with eng.Fori(0, NG // 2 - 2) as it:
                step(it * 2 + 1, 1, it + 1, False, False)
                step(it * 2 + 2, 0, it + 1, False, False)
            for n in range(NG - 3, NG):
                step(n, n % 2, (n + 1) // 2, False, n == NG - 1)

        @block.sync
        def _(sp):
            bc = lambda a, k: a.broadcast_to([P, k])
            flat = lambda a: a.rearrange("p (t h) c -> p t (h c)", t=GT)

            def load(n, b):
                sp.dma_start(xt[b][:], one(x_tiles, n)).then_inc(s_x[b], 16)
                sp.dma_start(flat(X[b][:, 0]), one(s_tiles, n)).then_inc(s_x[b], 16)
                sp.dma_start(flat(X[b][:, 3]), one(v_tiles, n)).then_inc(s_x[b], 16)

            load(0, 0)
            load(1, 1)
            loads = [(con[:], consts), (g1[:], w["g1"]), (g1s[:], w["g1s"]), (gb1[:], w["gb1"]), (gw2[:], w["gw2"]),
                     (wid[:], w["wid"]), (wo[:], w["wo"]), (onw[:], w["onw"]), (par[:, 0], bc(w["gb2"], 16)),
                     (par[:, 1], bc(w["log_temp"], 16)), (par[:, 2], bc(w["floor"], 16)), (crl[:], bc(w["crl"], 4)),
                     (alpha[:], bc(w["alpha"], 4))]
            for dst, src in loads:
                sp.dma_start(dst, src).then_inc(s_w, 16)

            def step(n, b, more=True, first=False):
                if more:
                    sp.wait_ge(s_o, n + 1)
                    load(n + 2, b)
                if not first:
                    sp.wait_ge(s_out, 16 * n)
                sp.wait_ge(s_xo, n + 1)
                sp.dma_start(one(o_tiles, n), xo[b][:]).then_inc(s_out, 16)

            step(0, 0, first=True)
            step(1, 1)
            with sp.Fori(1, NG // 2 - 1) as it:
                for b in range(2):
                    step(it * 2 + b, b)
            step(NG - 2, 0, more=False)
            step(NG - 1, 1, more=False)
            sp.wait_ge(s_out, 16 * NG)

        @block.gpsimd
        def _(pool):
            nc.gpsimd.memset(eps[:], LN_EPS).then_inc(s_set, 1)
            nc.gpsimd.memset(stt[:], 0.0).then_inc(s_set, 1)

            def delta_rows(n, b):
                nc.gpsimd.tensor_copy(od[b][:], oT[:, :, bass.ds(n * GSEQ, GSEQ), :].rearrange("p n s c -> p s n c")
                                      ).then_inc(s_od, 1)

            def long_rows(n, b):
                nc.gpsimd.tensor_copy(X[b][:, 1].rearrange("p (t h) c -> p t (h c)", t=GT),
                                      long_fir[:, bass.ds(n * GT, GT), :]).then_inc(s_Xl, 1)

            delta_rows(0, 0)
            long_rows(0, 0)
            delta_rows(1, 1)
            long_rows(1, 1)

            def step(n, b, r, first, last):
                if not isinstance(n, int) or n < NG - 2:
                    pool.wait_ge(s_Td, n + 1)
                    delta_rows(n + 2, b)
                    pool.wait_ge(s_o, n + 1)
                    long_rows(n + 2, b)

            steps(pool, step)

        @block.tensor
        def _(pe):
            mm = nc.tensor.matmul
            tiles = [slice(t * P, (t + 1) * P) for t in range(GT)]
            pe.wait_ge(s_w, NW)
            pe.wait_ge(s_pv, 1)

            def turn_residual(m, b, r, first=False):
                pe.wait_ge(s_x[b], 48 * r + 48)
                if not first:
                    pe.wait_ge(s_xT, m)
                for t in range(GT):
                    i = nc.tensor.transpose(B[0][:, tiles[t]], xt[b][:, t, :], C["ident"])
                i.then_inc(s_T, 1)

            def turn_delta(m, b, first=False):
                pe.wait_ge(s_od, m + 1)
                if not first:
                    pe.wait_ge(s_Xd, m)
                for t in range(GT):
                    i = nc.tensor.transpose(B[1][:, tiles[t]],
                                            od[b][:].rearrange("p s n c -> p (s n c)")[:, tiles[t]], C["ident"])
                i.then_inc(s_Td, 1)

            def hidden_state(m, b):
                pe.wait_ge(s_xT, m + 1)
                for h in range(NH):
                    mm(B[4 + h], g1[:], xT[b][:], start=True, stop=False)

            def hidden_statistics(m):
                pe.wait_ge(s_st, m + 1)
                stats = stt[:].rearrange("p (t h) k -> p t (h k)", t=GT)
                for t in range(GT):
                    i = nc.tensor.transpose(B[0][:, tiles[t]], stats[:, t, :], C["ident"])
                i.then_inc(s_stp, 1)
                pe.wait_ge(s_sT, m + 1)
                for h in range(NH):
                    rows = slice(32 * h, 32 * h + 32)
                    mm(B[4 + h], g1s[rows, :], sT[rows, :], start=False, stop=True).then_inc(s_h, 1)

            def step(n, b, r, first, last):
                for h in range(NH):
                    pe.wait_ge(s_hid, 4 * n + h + 1)
                    for t in range(GT):
                        i = mm(B[4][:, (t * NH + h) * NA:(t * NH + h + 1) * NA], hid[:, h, tiles[t]], gw2[:],
                               start=True, stop=True)
                i.then_inc(s_lg, 1)
                if not first:
                    pe.wait_ge(s_xo, n)
                for t in range(GT):
                    i = mm(B[2][:, tiles[t]], xT[b][:, tiles[t]], wid[:], start=True, stop=True)
                i.then_inc(s_id, 1)
                if not last:
                    turn_residual(n + 1, 1 - b, r)
                if not isinstance(n, int) or n < NG - 2:
                    turn_delta(n + 2, b)
                if not last:
                    pe.wait_ge(s_sh, n + 1)
                    hidden_state(n + 1, 1 - b)
                pe.wait_ge(s_o, n + 1)
                for t in range(GT):
                    mm(B[2][:, tiles[t]], xT[b][:, tiles[t]], C["ident"], start=(t == 0), stop=False,
                       skip_group_check=True)
                if not last:
                    hidden_statistics(n + 1)
                pe.wait_ge(s_on, n + 1)
                for t in range(GT):
                    i = nc.tensor.transpose(B[3][:, tiles[t]],
                                            o2[:].rearrange("p (t h) c -> p t (h c)", t=GT)[:, t, :], C["ident"])
                i.then_inc(s_ot, 1)
                pe.wait_ge(s_oc, n + 1)
                for t in range(GT):
                    i = mm(B[2][:, tiles[t]], oc[:, tiles[t]], wo[:], start=False, stop=True, skip_group_check=True)
                i.then_inc(s_pj, 1)

            turn_residual(0, 0, 0, first=True)
            turn_delta(0, 0, first=True)
            turn_delta(1, 1)
            hidden_state(0, 0)
            hidden_statistics(0)
            steps(pe, step)

        @block.scalar
        def _(act):
            op = nc.scalar.activation
            act.wait_ge(s_w, NW)
            act.wait_ge(s_set, 2)
            op(itemp[:], par[:, 1], ACT.Exp, scale=-1.0).then_inc(s_pa, 1)
            op(floor[:].rearrange("p h a -> p (h a)"), par[:, 2], ACT.Sigmoid).then_inc(s_pa, 1)
            op(res[:], crl[:], ACT.Sigmoid).then_inc(s_pa, 1)

            def channel_major(m, b):
                act.wait_ge(s_T, m + 1)
                op(xT[b][:], B[0], ACT.Copy).then_inc(s_xT, 1)

            def delta_branch(m, b):
                act.wait_ge(s_Td, m + 1)
                op(X[b][:, 2].rearrange("p a c -> p (a c)"), B[1], ACT.Copy).then_inc(s_Xd, 1)

            def square(m):
                act.wait_ge(s_xc, m + 1)
                op(xc[:], xc[:], ACT.Square).then_inc(s_sq, 1)

            def norms(m):
                act.wait_ge(s_ms, m + 1)
                op(stt[:].rearrange("p j (a k) -> p a j k", k=4)[:, 0:NA, :, 3],
                   ss[:, 3].rearrange("p (a j) -> p a j", a=NA), ACT.Sqrt, scale=32.0).then_inc(s_l2, 1)

            def statistics(m):
                act.wait_ge(s_stp, m + 1)
                op(sT[:], B[0], ACT.Copy).then_inc(s_sT, 1)

            def sum_deviation(n):
                act.wait_ge(s_z, n + 1)
                op(sdv[:], mv[:, :, 1], ACT.Sqrt, bias=eps[:, 0:1]).then_inc(s_sd, 1)

            def step(n, b, r, first, last):
                for h in range(NH):
                    act.wait_ge(s_h, 4 * n + h + 1)
                    op(hid[:, h, :], B[4 + h], ACT.Gelu, bias=gb1[:, 0:1]).then_inc(s_hid, 1)
                if not first:
                    sum_deviation(n - 1)
                if not last:
                    square(n + 1)
                    norms(n + 1)
                act.wait_ge(s_sh, n + 1)
                op(pr[:], lg[:], ACT.Exp).then_inc(s_ex, 1)
                if not last:
                    if not first:
                        act.wait_ge(s_pj, n)
                    channel_major(n + 1, 1 - b)
                act.wait_ge(s_o, n + 1)
                op(o2[:], o[:], ACT.Square).then_inc(s_o2, 1)
                if not isinstance(n, int) or n < NG - 2:
                    delta_branch(n + 2, b)
                if not last:
                    statistics(n + 1)
                act.wait_ge(s_rms, n + 1)
                op(mx[:], mx[:], ACT.Sqrt, bias=eps[:, 0:1], scale=1.0 / 32).then_inc(s_rsd, 1)
                act.wait_ge(s_ot, n + 1)
                op(oc[:], B[3], ACT.Copy).then_inc(s_oc, 1)

            channel_major(0, 0)
            delta_branch(0, 0)
            delta_branch(1, 1)
            square(0)
            norms(0)
            statistics(0)
            steps(act, step)
            sum_deviation(NG - 1)

        @block.vector
        def _(dve):
            v = nc.vector
            own = Steps(s_dve)

            def then(ins):
                dve.wait_ge(s_dve, own.mark(ins))

            dve.wait_ge(s_w, NW)
            dve.wait_ge(s_set, 2)
            dve.wait_ge(s_pa, 3)
            own.restart(dve)
            then(v.tensor_scalar(floor[:], floor[:], 0.05, None, ALU.mult))
            then(v.tensor_reduce(keepf[:], floor[:], AX_X, ALU.add))
            then(v.tensor_scalar(keepf[:], keepf[:], -1.0, 1.0, ALU.mult, ALU.add))
            then(v.tensor_tensor(floor[:, :, 0], floor[:, :, 0], res[:], ALU.add))
            then(v.tensor_tensor(wid[:].rearrange("p (h c) -> p h c", h=NH), wid[:].rearrange("p (h c) -> p h c", h=NH),
                                 alpha[:].unsqueeze(2).broadcast_to([P, NH, 32]), ALU.mult))
            v.tensor_scalar(wo[:], wo[:], onw[:, 0:1], None, ALU.mult).then_inc(s_pv, 1)
            dve.wait_ge(s_pv, 1)
            tiles4 = lambda a: a.unsqueeze(1).broadcast_to([P, GT, NH * NA])
            wide = lambda a, k: a.unsqueeze(2).broadcast_to([P, TH, k])
            st4 = stt[:].rearrange("p j (a k) -> p a j k", k=4)[:, 0:NA]
            by_a = lambda k: ss[:, k].rearrange("p (a j) -> p a j", a=NA)
            c64 = xc[:].rearrange("p a j c -> p (a j) c")

            def center(m, b, r):
                x64 = X[b][:].rearrange("p a j c -> p (a j) c")
                dve.wait_ge(s_x[b], 48 * r + 48)
                dve.wait_ge(s_Xl, m + 1)
                dve.wait_ge(s_Xd, m + 1)
                i = own.mark(v.tensor_reduce(ss[:, 0], x64, AX_X, ALU.add))
                v.tensor_reduce(ss[:, 1], x64, AX_X, ALU.add, apply_absolute_value=True)
                dve.wait_ge(s_dve, i)
                then(v.tensor_scalar(ss[:, 0], ss[:, 0], 1.0 / 32, None, ALU.mult))
                v.tensor_tensor(c64, x64, ss[:, 0].unsqueeze(2).broadcast_to([P, NA * TH, 32]), ALU.subtract
                                ).then_inc(s_xc, 1)

            def squares(m, first=False):
                if not first:
                    dve.wait_ge(s_stp, m)
                v.tensor_copy(st4[:, :, :, 0], by_a(0))
                then(v.tensor_scalar(st4[:, :, :, 2], by_a(1), 1.0 / 32, None, ALU.mult))
                then(v.tensor_tensor(ss[:, 3], ss[:, 0], ss[:, 0], ALU.mult))
                dve.wait_ge(s_sq, m + 1)
                then(v.tensor_reduce(ss[:, 2], c64, AX_X, ALU.add))
                v.scalar_tensor_tensor(ss[:, 3], ss[:, 2], 1.0 / 32, ss[:, 3], ALU.mult, ALU.add).then_inc(s_ms, 1)

            def variances(m):
                dve.wait_ge(s_l2, m + 1)
                v.tensor_scalar(st4[:, :, :, 1], by_a(2), 1.0 / 32, None, ALU.mult).then_inc(s_st, 1)

            def layer_norm(n, b, first=False):
                z = B[2].rearrange("p (t c) -> p t c", t=GT)
                dve.wait_ge(s_pj, n + 1)
                for t in range(GT):
                    i = own.mark(v.bn_stats(bst[:, t, :], z[:, t, :]))
                dve.wait_ge(s_dve, i)
                for t in range(GT):
                    i = v.bn_aggr(mv[:, t, :], bst[:, t, :])
                i.then_inc(s_z, 1)
                dve.wait_ge(s_sd, n + 1)
                then(v.reciprocal(rsv[:], sdv[:]))
                if not first:
                    dve.wait_ge(s_out, 16 * n)
                for t in range(GT):
                    i = v.tensor_scalar(xo[b][:, t, :], z[:, t, :], mv[:, t, 0:1], rsv[:, t:t + 1],
                                        ALU.subtract, ALU.mult)
                i.then_inc(s_xo, 1)

            def step(n, b, r, first, last):
                own.restart(dve)
                if not last:
                    center(n + 1, 1 - b, r)
                if not first:
                    layer_norm(n - 1, 1 - b, first=isinstance(n, int) and n == 1)
                if not last:
                    squares(n + 1)
                dve.wait_ge(s_lg, n + 1)
                then(v.tensor_tensor(lg[:].rearrange("p (t h) a -> p t (h a)", t=GT),
                                     B[4][:, 0:TH * NA].rearrange("p (t k) -> p t k", t=GT), tiles4(par[:, 0]), ALU.add))
                then(v.tensor_tensor(lg[:].rearrange("p (t h) a -> p t (h a)", t=GT),
                                     lg[:].rearrange("p (t h) a -> p t (h a)", t=GT), tiles4(itemp[:]), ALU.mult))
                then(v.tensor_reduce(mx[:], lg[:], AX_X, ALU.max))
                v.tensor_tensor(lg[:], lg[:], wide(mx[:], NA), ALU.subtract).then_inc(s_sh, 1)
                dve.wait_ge(s_ex, n + 1)
                then(v.tensor_reduce(mx[:], pr[:], AX_X, ALU.add))
                then(v.reciprocal(mx[:], mx[:]))
                then(v.tensor_tensor(mx[:].rearrange("p (t h) -> p t h", t=GT), mx[:].rearrange("p (t h) -> p t h", t=GT),
                                     keepf[:].unsqueeze(1).broadcast_to([P, GT, NH]), ALU.mult))
                then(v.tensor_tensor(pr[:], pr[:], wide(mx[:], NA), ALU.mult))
                then(v.tensor_tensor(pr[:].rearrange("p (t h) a -> p t (h a)", t=GT),
                                     pr[:].rearrange("p (t h) a -> p t (h a)", t=GT),
                                     tiles4(floor[:].rearrange("p h a -> p (h a)")), ALU.add))
                for a in range(NA):
                    i = own.mark(v.tensor_tensor(mix[:, a], X[b][:, a], wide(pr[:, :, a], 32), ALU.mult))
                dve.wait_ge(s_dve, i)
                then(v.tensor_reduce(o[:], mix[:].rearrange("p a j c -> p j c a"), AX_X, ALU.add))
                dve.wait_ge(s_id, n + 1)
                v.tensor_tensor(o[:], o[:], B[2].rearrange("p (j c) -> p j c", c=32), ALU.add).then_inc(s_o, 1)
                if not last:
                    variances(n + 1)
                dve.wait_ge(s_o2, n + 1)
                v.tensor_reduce(mx[:], o2[:], AX_X, ALU.add).then_inc(s_rms, 1)
                dve.wait_ge(s_rsd, n + 1)
                then(v.reciprocal(mx[:], mx[:]))
                v.tensor_tensor(o2[:], o[:], wide(mx[:], 32), ALU.mult).then_inc(s_on, 1)

            center(0, 0, 0)
            squares(0, first=True)
            variances(0)
            steps(dve, step)
            own.restart(dve)
            layer_norm(NG - 1, 1)


def delta_stage(nc, sem, x_in, x_out, v_rows, s_rows, w, consts):
    with ExitStack() as ctx:
        def sb(name, shape):
            return ctx.enter_context(nc.sbuf_tensor("keep_" + name, shape, F32))

        long_fir = sb("long_fir", [P, TOK // P, P])
        oT = sb("oT", [P, NCH, NSEQ, 32])
        with ExitStack() as inner:
            keep = {k: inner.enter_context(nc.sbuf_tensor("keep_" + k, [P, NCH, NSEQ, 32], F32))
                    for k in ("A", "kb", "vb", "k", "q", "attn")}
            delta_project(nc, sem, keep, x_in, v_rows, s_rows, w, consts)
            delta_invert(nc, sem, keep, long_fir, v_rows, w, consts)
            delta_recur(nc, sem, keep, oT)
        gate_stage(nc, sem, oT, long_fir, v_rows, s_rows, x_in, x_out, w, consts)


def host_layout(inp):
    a = {k: np.asarray(v) for k, v in inp.items()}
    col = lambda v: v.reshape(-1, 1)
    L = "L0_attn_"
    d = {}
    d["a_maa"] = np.stack([a[L + "time_maa_" + c].reshape(-1) for c in "xwkvrg"], 1)
    d["a_maa_w1"] = a[L + "time_maa_w1"]
    d["a_maa_w2"] = a[L + "time_maa_w2"]
    d["a_dec_w1"] = a[L + "time_decay_w1"]
    d["a_dec_w2"] = a[L + "time_decay_w2"]
    d["a_decay"] = col(a[L + "time_decay"])
    d["a_wT"] = np.stack([a[L + "W_" + c].T for c in "rkvgo"], 1)
    d["a_lnwb"] = np.stack([a[L + "ln_w"], a[L + "ln_b"]], 1)
    for tag, L in (("b", "L0_ffn_"), ("d", "L1_ffn_")):
        d[tag + "_gate_w"] = a[L + "gate_w"].T if tag == "b" else a[L + "gate_w"]
        if tag == "d":
            d[tag + "_gate_b"] = a[L + "gate_b"].reshape(1, -1)
        d[tag + "_w1"] = a[L + "w1"].transpose(1, 0, 2).reshape(P, 8, 4, P)
        d[tag + "_b1"] = a[L + "b1"].reshape(8, 4, P).transpose(2, 0, 1)
        d[tag + "_w2"] = a[L + "w2"].reshape(8, 4, P, P).transpose(2, 0, 1, 3)
        d[tag + "_b2"] = a[L + "b2"]
    delta_layout(a, d)
    return d


def delta_layout(a, d):
    L = "L1_attn_"
    d["c_wqkv"] = np.stack([a[L + "W" + c] for c in "qkv"], 1)
    d["c_wb"] = np.repeat(a[L + "Wb"], 32, axis=1)
    d["c_taps"] = np.stack([a[L + "cw" + c] for c in "qkv"], 1)
    d["c_firs"] = a[L + "firs"].reshape(P, 3)
    firl = a[L + "firl"].reshape(P, 63)
    d["c_firl"] = np.concatenate([np.zeros((P, 127), firl.dtype), firl[:, ::-1], np.zeros((P, 129), firl.dtype)], 1)
    d["c_g1"] = a[L + "gW1"][:P]
    g1s = np.zeros((4, 32, P), a[L + "gW1"].dtype)
    g1s[:, :16] = a[L + "gW1"][P:]
    d["c_g1s"] = g1s.reshape(P, P)
    d["c_gb1"] = a[L + "gb1"].reshape(P, 1)
    d["c_gw2"] = a[L + "gW2"]
    d["c_wid"] = a[L + "Wid"]
    d["c_wo"] = a[L + "Wo"]
    d["c_onw"] = np.tile(a[L + "o_norm_w"], 4).reshape(P, 1)
    d["c_gb2"] = np.tile(a[L + "gb2"], 4).reshape(1, 16)
    d["c_log_temp"] = a[L + "log_temp"].reshape(1, 16)
    d["c_floor"] = a[L + "floor_param"].reshape(1, 16)
    d["c_crl"] = a[L + "conv_res_logit"].reshape(1, 4)
    d["c_alpha"] = a[L + "alpha_id"].reshape(1, 4)


def block_program(nc, ins, out, scratch):
    pick = lambda tag: {k[2:]: v for k, v in ins.items() if k.startswith(tag + "_")}
    x1, x2, x3, v_rows, s_rows, b_sorted, b_results, d_sorted, d_results = scratch
    def stage(build, *args):
        sems = []

        def sem(name):
            sems.append(nc.alloc_semaphore(name=name))
            return sems[-1]

        build(nc, sem, *args)
        nc.all_engine_barrier()
        nc.clear_and_free_semaphores(sems)
        nc.all_engine_barrier()

    stage(lion_stage, ins["x"], x1, pick("a"), ins["consts"])
    stage(moe_stage, "b", x1, x2, b_sorted, b_results, pick("b"), ins["consts"], 2, ACT.Relu, False)
    stage(delta_stage, x2, x3, v_rows, s_rows, pick("c"), ins["consts"])
    stage(moe_stage, "d", x3, out, d_sorted, d_results, pick("d"), ins["consts"], 1, ACT.Gelu, True)


def kernel(**inputs):
    import concourse.bacc as _bacc
    from concourse.bass_utils import run_bass_kernel_spmd as _run

    given = {k: np.asarray(v) for k, v in inputs.items()}
    nc = _bacc.Bacc("TRN2", target_bir_lowering=False, num_devices=1)
    laid = {"x": given["L0_attn_x"].reshape(TOK, P),
            "consts": np.concatenate(list(shape_constants().values()), 1)}
    laid.update(host_layout(given))
    arrays, ins = {}, {}
    for name, a in laid.items():
        a = np.ascontiguousarray(a)
        arrays["in_" + name] = a
        ins[name] = nc.dram_tensor("in_" + name, a.shape, mybir.dt.from_np(a.dtype), kind="ExternalInput").ap()
    out = nc.dram_tensor("out_rows", (TOK, P), F32, kind="ExternalOutput").ap()
    scratch = [nc.dram_tensor(f"rows_{i}", (TOK, P), F32, kind="Internal").ap() for i in range(5)]
    for tag, topk in (("b", 2), ("d", 1)):
        scratch += [[nc.dram_tensor(f"{name}_{tag}{i}", (LT * P, P), F32, kind="Internal").ap() for i in range(topk)]
                    for name in ("sorted", "results")]
    block_program(nc, ins, out, scratch)
    r = _run(nc, [arrays], core_ids=[0])
    return r.results[0]["out_rows"].reshape(NSEQ, SEQ, P)
```
